# Optimizing a Trainium2 kernel written in Bass

```python
import numpy as np
import jax
import jax.numpy as jnp

def _softmax(x, axis=-1):
    return jax.nn.softmax(x, axis=axis)

def _gelu(x):
    return jax.nn.gelu(x, approximate=True)

def _silu(x):
    return jax.nn.silu(x)

def _sigmoid(x):
    return jax.nn.sigmoid(x)

def _layernorm(x, axis=-1, eps=1e-05):
    m = jnp.mean(x, axis=axis, keepdims=True)
    v = jnp.var(x, axis=axis, keepdims=True)
    return (x - m) / jnp.sqrt(v + eps)

def _scatter_add(tgt, idx, src, axis=0):
    return tgt.at[idx].add(src)

def _segment_sum(src, seg, n):
    return jax.ops.segment_sum(src, seg, n)
kernel_name = 'mk_adaln_ffn_d2_seqx_r8_d34ab4'

def setup_inputs(seed: int=0):
    np.random.seed(seed)
    _w = jnp.asarray

    def _rec_inputs():
        import jax
        import jax.numpy as jnp
        _rk = jax.random.key(seed)
        x = -0.000125 + 0.9999 * jax.random.normal(jax.random.fold_in(_rk, 1), (8, 128, 512), jnp.float32)
        _lenS = 128 - jax.random.randint(jax.random.fold_in(_rk, 7), (8,), 0, max(1, 128 // 4) + 1, jnp.int32)
        _lenS2 = 128 - jax.random.randint(jax.random.fold_in(_rk, 8), (8,), 0, max(1, 128 // 4) + 1, jnp.int32)
        itok_B_3_7 = jax.random.randint(jax.random.fold_in(_rk, 11), (8,), 3, 8, jnp.int32)
        itok_Bx16_0_63 = jax.random.randint(jax.random.fold_in(_rk, 12), (8, 16), 0, 64, jnp.int32)
        itok_B_207_1644 = jax.random.randint(jax.random.fold_in(_rk, 13), (8,), 207, 1645, jnp.int32)
        return (x, itok_B_3_7, itok_Bx16_0_63, itok_B_207_1644)
    x, itok_B_3_7, itok_Bx16_0_63, itok_B_207_1644 = _rec_inputs()

    def _L0_cond_setup():
        import jax, jax.numpy as jnp
        import numpy as np
        MAX_LORAS, OUT, IN = (8, 512, 512)
        B, S = (4, 256)
        key = jax.random.key(seed)
        k1, k2, k3 = jax.random.split(key, 3)
        x = jax.random.normal(k1, (B, S, IN), dtype=jnp.float32)
        weight = jax.random.normal(k2, (MAX_LORAS, OUT, IN), dtype=jnp.float32) * 0.02
        adapter_ids = jax.random.randint(k3, (B,), 0, MAX_LORAS, dtype=jnp.int32)
        return {'x': x, 'weight': weight, 'adapter_ids': adapter_ids}
    _L0_cond_all = _L0_cond_setup()
    _L0_cond_in = {k: v for k, v in _L0_cond_all.items() if k in ('weight',)}
    del _L0_cond_all

    def _L0_ffn_setup():
        import jax, jax.numpy as jnp
        import numpy as np
        B, S, D_IN, D_OUT = (2, 256, 512, 512)
        E, K, R = (8, 2, 16)
        SCALING = 32.0 / 16.0
        key = jax.random.key(seed)
        ks = jax.random.split(key, 6)
        x = jax.random.normal(ks[0], (B, S, D_IN), dtype=jnp.float32)
        gate_w = jax.random.normal(ks[1], (E, D_IN), dtype=jnp.float32) * 0.02
        base_w = jax.random.normal(ks[2], (D_OUT, D_IN), dtype=jnp.float32) * 0.02
        base_b = jax.random.normal(ks[3], (D_OUT,), dtype=jnp.float32) * 0.02
        lora_A = jax.random.normal(ks[4], (E, R, D_IN), dtype=jnp.float32) * 0.02
        lora_B = jax.random.normal(ks[5], (E, D_OUT, R), dtype=jnp.float32) * 0.02
        return {'x': x, 'gate_w': gate_w, 'base_w': base_w, 'base_b': base_b, 'lora_A': lora_A, 'lora_B': lora_B}
    _L0_ffn_all = _L0_ffn_setup()
    _L0_ffn_in = {k: v for k, v in _L0_ffn_all.items() if k in ('gate_w', 'base_w', 'base_b', 'lora_A', 'lora_B')}
    del _L0_ffn_all

    def _L1_cond_setup():
        import jax, jax.numpy as jnp
        import numpy as np
        B, S, HID = (4, 128, 512)
        D, HQ, HK = (128, 32, 8)
        PAGES, PSIZE, NPP = (64, 32, 16)
        THETA = 10000.0
        EPS = 1e-06
        SCALE = 1.0 / float(np.sqrt(D))

        def _rmsnorm(t, w):
            var = jnp.mean(t * t, axis=-1, keepdims=True)
            return t * jax.lax.rsqrt(var + EPS) * w

        def _rope(t, pos):
            inv_freq = 1.0 / THETA ** (jnp.arange(0, D, 2, dtype=jnp.float32) / D)
            freqs = pos[..., None].astype(jnp.float32) * inv_freq
            cos = jnp.cos(freqs)[:, :, None, :]
            sin = jnp.sin(freqs)[:, :, None, :]
            t1, t2 = (t[..., :D // 2], t[..., D // 2:])
            return jnp.concatenate([t1 * cos - t2 * sin, t2 * cos + t1 * sin], axis=-1)
        key = jax.random.key(seed)
        ks = jax.random.split(key, 10)
        x = jax.random.normal(ks[0], (B, S, HID), jnp.float32)
        Wq = jax.random.normal(ks[1], (HQ * D, HID), jnp.float32) * 0.02
        Wk = jax.random.normal(ks[2], (HK * D, HID), jnp.float32) * 0.02
        Wv = jax.random.normal(ks[3], (HK * D, HID), jnp.float32) * 0.02
        Wo = jax.random.normal(ks[4], (HID, HQ * D), jnp.float32) * 0.02
        q_norm_w = jax.random.uniform(ks[5], (D,), jnp.float32)
        k_norm_w = jax.random.uniform(ks[6], (D,), jnp.float32)
        k_cache = jax.random.normal(ks[7], (PAGES, PSIZE, HK, D), jnp.float32)
        v_cache = jax.random.normal(ks[8], (PAGES, PSIZE, HK, D), jnp.float32)
        block_table = jnp.arange(B * NPP, dtype=jnp.int32).reshape(B, NPP)
        cache_seqlens = jax.random.randint(ks[9], (B,), 0, 475).astype(jnp.int32)
        return dict(x=x, Wq=Wq, Wk=Wk, Wv=Wv, Wo=Wo, q_norm_w=q_norm_w, k_norm_w=k_norm_w, k_cache=k_cache, v_cache=v_cache, block_table=block_table, cache_seqlens=cache_seqlens)
    _L1_cond_all = _L1_cond_setup()
    _L1_cond_in = {k: v for k, v in _L1_cond_all.items() if k in ('Wq', 'Wk', 'Wv', 'Wo', 'q_norm_w', 'k_norm_w', 'k_cache', 'v_cache')}
    del _L1_cond_all

    def _L1_ffn_setup():
        import jax, jax.numpy as jnp
        import numpy as np
        IN_F = 512
        OUT_F = 512
        RANK = 8
        NUM_EXPERTS = 64
        TOP_K = 16
        ROUTER_DIM = 16
        ALPHA = 32
        SCALING = ALPHA / TOP_K
        BOTTLENECK = NUM_EXPERTS * RANK
        key = jax.random.key(seed)
        ks = jax.random.split(key, 5)
        x = jax.random.normal(ks[0], (4, 512, IN_F), dtype=jnp.float32)
        bound_a = float(np.sqrt(6.0 / IN_F))
        A_w = jax.random.uniform(ks[1], (BOTTLENECK, IN_F), jnp.float32, -bound_a, bound_a)
        B_w = jax.random.normal(ks[2], (OUT_F, BOTTLENECK), dtype=jnp.float32) * 0.02
        Wq_w = jax.random.normal(ks[3], (ROUTER_DIM, IN_F), dtype=jnp.float32) * 0.02
        keys = jax.random.normal(ks[4], (NUM_EXPERTS, ROUTER_DIM), dtype=jnp.float32) * 0.01
        return {'x': x, 'A_w': A_w, 'B_w': B_w, 'Wq_w': Wq_w, 'keys': keys}
    _L1_ffn_all = _L1_ffn_setup()
    _L1_ffn_in = {k: v for k, v in _L1_ffn_all.items() if k in ('A_w', 'B_w', 'Wq_w', 'keys')}
    del _L1_ffn_all
    return {'x': x, 'itok_B_3_7': itok_B_3_7, 'itok_Bx16_0_63': itok_Bx16_0_63, 'itok_B_207_1644': itok_B_207_1644, 'L0_cond_weight': _L0_cond_in['weight'], 'L0_ffn_gate_w': _L0_ffn_in['gate_w'], 'L0_ffn_base_w': _L0_ffn_in['base_w'], 'L0_ffn_base_b': _L0_ffn_in['base_b'], 'L0_ffn_lora_A': _L0_ffn_in['lora_A'], 'L0_ffn_lora_B': _L0_ffn_in['lora_B'], 'L1_cond_Wq': _L1_cond_in['Wq'], 'L1_cond_Wk': _L1_cond_in['Wk'], 'L1_cond_Wv': _L1_cond_in['Wv'], 'L1_cond_Wo': _L1_cond_in['Wo'], 'L1_cond_q_norm_w': _L1_cond_in['q_norm_w'], 'L1_cond_k_norm_w': _L1_cond_in['k_norm_w'], 'L1_cond_k_cache': _L1_cond_in['k_cache'], 'L1_cond_v_cache': _L1_cond_in['v_cache'], 'L1_ffn_A_w': _L1_ffn_in['A_w'], 'L1_ffn_B_w': _L1_ffn_in['B_w'], 'L1_ffn_Wq_w': _L1_ffn_in['Wq_w'], 'L1_ffn_keys': _L1_ffn_in['keys']}

def reference(x, itok_B_3_7, itok_Bx16_0_63, itok_B_207_1644, L0_cond_weight, L0_ffn_gate_w, L0_ffn_base_w, L0_ffn_base_b, L0_ffn_lora_A, L0_ffn_lora_B, L1_cond_Wq, L1_cond_Wk, L1_cond_Wv, L1_cond_Wo, L1_cond_q_norm_w, L1_cond_k_norm_w, L1_cond_k_cache, L1_cond_v_cache, L1_ffn_A_w, L1_ffn_B_w, L1_ffn_Wq_w, L1_ffn_keys):
    import jax
    import jax.numpy as jnp

    def _L0_cond_ref(x, weight, adapter_ids):
        import jax, jax.numpy as jnp
        import numpy as np
        MAX_LORAS, OUT, IN = (8, 512, 512)
        B, S = (4, 256)
        w = weight[adapter_ids]
        return jnp.einsum('bsi,boi->bso', x, w)

    def _L0_ffn_ref(x, gate_w, base_w, base_b, lora_A, lora_B):
        import jax, jax.numpy as jnp
        import numpy as np
        B, S, D_IN, D_OUT = (2, 256, 512, 512)
        E, K, R = (8, 2, 16)
        SCALING = 32.0 / 16.0
        gate_logits = jnp.einsum('bsd,ed->bse', x, gate_w)
        weights, selected = jax.lax.top_k(gate_logits, K)
        weights = jax.nn.softmax(weights.astype(jnp.float32), axis=2).astype(x.dtype)
        result = jnp.einsum('bsd,od->bso', x, base_w) + base_b
        w_full = jnp.sum(jax.nn.one_hot(selected, E, dtype=x.dtype) * weights[..., None], axis=2)
        low = jnp.einsum('bsd,erd->ebsr', x, lora_A)
        lora_out = jnp.einsum('ebsr,eor,bse->bso', low, lora_B, w_full)
        result = result + SCALING * lora_out
        return result

    def _L1_cond_ref(x, Wq, Wk, Wv, Wo, q_norm_w, k_norm_w, k_cache, v_cache, block_table, cache_seqlens):
        import jax, jax.numpy as jnp
        import numpy as np
        B, S, HID = (4, 128, 512)
        D, HQ, HK = (128, 32, 8)
        PAGES, PSIZE, NPP = (64, 32, 16)
        THETA = 10000.0
        EPS = 1e-06
        SCALE = 1.0 / float(np.sqrt(D))

        def _rmsnorm(t, w):
            var = jnp.mean(t * t, axis=-1, keepdims=True)
            return t * jax.lax.rsqrt(var + EPS) * w

        def _rope(t, pos):
            inv_freq = 1.0 / THETA ** (jnp.arange(0, D, 2, dtype=jnp.float32) / D)
            freqs = pos[..., None].astype(jnp.float32) * inv_freq
            cos = jnp.cos(freqs)[:, :, None, :]
            sin = jnp.sin(freqs)[:, :, None, :]
            t1, t2 = (t[..., :D // 2], t[..., D // 2:])
            return jnp.concatenate([t1 * cos - t2 * sin, t2 * cos + t1 * sin], axis=-1)
        bsz, seqlen, _ = x.shape
        q = jnp.einsum('bsd,ed->bse', x, Wq).reshape(bsz, seqlen, HQ, D)
        k = jnp.einsum('bsd,ed->bse', x, Wk).reshape(bsz, seqlen, HK, D)
        v = jnp.einsum('bsd,ed->bse', x, Wv).reshape(bsz, seqlen, HK, D)
        q = _rmsnorm(q, q_norm_w)
        k = _rmsnorm(k, k_norm_w)
        pos = cache_seqlens[:, None] + jnp.arange(seqlen)[None, :]
        q = _rope(q, pos)
        k = _rope(k, pos)
        L = NPP * PSIZE
        kc = k_cache[block_table].reshape(bsz, L, HK, D)
        vc = v_cache[block_table].reshape(bsz, L, HK, D)
        k_all = jnp.concatenate([kc, k], axis=1)
        v_all = jnp.concatenate([vc, v], axis=1)
        valid_c = jnp.arange(L)[None, :] < cache_seqlens[:, None]
        valid = jnp.concatenate([valid_c, jnp.ones((bsz, seqlen), dtype=bool)], axis=1)
        rep = HQ // HK
        k_all = jnp.repeat(k_all, rep, axis=2)
        v_all = jnp.repeat(v_all, rep, axis=2)
        scores = jnp.einsum('bqhd,bkhd->bhqk', q, k_all) * SCALE
        scores = jnp.where(valid[:, None, None, :], scores, -1e+30)
        probs = jax.nn.softmax(scores, axis=-1)
        o = jnp.einsum('bhqk,bkhd->bqhd', probs, v_all)
        o = o.reshape(bsz, seqlen, HQ * D)
        return jnp.einsum('bse,de->bsd', o, Wo)

    def _L1_ffn_ref(x, A_w, B_w, Wq_w, keys):
        import jax, jax.numpy as jnp
        import numpy as np
        IN_F = 512
        OUT_F = 512
        RANK = 8
        NUM_EXPERTS = 64
        TOP_K = 16
        ROUTER_DIM = 16
        ALPHA = 32
        SCALING = ALPHA / TOP_K
        BOTTLENECK = NUM_EXPERTS * RANK
        q = jnp.einsum('bsd,rd->bsr', x, Wq_w)
        scores = jnp.einsum('bsr,er->bse', q, keys)
        top_vals, top_idx = jax.lax.top_k(scores, TOP_K)
        top_w = jax.nn.softmax(top_vals, axis=-1)
        gate = jnp.sum(jax.nn.one_hot(top_idx, NUM_EXPERTS, dtype=top_w.dtype) * top_w[..., None], axis=-2)
        z = jnp.einsum('bsd,nd->bsn', x, A_w)
        z = z.reshape(*z.shape[:-1], NUM_EXPERTS, RANK)
        z_gated = (z * gate[..., None]).reshape(*z.shape[:-2], BOTTLENECK)
        out = jnp.einsum('bsn,on->bso', z_gated, B_w) * SCALING
        return out
    x = x + _L0_ffn_ref(_L0_cond_ref(x, L0_cond_weight, itok_B_3_7), L0_ffn_gate_w, L0_ffn_base_w, L0_ffn_base_b, L0_ffn_lora_A, L0_ffn_lora_B)
    x = x + _L1_ffn_ref(_L1_cond_ref(x, L1_cond_Wq, L1_cond_Wk, L1_cond_Wv, L1_cond_Wo, L1_cond_q_norm_w, L1_cond_k_norm_w, L1_cond_k_cache, L1_cond_v_cache, itok_Bx16_0_63, itok_B_207_1644), L1_ffn_A_w, L1_ffn_B_w, L1_ffn_Wq_w, L1_ffn_keys)
    return x

_drawn_inputs = setup_inputs


def setup_inputs(seed=0):
    import zlib

    import numpy as np

    out = dict(_drawn_inputs(seed))
    spreads = {}
    factors = {'L0_ffn_gate_w': 2.886,
     'L0_ffn_base_b': 3.072,
     'L1_cond_Wq': 8.0,
     'L1_cond_Wk': 8.0,
     'L1_cond_Wv': 8.0,
     'L1_cond_Wo': 8.0,
     'L1_cond_q_norm_w': 8.0,
     'L1_cond_k_norm_w': 8.0,
     'L1_cond_k_cache': 8.0,
     'L1_cond_v_cache': 8.0,
     'L1_ffn_A_w': 8.0,
     'L1_ffn_B_w': 8.0,
     'L1_ffn_Wq_w': 8.0,
     'L1_ffn_keys': 8.0}
    for name, (base, spread) in spreads.items():
        noise = np.random.default_rng([zlib.crc32(name.encode()), seed]).standard_normal(out[name].shape)
        drawn = base * np.exp(spread * noise) if base else spread * noise
        out[name] = jnp.asarray(drawn.astype(out[name].dtype))
    for name, factor in factors.items():
        out[name] = (out[name] * factor).astype(out[name].dtype)
    return out
```

```python
from contextlib import ExitStack

import concourse.bass as bass
from concourse import mybir

ALU = mybir.AluOpType
ACT = mybir.ActivationFunctionType
F32 = mybir.dt.float32
F32R = mybir.dt.float32r
BF16 = mybir.dt.bfloat16
I32 = mybir.dt.int32
U32 = mybir.dt.uint32

B, S, D = 8, 128, 512
KT = D // 128
HD, HQ, HK = 128, 32, 8
REP = HQ // HK
GQ = REP * HD
PAGE, NPP = 32, 16
L = PAGE * NPP
LT = L // 128
NKEY = L + S
KTILES = NKEY // 128
E0, R0 = 8, 16
NE, RANK, RD = 64, 8, 16
UNITS = HK * B
WQ, WKV, WO = KT * GQ, KT * 2 * HD, REP * D
WCOLS = WQ + WKV + WO
NPT = 4
CH = WCOLS // B
EPS = 1e-6
NEG = -1e30
TWO_PI_HI = 6.28125
TWO_PI_MID = 2029.0 / 2 ** 20
TWO_PI_LO = 6.283185307179586 - TWO_PI_HI - TWO_PI_MID
ROUND = 1.5 * 2 ** 23
PI_SAFE = 3.1415925


def wait_alone(eng, tick, *waits):
    for s, v in waits:
        eng.wait_ge(s, v)
        eng.sem_inc(tick, 1)


def layer0(nc, t, dram, keep):
    with ExitStack() as ctx:
        def sb(name, shape, dt=F32):
            return ctx.enter_context(nc.sbuf_tensor(name, shape, dt))

        def ps(name, shape, dt=F32):
            return ctx.enter_context(nc.psum_tensor(name, shape, dt))

        def sem(name):
            return ctx.enter_context(nc.semaphore(name))

        ident, rope, yacc = keep["ident"], keep["rope"], keep["yacc"]

        seq_i = sb("seq_i", [128, B], I32)
        seq_f = sb("seq_f", [128, B])
        pos = sb("pos", [128, B])
        tok = sb("tok", [128, 1])
        invf = sb("invf", [128, 64])
        normw = sb("normw", [128, 2, 128])
        keyno = sb("keyno", [1, L])
        ang = sb("ang", [128, B, 64])
        turn = sb("turn", [128, 2, B, 64])
        red = sb("red", [128, 2, B, 64])
        trig = sb("trig", [128, 2, B, 64])
        mask = sb("mask_rows", [1, B, NKEY], BF16)
        ids = sb("ids", [1, B], I32)
        w_raw = sb("w_raw", [128, 2, KT, D])
        w_hi = sb("w_hi", [128, KT, D], F32R)
        w_lo = sb("w_lo", [128, KT, D], F32R)
        base_raw = sb("base_raw", [128, KT, D])
        base_hi = sb("base_hi", [128, KT, D], F32R)
        base_lo = sb("base_lo", [128, KT, D], F32R)
        NLG = E0 * R0 + E0
        lg_raw = sb("lg_raw", [128, KT, NLG])
        lg_hi = sb("lg_hi", [128, KT, NLG], F32R)
        lg_lo = sb("lg_lo", [128, KT, NLG], F32R)
        lb_raw = sb("lb_raw", [128, D])
        lb_hi = sb("lb_hi", [128, D], F32R)
        lb_lo = sb("lb_lo", [128, D], F32R)
        bias = sb("bias", [128, D])
        xT_raw = sb("xT_raw", [128, 2, KT, 128])
        x_raw = sb("x_raw", [128, 2, D])
        xT_hi = sb("xT_hi", [128, KT, 128], F32R)
        xT_lo = sb("xT_lo", [128, KT, 128], F32R)
        yT_hi = sb("yT_hi", [128, KT, 128], F32R)
        yT_lo = sb("yT_lo", [128, KT, 128], F32R)
        xb = sb("xb", [128, D])
        lgs = sb("lgs", [128, E0])
        v8 = sb("v8", [128, 8])
        i8 = sb("i8", [128, 8], U32)
        i8f = sb("i8f", [128, 8])
        iota8 = sb("iota8", [128, E0])
        diff = sb("diff", [128, 1])
        ex = sb("ex_l0", [128, 1])
        den = sb("den_l0", [128, 1])
        pr = sb("pr", [128, 2])
        wa = sb("wa", [128, E0])
        wb = sb("wb", [128, E0])
        wf = sb("wf", [128, E0])
        low = sb("low", [128, E0 * R0])
        lowT_hi = sb("lowT_hi", [128, 128], F32R)
        lowT_lo = sb("lowT_lo", [128, 128], F32R)
        x1 = sb("x1_l0", [128, D])
        x1T = sb("x1T_l0", [128, 2, KT, 128], F32R)

        p_y = ps("p_y", [128, KT, 128])
        p_r = ps("p_r", [128, D])
        p_lg = ps("p_lg", [128, 512])
        p_t = ps("p_t", [128, 512])
        p_x = ps("p_x", [128, KT, 128])

        s_tick_sp, s_tick_dve = sem("l0_tick_sp"), sem("l0_tick_dve")
        s_const = sem("l0_const")
        s_ids = sem("l0_ids")
        s_wts = sem("l0_wts")
        s_w = [sem("l0_w0"), sem("l0_w1")]
        s_tab = sem("l0_tab")
        s_red = sem("l0_red")
        s_trig = sem("l0_trig")
        s_tables = sem("l0_tables")
        s_whi, s_wlo = sem("l0_whi"), sem("l0_wlo")
        s_bhi, s_blo = sem("l0_bhi"), sem("l0_blo")
        s_xb = sem("l0_xb")
        s_y = sem("l0_y")
        s_yhi, s_ylo = sem("l0_yhi"), sem("l0_ylo")
        s_lg = sem("l0_lg")
        s_gate = sem("l0_gate")
        s_exp = sem("l0_exp")
        s_low = sem("l0_low")
        s_lt = sem("l0_lt")
        s_lthi, s_ltlo = sem("l0_lthi"), sem("l0_ltlo")
        s_r = sem("l0_r")
        s_x1 = sem("l0_x1")
        s_xt = sem("l0_xt")
        s_xthi, s_xtlo = sem("l0_xthi"), sem("l0_xtlo")
        s_mask = sem("l0_mask")
        s_mst = sem("l0_mst")
        s_st = sem("l0_st")
        s_stT = sem("l0_stT")

        block = ctx.enter_context(nc.Block())

        @block.sync
        def _(sp):
            sp.dma_start(ids[:, :], t["lora_id"].rearrange("(o b) -> o b", o=1)).then_inc(s_ids, 16)
            sp.dma_start(seq_i[:, :], t["seq"].rearrange("(o b) -> o b", o=1).to_broadcast([128, B])).then_inc(s_const, 16)
            sp.dma_start(tok[:, :], t["tok"]).then_inc(s_const, 16)
            sp.dma_start(invf[:, :], t["invf"].rearrange("(o n) -> o n", o=1).to_broadcast([128, 64])).then_inc(s_const, 16)
            sp.dma_start(normw[:, 0, :], t["qn"].rearrange("(o n) -> o n", o=1).to_broadcast([128, 128])).then_inc(s_const, 16)
            sp.dma_start(normw[:, 1, :], t["kn"].rearrange("(o n) -> o n", o=1).to_broadcast([128, 128])).then_inc(s_const, 16)
            sp.dma_start(keyno[:, :], t["keyno"].rearrange("(o n) -> o n", o=1)).then_inc(s_const, 16)
            sp.dma_start(iota8[:, :], t["keyno"][0:E0].rearrange("(o n) -> o n", o=1).to_broadcast([128, E0])).then_inc(s_const, 16)
            sp.dma_start(ident[:, :], t["ident"]).then_inc(s_const, 16)
            sp.wait_ge(s_ids, 16)

            def load(b, slot):
                a = sp.value_load(ids[0:1, bass.ds(b, 1)], min_val=0, max_val=7)
                sp.dma_start(w_raw[:, slot, :, :],
                             t["loraT"][bass.ds(a, 1)].rearrange("o (k p) n -> p (o k) n", p=128)).then_inc(s_w[slot], 16)
                sp.dma_start(xT_raw[:, slot, :, :],
                             t["xT"][bass.ds(b, 1)].rearrange("o (k p) n -> p (o k) n", p=128)).then_inc(s_w[slot], 16)
                sp.dma_start(x_raw[:, slot, :], t["x"][bass.ds(b, 1)].rearrange("o p n -> (o p) n")).then_inc(s_w[slot], 16)

            load(0, 0)
            load(1, 1)
            sp.dma_start(base_raw[:, :, :], t["baseT"].rearrange("(k p) n -> p k n", p=128)).then_inc(s_wts, 16)
            sp.dma_start(lg_raw[:, :, :], t["lgT"].rearrange("(k p) n -> p k n", p=128)).then_inc(s_wts, 16)
            sp.dma_start(lb_raw[:, :], t["loraBT"]).then_inc(s_wts, 16)
            sp.dma_start(bias[:, :], t["base_b"].rearrange("(o n) -> o n", o=1).to_broadcast([128, D])).then_inc(s_wts, 16)
            sp.wait_ge(s_mask, 1 + B)
            sp.dma_start(dram["mask"].rearrange("(o b) n -> o (b n)", o=1), mask[:, :, :].rearrange("p b n -> p (b n)")).then_inc(s_mst, 16)
            sp.wait_ge(s_mst, 16)
            with sp.Fori(1, B // 2) as i:
                for slot in range(2):
                    wait_alone(sp, s_tick_sp, (s_blo, 4 * i + 2 * slot - 2), (s_xb, 2 * i + slot - 1))
                    load(2 * i + slot, slot)

        @block.gpsimd
        def _(pool):
            nc.gpsimd.memset(yacc[:, :, :], 0.0).then_inc(s_tables, 1)
            nc.gpsimd.memset(mask[:, :, L:NKEY], 0.0).then_inc(s_mask, 1)
            pool.wait_ge(s_wts, 64)
            with pool.Fori(0, B // 2) as i:
                for slot in range(2):
                    pool.wait_ge(s_w[slot], 48 * i + 48)
                    pool.wait_ge(s_x1, 2 * i + slot + 1)
                    nc.gpsimd.tensor_tensor(xb[:, :], x_raw[:, slot, :], bias[:, :], ALU.add).then_inc(s_xb, 1)

        @block.vector
        def _(dve):
            V = nc.vector
            step = [0]

            def link(ins):
                step[0] += 1
                ins.then_inc(s_tab, 1)
                dve.wait_ge(s_tab, step[0])

            dve.wait_ge(s_const, 8 * 16)
            link(V.tensor_copy(seq_f[:, :], seq_i[:, :]))
            link(V.tensor_scalar(pos[:, :], seq_f[:, :], tok[:, 0:1], None, ALU.add))
            link(V.tensor_tensor(ang[:, :, :], pos[:, :].unsqueeze(2).to_broadcast([128, B, 64]),
                                 invf[:, :].unsqueeze(1).to_broadcast([128, B, 64]), ALU.mult))
            for c in range(2):
                link(V.tensor_scalar(turn[:, c], ang[:, :, :], 1 / 6.283185307179586, 0.25 * c, ALU.mult, ALU.add))
                link(V.tensor_scalar(turn[:, c], turn[:, c], ROUND, None, ALU.add))
                link(V.tensor_scalar(turn[:, c], turn[:, c], ROUND, None, ALU.subtract))
                link(V.scalar_tensor_tensor(out=red[:, c], in0=turn[:, c], scalar=-TWO_PI_HI, in1=ang[:, :, :], op0=ALU.mult, op1=ALU.add))
                link(V.scalar_tensor_tensor(out=red[:, c], in0=turn[:, c], scalar=-TWO_PI_MID, in1=red[:, c], op0=ALU.mult, op1=ALU.add))
                link(V.scalar_tensor_tensor(out=red[:, c], in0=turn[:, c], scalar=-TWO_PI_LO, in1=red[:, c], op0=ALU.mult, op1=ALU.add))
                if c:
                    link(V.tensor_scalar(red[:, c], red[:, c], 1.5707963267948966, None, ALU.add))
                link(V.tensor_scalar(red[:, c], red[:, c], PI_SAFE, -PI_SAFE, ALU.min, ALU.max))
            V.engine_nop().then_inc(s_red, 1)
            for b in range(B):
                V.tensor_scalar(mask[:, b, 0:L], keyno[:, :], seq_f[0:1, b:b + 1], NEG, ALU.is_ge, ALU.mult).then_inc(s_mask, 1)

            dve.wait_ge(s_whi, 3)
            V.tensor_tensor(base_lo[:, :, :], base_raw[:, :, :], base_hi[:, :, :].bitcast(F32), ALU.subtract)
            V.tensor_tensor(lg_lo[:, :, :], lg_raw[:, :, :], lg_hi[:, :, :].bitcast(F32), ALU.subtract)
            V.tensor_tensor(lb_lo[:, :], lb_raw[:, :], lb_hi[:, :].bitcast(F32), ALU.subtract).then_inc(s_wlo, 1)
            dve.wait_ge(s_trig, 2)
            for n in range(2):
                for half in range(2):
                    own = normw[:, n, 64 * half:64 * half + 64].unsqueeze(1).to_broadcast([128, B, 64])
                    other = normw[:, n, 64 - 64 * half:128 - 64 * half].unsqueeze(1).to_broadcast([128, B, 64])
                    V.tensor_tensor(rope[:, :, n, 0, 64 * half:64 * half + 64], trig[:, 1], own, ALU.mult).then_inc(s_tables, 1)
                    V.scalar_tensor_tensor(out=rope[:, :, n, 1, 64 * half:64 * half + 64], in0=trig[:, 0],
                                           scalar=(1.0 if half else -1.0), in1=other, op0=ALU.mult, op1=ALU.mult).then_inc(s_tables, 1)
            V.engine_nop().then_inc(s_x1, 1)

            with dve.Fori(0, B // 2) as i:
                for slot in range(2):
                    n = 2 * i + slot
                    dve.wait_ge(s_bhi, 2 * n + 2)
                    V.tensor_tensor(w_lo[:, :, :], w_raw[:, slot], w_hi[:, :, :].bitcast(F32), ALU.subtract).then_inc(s_blo, 1)
                    V.tensor_tensor(xT_lo[:, :, :], xT_raw[:, slot], xT_hi[:, :, :].bitcast(F32), ALU.subtract).then_inc(s_blo, 1)
                    dve.wait_ge(s_yhi, n + 1)
                    V.tensor_tensor(yT_lo[:, :, :], p_y[:, :, :], yT_hi[:, :, :].bitcast(F32), ALU.subtract).then_inc(s_ylo, 1)
                    dve.wait_ge(s_lg, n + 1)
                    V.tensor_copy(lgs[:, :], p_lg[:, E0 * R0:NLG]).then_inc(s_gate, 1)
                    wait_alone(dve, s_tick_dve, (s_gate, 11 * n + 1))
                    V.max(v8[:, :], lgs[:, :]).then_inc(s_gate, 1)
                    dve.wait_ge(s_gate, 11 * n + 2)
                    V.tensor_tensor(diff[:, :], v8[:, 1:2], v8[:, 0:1], ALU.subtract).then_inc(s_gate, 1)
                    dve.wait_ge(s_wlo, 1)
                    V.max_index(i8[:, :], v8[:, :], lgs[:, :]).then_inc(s_gate, 1)
                    dve.wait_ge(s_gate, 11 * n + 4)
                    V.tensor_copy(i8f[:, :], i8[:, :]).then_inc(s_gate, 1)
                    dve.wait_ge(s_exp, n + 1)
                    V.tensor_scalar(den[:, :], ex[:, :], 1.0, None, ALU.add).then_inc(s_gate, 1)
                    dve.wait_ge(s_gate, 11 * n + 6)
                    V.reciprocal(pr[:, 0:1], den[:, :]).then_inc(s_gate, 1)
                    dve.wait_ge(s_gate, 11 * n + 7)
                    V.tensor_tensor(pr[:, 1:2], pr[:, 0:1], ex[:, :], ALU.mult).then_inc(s_gate, 1)
                    dve.wait_ge(s_gate, 11 * n + 8)
                    V.tensor_scalar(wa[:, :], iota8[:, :], i8f[:, 0:1], pr[:, 0:1], ALU.is_equal, ALU.mult).then_inc(s_gate, 1)
                    V.tensor_scalar(wb[:, :], iota8[:, :], i8f[:, 1:2], pr[:, 1:2], ALU.is_equal, ALU.mult).then_inc(s_gate, 1)
                    dve.wait_ge(s_gate, 11 * n + 10)
                    V.tensor_tensor(wf[:, :], wa[:, :], wb[:, :], ALU.add).then_inc(s_gate, 1)
                    dve.wait_ge(s_gate, 11 * n + 11)
                    V.scalar_tensor_tensor(out=low[:, :].rearrange("p (e r) -> p e r", e=E0),
                                           in0=p_lg[:, 0:E0 * R0].rearrange("p (e r) -> p e r", e=E0), scalar=2.0,
                                           in1=wf[:, :].unsqueeze(2).to_broadcast([128, E0, R0]),
                                           op0=ALU.mult, op1=ALU.mult).then_inc(s_low, 1)
                    dve.wait_ge(s_lthi, n + 1)
                    V.tensor_tensor(lowT_lo[:, :], p_t[:, 0:128], lowT_hi[:, :].bitcast(F32), ALU.subtract).then_inc(s_ltlo, 1)
                    dve.wait_ge(s_r, n + 1)
                    dve.wait_ge(s_xb, n + 1)
                    dve.wait_ge(s_st, 16 * n)
                    V.tensor_tensor(x1[:, :], p_r[:, :], xb[:, :], ALU.add).then_inc(s_x1, 1)
                    dve.wait_ge(s_xthi, n + 1)
                    V.tensor_tensor(x1T[:, 1], p_x[:, :, :], x1T[:, 0].bitcast(F32), ALU.subtract).then_inc(s_xtlo, 1)

        @block.scalar
        def _(act):
            A = nc.scalar
            act.wait_ge(s_red, 1)
            A.activation(trig[:, 0], red[:, 0], ACT.Sin).then_inc(s_trig, 1)
            A.activation(trig[:, 1], red[:, 1], ACT.Sin).then_inc(s_trig, 1)
            act.wait_ge(s_wts, 64)
            A.activation(base_hi[:, :, :], base_raw[:, :, :], ACT.Copy).then_inc(s_whi, 1)
            A.activation(lg_hi[:, :, :], lg_raw[:, :, :], ACT.Copy).then_inc(s_whi, 1)
            A.activation(lb_hi[:, :], lb_raw[:, :], ACT.Copy).then_inc(s_whi, 1)
            with act.Fori(0, B // 2) as i:
                for slot in range(2):
                    n = 2 * i + slot
                    act.wait_ge(s_w[slot], 48 * i + 48)
                    act.wait_ge(s_x1, n + 1)
                    A.activation(w_hi[:, :, :], w_raw[:, slot], ACT.Copy).then_inc(s_bhi, 1)
                    A.activation(xT_hi[:, :, :], xT_raw[:, slot], ACT.Copy).then_inc(s_bhi, 1)
                    act.wait_ge(s_y, n + 1)
                    A.activation(yT_hi[:, :, :], p_y[:, :, :], ACT.Copy).then_inc(s_yhi, 1)
                    act.wait_ge(s_gate, 11 * n + 3)
                    A.activation(ex[:, :], diff[:, :], ACT.Exp).then_inc(s_exp, 1)
                    act.wait_ge(s_lt, n + 1)
                    A.activation(lowT_hi[:, :], p_t[:, 0:128], ACT.Copy).then_inc(s_lthi, 1)
                    act.wait_ge(s_x1, n + 2)
                    act.dma_start(dram["x1"][bass.ds(n, 1)].rearrange("o p n -> (o p) n"), x1[:, :]).then_inc(s_st, 16)
                    act.wait_ge(s_xt, n + 1)
                    act.wait_ge(s_stT, 16 * n)
                    A.activation(x1T[:, 0], p_x[:, :, :], ACT.Copy).then_inc(s_xthi, 1)
                    act.wait_ge(s_xtlo, n + 1)
                    act.dma_start(dram["x1T"][bass.ds(n, 1)].rearrange("o p n -> (o p) n"),
                                  x1T[:, :, :, :].bitcast(F32).rearrange("p a k n -> p (a k n)")).then_inc(s_stT, 16)
            act.wait_ge(s_st, 16 * B)
            act.wait_ge(s_stT, 16 * B)

        @block.tensor
        def _(pe):
            PE = nc.tensor
            pe.wait_ge(s_wlo, 1)
            pe.wait_ge(s_const, 128)
            with pe.Fori(0, B // 2) as i:
                for slot in range(2):
                    n = 2 * i + slot
                    pe.wait_ge(s_blo, 2 * n + 2)
                    for o in range(KT):
                        terms = [(w, x, k) for w, x in ((w_hi, xT_hi), (w_hi, xT_lo), (w_lo, xT_hi)) for k in range(KT)]
                        for m, (w, x, k) in enumerate(terms):
                            mm = PE.matmul(p_y[:, o, :], w[:, k, 128 * o:128 * o + 128], x[:, k, :],
                                           start=(m == 0), stop=(m == len(terms) - 1))
                    mm.then_inc(s_y, 1)
                    pe.wait_ge(s_ylo, n + 1)
                    for m, (y, w, k) in enumerate([(y, w, k) for y, w in ((yT_hi, lg_hi), (yT_hi, lg_lo), (yT_lo, lg_hi)) for k in range(KT)]):
                        mm = PE.matmul(p_lg[:, 0:NLG], y[:, k, :], w[:, k, :], start=(m == 0), stop=(m == 3 * KT - 1))
                    mm.then_inc(s_lg, 1)
                    for m, (y, w, k) in enumerate([(y, w, k) for y, w in ((yT_hi, base_hi), (yT_hi, base_lo), (yT_lo, base_hi)) for k in range(KT)]):
                        PE.matmul(p_r[:, :], y[:, k, :], w[:, k, :], start=(m == 0), stop=False)
                    pe.wait_ge(s_low, n + 1)
                    PE.transpose(p_t[:, 0:128], low[:, :], ident[:, :]).then_inc(s_lt, 1)
                    pe.wait_ge(s_ltlo, n + 1)
                    for m, (a, w) in enumerate(((lowT_hi, lb_hi), (lowT_hi, lb_lo), (lowT_lo, lb_hi))):
                        mm = PE.matmul(p_r[:, :], a[:, :], w[:, :], start=False, stop=(m == 2))
                    mm.then_inc(s_r, 1)
                    pe.wait_ge(s_x1, n + 2)
                    for k in range(KT):
                        mm = PE.transpose(p_x[:, k, :], x1[:, 128 * k:128 * k + 128], ident[:, :])
                    mm.then_inc(s_xt, 1)


def attention(nc, t, dram, keep):
    with ExitStack() as ctx:
        def sb(name, shape, dt=F32):
            return ctx.enter_context(nc.sbuf_tensor(name, shape, dt))

        def ps(name, shape, dt=F32):
            return ctx.enter_context(nc.psum_tensor(name, shape, dt))

        def sem(name):
            return ctx.enter_context(nc.semaphore(name))

        ident, rope, yacc = keep["ident"], keep["rope"], keep["yacc"]
        mask = sb("mask", [128, 2, NKEY], BF16)
        pages = sb("pages", [1, B * NPP], I32)
        w_raw = sb("wg_raw", [128, 2, CH])
        w_hi = sb("wg_hi", [128, 2 * WCOLS], F32R)
        w_lo = sb("wg_lo", [128, 2 * WCOLS], F32R)
        xT = sb("xT", [128, 2, 2, KT, 128], F32R)
        kv = sb("kv", [128, 2, LT, 2, HD])
        kT_hi = sb("kT_hi", [128, NKEY], F32R)
        kT_lo = sb("kT_lo", [128, NKEY], F32R)
        v_hi = sb("v_hi", [128, 2, KTILES, HD], F32R)
        v_lo = sb("v_lo", [128, 2, KTILES, HD], F32R)
        qT_hi = sb("qT_hi", [128, GQ], F32R)
        qT_lo = sb("qT_lo", [128, GQ], F32R)
        rot_a = sb("rot_a", [128, REP, HD])
        rot_b = sb("rot_b", [128, REP, HD])
        krot_a = sb("krot_a", [128, HD])
        krot_b = sb("krot_b", [128, HD])
        junk = sb("junk", [128, REP + 1, HD])
        ss = sb("ss", [128, REP + 1])
        rs_a = sb("rs_a", [128, REP + 1])
        rs_b = sb("rs_b", [128, REP + 1])
        rstd = sb("rstd", [128, 2, REP + 1])
        c_mul = sb("c_mul", [128, REP + 1])
        c_add = sb("c_add", [128, REP + 1])
        c_pow = sb("c_pow", [128, REP + 1])
        P = sb("P", [128, REP, NKEY])
        mx = sb("mx", [128, REP])
        nb = sb("nb", [128, REP])
        den = sb("den", [128, REP])
        rden = sb("rden", [128, 2, REP])
        bc = sb("bc", [128, S, REP])
        pT_hi = sb("pT_hi", [128, NPT, REP * S], F32R)
        pT_lo = sb("pT_lo", [128, NPT, REP * S], F32R)
        oT = sb("oT", [128, REP * S])
        oT_hi = sb("oT_hi", [128, REP * S], F32R)
        oT_lo = sb("oT_lo", [128, REP * S], F32R)

        bank = [ps(f"bank{n}", [128, 1024]) for n in range(2)]
        b_kv = ps("b_kv", [128, 512])
        b_q = ps("b_q", [128, 512])
        b_y = ps("b_y", [128, 512])
        b_o = ps("b_o", [128, 512])

        s_tick_sp, s_tick_dve, s_tick_pool = sem("s_tick_sp"), sem("s_tick_dve"), sem("s_tick_pool")
        s_pg = sem("s_pg")
        s_c = sem("s_c")
        s_wraw = [sem("s_wraw0"), sem("s_wraw1")]
        s_xT = [sem("s_xT0"), sem("s_xT1")]
        s_kv = [sem("s_kv0"), sem("s_kv1")]
        s_mk = [sem("s_mk0"), sem("s_mk1")]
        s_rw = sem("s_rw")
        s_bc = sem("s_bc")
        s_ws = sem("s_ws")
        s_wh = sem("s_wh")
        s_kvp = sem("s_kvp")
        s_qp = sem("s_qp")
        s_sc = sem("s_sc")
        s_y = sem("s_y")
        s_pt = sem("s_pt")
        s_pv = sem("s_pv")
        s_kcT = sem("s_kcT")
        s_qkT = sem("s_qkT")
        s_sq = sem("s_sq")
        s_vh = sem("s_vh")
        s_ex = sem("s_ex")
        s_pth = sem("s_pth")
        s_kch = sem("s_kch")
        s_qkh = sem("s_qkh")
        s_oh = sem("s_oh")
        s_mx = sem("s_mx")
        s_nb = sem("s_nb")
        s_rq = sem("s_rq")
        s_rk = sem("s_rk")
        s_kr = sem("s_kr")
        s_rd = sem("s_rd")
        s_ya = sem("s_ya")
        s_ptl = sem("s_ptl")
        s_qkl = sem("s_qkl")
        s_ot = sem("s_ot")
        s_rs = sem("s_rs")
        s_qa = sem("s_qa")
        s_vc = sem("s_vc")
        s_vs = sem("s_vs")
        s_ol = sem("s_ol")

        block = ctx.enter_context(nc.Block())
        LAST = UNITS - 1

        @block.sync
        def _(sp):
            sp.dma_start(pages[:, :], t["pages"].rearrange("(o b) p -> o (b p)", o=1)).then_inc(s_pg, 16)
            sp.wait_ge(s_pg, 16)

            def load_x(u, par):
                sp.dma_start(xT[:, par].bitcast(F32).rearrange("p a k n -> p (a k n)"),
                             dram["x1T"][bass.ds(u % B, 1)].rearrange("o p n -> (o p) n")).then_inc(s_xT[par], 16)

            def load_mask(u, par):
                sp.dma_start(mask[:, par], dram["mask"][bass.ds(u % B, 1)].to_broadcast([128, NKEY])).then_inc(s_mk[par], 16)

            def load_w(n, par):
                sp.dma_start(w_raw[:, par], t["wg"][bass.ds(n % UNITS, 1)].rearrange("o p n -> (o p) n")).then_inc(s_wraw[par], 16)

            def page_numbers(u):
                return nc.values_load_multi_w_load_instructions(
                    pages[0:1, bass.ds((u % B) * NPP, NPP)], engines=(mybir.EngineType.SP,), min_val=0, max_val=63)[1]

            def load_kv(u, par, numbers, j0, j1):
                for j in range(j0, j1):
                    page = numbers[j]
                    at = PAGE * (j % 4)
                    src = t["kv"][bass.ds(u // B, 1), bass.ds(page, 1)]
                    sp.dma_start(kv[at:at + PAGE, par, j // 4].rearrange("p a d -> p (a d)"),
                                 src.rearrange("g o k n -> (g o k) n")).then_inc(s_kv[par], 16)

            def rden_out(u, par):
                wait_alone(sp, s_tick_sp, (s_rd, u + 1))
                sp.dma_start(dram["rden"], rden[:, par]).then_inc(s_rw, 16)

            def rden_in(u, skip=False):
                wait_alone(sp, s_tick_sp, (s_rw, 16 * (u + 1)), *([(s_ot, u)] if not skip else []))
                sp.dma_start(bc[:, :, :].rearrange("p s h -> p (s h)"),
                             dram["rden"].rearrange("(o s) h -> o (s h)", o=1).to_broadcast([128, S * REP])).then_inc(s_bc, 16)

            load_mask(0, 0)
            load_mask(1, 1)
            load_w(0, 0)
            load_x(0, 0)
            load_kv(0, 0, page_numbers(0), 0, NPP)
            load_w(1, 1)
            load_x(1, 1)
            load_kv(1, 1, page_numbers(1), 0, NPP)
            for n in range(2, B + 2):
                sp.wait_ge(s_ws, n - 1)
                load_w(n, n % 2)

            def unit(u, par, n, more=True, weights=True):
                if more:
                    wait_alone(sp, s_tick_sp, (s_qp, u + 1))
                    load_x(u + 2, par)
                    wait_alone(sp, s_tick_sp, (s_kcT, u + 1), (s_vs, u + 1))
                    numbers = page_numbers(u + 2)
                    load_kv(u + 2, par, numbers, 0, NPP // 2)
                rden_out(u, par)
                if more:
                    load_mask(u + 2, par)
                    load_kv(u + 2, par, numbers, NPP // 2, 3 * NPP // 4)
                rden_in(u, n == "first")
                if more:
                    load_kv(u + 2, par, numbers, 3 * NPP // 4, NPP)
                if weights:
                    wait_alone(sp, s_tick_sp, (s_ws, u + B + 1))
                    load_w(u + B + 2, par)

            unit(0, 0, "first")
            with sp.Fori(0, (UNITS - 4) // 2) as i:
                unit(2 * i + 1, 1, "body")
                unit(2 * i + 2, 0, "body")
            unit(LAST - 2, 1, "body", weights=False)
            unit(LAST - 1, 0, "body", more=False, weights=False)
            unit(LAST, 1, "last", more=False, weights=False)

        @block.tensor
        def _(pe):
            PE = nc.tensor

            def project(u, par):
                at = ((u // B) % 2) * WCOLS
                pe.wait_ge(s_xT[par], (u // 2) * 16 + 16)
                pe.wait_ge(s_ws, (u // B) * B + 5)
                terms = [(a, w, k) for a, w in ((0, w_hi), (0, w_lo), (1, w_hi)) for k in range(KT)]
                for m, (a, w, k) in enumerate(terms):
                    mm = PE.matmul(b_kv[:, 0:2 * HD], xT[:, par, a, k], w[:, bass.ds(at + WQ + 2 * HD * k, 2 * HD)],
                                   start=(m == 0), stop=(m == len(terms) - 1))
                mm.then_inc(s_kvp, 1)
                for m, (a, w, k) in enumerate(terms):
                    mm = PE.matmul(b_q[:, :], xT[:, par, a, k], w[:, bass.ds(at + GQ * k, GQ)],
                                   start=(m == 0), stop=(m == len(terms) - 1))
                mm.then_inc(s_qp, 1)

            def turn(u, par):
                pe.wait_ge(s_kv[par], (u // 2) * 16 * NPP + 16 * NPP)
                if not isinstance(u, int) or u > 0:
                    pe.wait_ge(s_ya, u)
                for k in range(LT):
                    mm = PE.transpose(b_y[:, 128 * k:128 * k + 128], kv[:, par, k, 0], ident[:, :])
                mm.then_inc(s_kcT, 1)
                pe.wait_ge(s_kr, 2 * u + 2)
                PE.transpose(b_kv[:, 0:128], krot_a[:, :], ident[:, :])
                pe.wait_ge(s_qa, u + 1)
                for h in range(REP):
                    mm = PE.transpose(b_q[:, 128 * h:128 * h + 128], rot_a[:, h], ident[:, :])
                mm.then_inc(s_qkT, 1)

            def scores(u, par):
                pe.wait_ge(s_qkl, 3 * u + 3)
                for h in range(REP):
                    if h >= 2:
                        pe.wait_ge(s_mx, 4 * u + h - 1)
                    out = bank[h % 2]
                    q = slice(128 * h, 128 * h + 128)
                    terms = ((qT_hi, kT_hi), (qT_hi, kT_lo), (qT_lo, kT_hi))
                    for m, (a, k) in enumerate(terms):
                        PE.matmul(out[:, 0:L], a[:, q], k[:, 0:L], start=(m == 0), stop=(m == 2))
                        mm = PE.matmul(out[:, L:NKEY], a[:, q], k[:, L:NKEY], start=(m == 0), stop=(m == 2))
                    mm.then_inc(s_sc, 1)

            def output(u):
                at = ((u // B) % 2) * WCOLS + WQ + WKV
                pe.wait_ge(s_ol, u + 1)
                pe.wait_ge(s_ws, (u // B) * B + B)
                terms = [(o, w, h) for o, w in ((oT_hi, w_hi), (oT_hi, w_lo), (oT_lo, w_hi)) for h in range(REP)]
                for m, (o, w, h) in enumerate(terms):
                    mm = PE.matmul(b_y[:, :], o[:, 128 * h:128 * h + 128], w[:, bass.ds(at + D * h, D)],
                                   start=(m == 0), stop=(m == len(terms) - 1))
                mm.then_inc(s_y, 1)

            def p_turn(u, k):
                for h in range(REP):
                    mm = PE.transpose(bank[(k % 4) // 2][:, 512 * (k % 2) + 128 * h:512 * (k % 2) + 128 * h + 128],
                                      P[:, h, 128 * k:128 * k + 128], ident[:, :])
                mm.then_inc(s_pt, 1)

            def pv(u, par, k):
                pe.wait_ge(s_ptl, 5 * u + k + 1)
                for m, (v, p) in enumerate(((v_hi, pT_hi), (v_lo, pT_hi), (v_hi, pT_lo))):
                    mm = PE.matmul(b_o[:, :], v[:, par, k], p[:, k % NPT], start=(k == 0 and m == 0),
                                   stop=(k == KTILES - 1 and m == 2))
                mm.then_inc(s_pv, 1)

            def unit(u, par, n):
                scores(u, par)
                if n != "last":
                    project(u + 1, 1 - par)
                if n != "first":
                    output(u - 1)
                pe.wait_ge(s_ex, 4 * u + 4)
                for k in range(4):
                    p_turn(u, k)
                pe.wait_ge(s_vs, u + 1)
                pv(u, par, 0)
                p_turn(u, 4)
                if n != "last":
                    turn(u + 1, 1 - par)
                for k in range(1, KTILES):
                    pv(u, par, k)

            project(0, 0)
            turn(0, 0)
            unit(0, 0, "first")
            with pe.Fori(0, (UNITS - 2) // 2) as i:
                unit(2 * i + 1, 1, "body")
                unit(2 * i + 2, 0, "body")
            unit(LAST, 1, "last")
            output(LAST)

        @block.scalar
        def _(act):
            A = nc.scalar

            def own(u, par):
                act.wait_ge(s_kvp, u + 1)
                A.activation(v_hi[:, par, LT], b_kv[:, HD:2 * HD], ACT.Copy).then_inc(s_vh, 1)
                A.activation(junk[:, REP], b_kv[:, 0:HD], ACT.Square, accum_out=ss[:, REP:REP + 1]).then_inc(s_sq, 1)
                act.wait_ge(s_qp, u + 1)
                for h in range(REP):
                    A.activation(junk[:, h], b_q[:, 128 * h:128 * h + 128], ACT.Square, accum_out=ss[:, h:h + 1]).then_inc(s_sq, 1)

            def turned(u, par):
                act.wait_ge(s_kcT, u + 1)
                A.activation(kT_hi[:, 0:L], b_y[:, :], ACT.Copy).then_inc(s_kch, 1)
                act.wait_ge(s_qkT, u + 1)
                A.activation(kT_hi[:, L:NKEY], b_kv[:, 0:128], ACT.Copy).then_inc(s_qkh, 1)
                A.activation(qT_hi[:, :], b_q[:, :], ACT.Copy).then_inc(s_qkh, 1)

            def p_hi(u, k):
                act.wait_ge(s_pt, 5 * u + k + 1)
                if k >= NPT:
                    act.wait_ge(s_pv, 5 * u + k - NPT + 1)
                A.activation(pT_hi[:, k % NPT], bank[(k % 4) // 2][:, 512 * (k % 2):512 * (k % 2) + 512], ACT.Copy).then_inc(s_pth, 1)

            def out_hi(u):
                act.wait_ge(s_ot, u + 1)
                A.activation(oT_hi[:, :], oT[:, :], ACT.Copy).then_inc(s_oh, 1)

            def unit(u, par, n):
                for h in range(REP):
                    act.wait_ge(s_nb, 4 * u + h + 1)
                    A.activation(P[:, h], P[:, h], ACT.Exp, bias=nb[:, h:h + 1], scale=rstd[:, par, h:h + 1],
                                 accum_out=den[:, h:h + 1]).then_inc(s_ex, 1)
                    if h == 1 and n != "first":
                        out_hi(u - 1)
                if n != "last":
                    own(u + 1, 1 - par)
                for k in range(KTILES):
                    p_hi(u, k)
                if n != "last":
                    turned(u + 1, 1 - par)

            own(0, 0)
            turned(0, 0)
            unit(0, 0, "first")
            with act.Fori(0, (UNITS - 2) // 2) as i:
                unit(2 * i + 1, 1, "body")
                unit(2 * i + 2, 0, "body")
            unit(LAST, 1, "last")
            out_hi(LAST)

        @block.vector
        def _(dve):
            V = nc.vector
            V.engine_nop().then_inc(s_ya, 1)

            def tab(at, n, j, lo, hi, reps):
                a = rope[:, bass.ds(at, 1), n, j, lo:hi]
                return a.to_broadcast([128, reps, hi - lo]) if reps > 1 else a

            def rotate_q(u):
                at = u % B
                dve.wait_ge(s_sq, 5 * u + 5)
                q = b_q[:, :].rearrange("p (h d) -> p h d", h=REP)

                V.tensor_tensor(rot_a[:, :, :], q, tab(at, 0, 0, 0, HD, REP), ALU.mult).then_inc(s_rq, 1)
                V.tensor_tensor(rot_b[:, :, 0:64], q[:, :, 64:128], tab(at, 0, 1, 0, 64, REP), ALU.mult).then_inc(s_rq, 1)
                V.tensor_tensor(rot_b[:, :, 64:128], q[:, :, 0:64], tab(at, 0, 1, 64, 128, REP), ALU.mult).then_inc(s_rq, 1)

            def rotate_k(u, par):
                at = u % B
                dve.wait_ge(s_rs, 3 * u + 3)
                rk = rstd[:, par, REP:REP + 1]
                k1 = b_kv[:, 0:HD].unsqueeze(1)
                V.scalar_tensor_tensor(out=krot_a[:, :].unsqueeze(1), in0=k1, scalar=rk, in1=tab(at, 1, 0, 0, HD, 1),
                                       op0=ALU.mult, op1=ALU.mult).then_inc(s_rk, 1)
                V.scalar_tensor_tensor(out=krot_b[:, 0:64].unsqueeze(1), in0=k1[:, :, 64:128], scalar=rk, in1=tab(at, 1, 1, 0, 64, 1),
                                       op0=ALU.mult, op1=ALU.mult).then_inc(s_rk, 1)
                V.scalar_tensor_tensor(out=krot_b[:, 64:128].unsqueeze(1), in0=k1[:, :, 0:64], scalar=rk, in1=tab(at, 1, 1, 64, 128, 1),
                                       op0=ALU.mult, op1=ALU.mult).then_inc(s_rk, 1)
                dve.wait_ge(s_vh, u + 1)
                V.tensor_tensor(v_lo[:, par, LT], b_kv[:, HD:2 * HD], v_hi[:, par, LT].bitcast(F32), ALU.subtract).then_inc(s_kr, 1)
                dve.wait_ge(s_rk, 3 * u + 3)
                V.tensor_tensor(krot_a[:, :], krot_a[:, :], krot_b[:, :], ALU.add).then_inc(s_kr, 1)

            def turned(u, par):
                dve.wait_ge(s_kch, u + 1)
                V.tensor_tensor(kT_lo[:, 0:L], b_y[:, :], kT_hi[:, 0:L].bitcast(F32), ALU.subtract).then_inc(s_qkl, 1)
                dve.wait_ge(s_qkh, 2 * u + 2)
                V.tensor_tensor(kT_lo[:, L:NKEY], b_kv[:, 0:128], kT_hi[:, L:NKEY].bitcast(F32), ALU.subtract).then_inc(s_qkl, 1)
                V.tensor_tensor(qT_lo[:, :], b_q[:, :], qT_hi[:, :].bitcast(F32), ALU.subtract).then_inc(s_qkl, 1)

            def p_lo(u, k):
                dve.wait_ge(s_pth, 5 * u + k + 1)
                V.tensor_tensor(pT_lo[:, k % NPT], bank[(k % 4) // 2][:, 512 * (k % 2):512 * (k % 2) + 512],
                                pT_hi[:, k % NPT].bitcast(F32), ALU.subtract).then_inc(s_ptl, 1)

            def add_y(u):
                dve.wait_ge(s_y, u + 1)
                dve.wait_ge(s_ya, u + 1)
                ya = yacc[:, bass.ds(u % B, 1), :].rearrange("p o n -> p (o n)")
                V.tensor_tensor(ya, b_y[:, :], ya, ALU.add).then_inc(s_ya, 1)

            def unit(u, par, n):
                dve.wait_ge(s_mk[par], (u // 2) * 16 + 16)

                def biggest(h):
                    wait_alone(dve, s_tick_dve, (s_sc, 4 * u + h + 1))
                    V.tensor_tensor_reduce(out=P[:, h], in0=bank[h % 2][:, 0:NKEY], in1=mask[:, par], scale=1.0, scalar=-3e38,
                                           op0=ALU.add, op1=ALU.max, accum_out=mx[:, h:h + 1]).then_inc(s_mx, 1)

                def bias(h):
                    dve.wait_ge(s_mx, 4 * u + h + 1)
                    V.tensor_scalar(nb[:, h:h + 1], mx[:, h:h + 1], -1.0, rstd[:, par, h:h + 1], ALU.mult, ALU.mult).then_inc(s_nb, 1)

                biggest(0)
                biggest(1)
                bias(0)
                bias(1)
                if n != "first":
                    out_norm(u - 1)
                biggest(2)
                bias(2)
                biggest(3)
                bias(3)
                dve.wait_ge(s_ex, 4 * u + 4)
                V.reciprocal(rden[:, par], den[:, :]).then_inc(s_rd, 1)
                if n != "last":
                    rotate_q(u + 1)
                    rotate_k(u + 1, 1 - par)
                p_lo(u, 0)
                if n != "first":
                    add_y(u - 1)
                for k in range(1, KTILES):
                    p_lo(u, k)
                if n != "last":
                    turned(u + 1, 1 - par)

            def out_norm(u):
                dve.wait_ge(s_pv, 5 * u + 5)
                dve.wait_ge(s_bc, 16 * u + 16)
                V.tensor_tensor(oT[:, :].rearrange("p (h s) -> p h s", h=REP), b_o[:, :].rearrange("p (h s) -> p h s", h=REP),
                                bc[:, :, :].rearrange("p s h -> p h s"), ALU.mult).then_inc(s_ot, 1)

            rotate_q(0)
            rotate_k(0, 0)
            turned(0, 0)
            unit(0, 0, "first")
            with dve.Fori(0, (UNITS - 2) // 2) as i:
                unit(2 * i + 1, 1, "body")
                unit(2 * i + 2, 0, "body")
            unit(LAST, 1, "last")
            out_norm(LAST)
            add_y(LAST)

        @block.gpsimd
        def _(pool):
            G = nc.gpsimd
            G.memset(c_mul[:, 0:REP], 1.0).then_inc(s_c, 1)
            G.memset(c_mul[:, REP:REP + 1], 1.0 / HD).then_inc(s_c, 1)
            G.memset(c_add[:, 0:REP], HD * EPS).then_inc(s_c, 1)
            G.memset(c_add[:, REP:REP + 1], EPS).then_inc(s_c, 1)
            G.memset(c_pow[:, :], -0.5).then_inc(s_c, 1)

            def chunk(n, par, group_par, added=None):
                at = group_par * WCOLS + (n % B) * CH
                wait_alone(pool, s_tick_pool, *([(s_ya, added)] if added is not None else []), (s_wraw[par], (n // 2) * 16 + 16))
                G.tensor_copy(w_hi[:, bass.ds(at, CH)], w_raw[:, par]).then_inc(s_wh, 1)
                wait_alone(pool, s_tick_pool, (s_wh, n + 1))
                G.tensor_tensor(w_lo[:, bass.ds(at, CH)], w_raw[:, par], w_hi[:, bass.ds(at, CH)].bitcast(F32), ALU.subtract).then_inc(s_ws, 1)

            def norms(u, par):
                pool.wait_ge(s_sq, 5 * u + 5)
                G.tensor_tensor(rs_a[:, :], ss[:, :], c_mul[:, :], ALU.mult).then_inc(s_rs, 1)
                pool.wait_ge(s_rs, 3 * u + 1)
                G.tensor_tensor(rs_b[:, :], rs_a[:, :], c_add[:, :], ALU.add).then_inc(s_rs, 1)
                pool.wait_ge(s_rs, 3 * u + 2)
                G.tensor_tensor(rstd[:, par], rs_b[:, :], c_pow[:, :], ALU.pow).then_inc(s_rs, 1)

            def add_q(u):
                pool.wait_ge(s_rq, 3 * u + 3)
                G.tensor_tensor(rot_a[:, :, :], rot_a[:, :, :], rot_b[:, :, :], ALU.add).then_inc(s_qa, 1)

            def values(u, par):
                wait_alone(pool, s_tick_pool, (s_kv[par], (u // 2) * 16 * NPP + 16 * NPP))
                G.tensor_copy(v_hi[:, par, 0:LT], kv[:, par, :, 1]).then_inc(s_vc, 1)
                pool.wait_ge(s_vc, u + 1)
                G.tensor_tensor(v_lo[:, par, 0:LT], kv[:, par, :, 1], v_hi[:, par, 0:LT].bitcast(F32), ALU.subtract).then_inc(s_vs, 1)

            def out_lo(u):
                pool.wait_ge(s_oh, u + 1)
                G.tensor_tensor(oT_lo[:, :], oT[:, :], oT_hi[:, :].bitcast(F32), ALU.subtract).then_inc(s_ol, 1)

            def unit(u, par, n):
                if n != "first":
                    out_lo(u - 1)
                if n != "last":
                    norms(u + 1, 1 - par)
                    add_q(u + 1)
                    chunk(u + B, par, (u // B + 1) % 2, u if n == "body" else None)
                    values(u + 1, 1 - par)

            pool.wait_ge(s_c, 5)
            for n in range(B):
                chunk(n, n % 2, 0)
            norms(0, 0)
            add_q(0)
            values(0, 0)
            unit(0, 0, "first")
            with pool.Fori(0, (UNITS - 2) // 2) as i:
                unit(2 * i + 1, 1, "body")
                unit(2 * i + 2, 0, "body")
            unit(LAST, 1, "last")
            out_lo(LAST)


def layer1_ffn(nc, t, dram, keep, out):
    with ExitStack() as ctx:
        def sb(name, shape, dt=F32):
            return ctx.enter_context(nc.sbuf_tensor(name, shape, dt))

        def ps(name, shape, dt=F32):
            return ctx.enter_context(nc.psum_tensor(name, shape, dt))

        def sem(name):
            return ctx.enter_context(nc.semaphore(name))

        ident, yacc = keep["ident"], keep["yacc"]
        NZ = NE * RANK
        a_raw = sb("a_raw", [128, KT, NZ])
        a_hi = sb("a_hi", [128, KT, NZ], F32R)
        a_lo = sb("a_lo", [128, KT, NZ], F32R)
        b_raw = sb("b_raw", [128, KT, D])
        b_hi = sb("b_hi", [128, KT, D], F32R)
        b_lo = sb("b_lo", [128, KT, D], F32R)
        r_raw = sb("r_raw", [128, KT, RD])
        r_hi = sb("r_hi", [128, KT, RD], F32R)
        r_lo = sb("r_lo", [128, KT, RD], F32R)
        keysT = sb("keysT", [RD, NE])
        yT_hi = sb("y1T_hi", [128, KT, 128], F32R)
        yT_lo = sb("y1T_lo", [128, KT, 128], F32R)
        rq = sb("rq", [128, RD])
        rqT = sb("rqT", [RD, 128])
        sc = sb("sc", [128, NE])
        v1 = sb("v1", [128, 8])
        v2 = sb("v2", [128, 8])
        r1 = sb("r1", [128, NE])
        r2 = sb("r2", [128, NE])
        nm = sb("nm", [128, 1])
        e = sb("e", [128, NE])
        sel = sb("sel", [128, NE])
        es = sb("es", [128, NE])
        tot = sb("tot", [128, 1])
        rt = sb("rt", [128, 1])
        gate = sb("gate", [128, NE])
        zg = sb("zg", [128, NZ])
        zT_hi = sb("zT_hi", [128, KT, 128], F32R)
        zT_lo = sb("zT_lo", [128, KT, 128], F32R)
        x1 = sb("x1_l1", [128, B, D])
        res = sb("res", [128, B, D])
        ybuf = sb("ybuf", [128, D])

        p_y = ps("p1_y", [128, 512])
        p_z = ps("p1_z", [128, 512])
        p_q = ps("p1_q", [128, 512])
        p_qT = ps("p1_qT", [128, 512])
        p_s = ps("p1_s", [128, 512])
        p_zT = ps("p1_zT", [128, 512])
        p_o = ps("p1_o", [128, 512])

        s_tick_sp, s_tick_dve = sem("f_tick_sp"), sem("f_tick_dve")
        s_in = sem("f_in")
        s_x1 = sem("f_x1")
        s_whi, s_wlo = sem("f_whi"), sem("f_wlo")
        s_yT = sem("f_yT")
        s_yhi, s_ylo = sem("f_yhi"), sem("f_ylo")
        s_z = sem("f_z")
        s_q = sem("f_q")
        s_qs = sem("f_qs")
        s_qT = sem("f_qT")
        s_qTs = sem("f_qTs")
        s_s = sem("f_s")
        s_g = sem("f_g")
        s_e = sem("f_e")
        s_zg = sem("f_zg")
        s_zT = sem("f_zT")
        s_zhi, s_zlo = sem("f_zhi"), sem("f_zlo")
        s_o = sem("f_o")
        s_res = sem("f_res")
        s_out = sem("f_out")
        s_yb = sem("f_yb")
        GS = 11

        block = ctx.enter_context(nc.Block())

        @block.sync
        def _(sp):
            sp.dma_start(r_raw[:, :, :], t["routerT"].rearrange("(k p) n -> p k n", p=128)).then_inc(s_in, 16)
            sp.dma_start(a_raw[:, :, :], t["AT"].rearrange("(k p) n -> p k n", p=128)).then_inc(s_in, 16)
            sp.dma_start(keysT[:, :], t["keysT"]).then_inc(s_in, 16)
            sp.dma_start(b_raw[:, :, :], t["BT"].rearrange("(k p) n -> p k n", p=128)).then_inc(s_in, 16)
            sp.dma_start(x1[:, :, :], dram["x1"].rearrange("b p n -> p b n")).then_inc(s_x1, 16)
            with sp.Fori(0, B) as n:
                wait_alone(sp, s_tick_sp, (s_res, n + 1))
                sp.dma_start(out[bass.ds(n, 1)].rearrange("o p n -> (o p) n"),
                             res[:, bass.ds(n, 1), :].rearrange("p o n -> p (o n)")).then_inc(s_out, 16)
            sp.wait_ge(s_out, 16 * B)

        @block.tensor
        def _(pe):
            PE = nc.tensor
            pe.wait_ge(s_wlo, 3)
            with pe.Fori(0, B) as n:
                pe.wait_ge(s_yb, n + 1)
                for k in range(KT):
                    mm = PE.transpose(p_y[:, 128 * k:128 * k + 128], ybuf[:, 128 * k:128 * k + 128], ident[:, :])
                mm.then_inc(s_yT, 1)
                pe.wait_ge(s_ylo, n + 1)
                terms = [(y, c, k) for y, c in ((yT_hi, 0), (yT_hi, 1), (yT_lo, 0)) for k in range(KT)]
                for m, (y, c, k) in enumerate(terms):
                    mm = PE.matmul(p_q[:, 0:RD], y[:, k, :], (r_hi, r_lo)[c][:, k, :], start=(m == 0), stop=(m == len(terms) - 1))
                mm.then_inc(s_q, 1)
                for m, (y, c, k) in enumerate(terms):
                    mm = PE.matmul(p_z[:, :], y[:, k, :], (a_hi, a_lo)[c][:, k, :], start=(m == 0), stop=(m == len(terms) - 1))
                mm.then_inc(s_z, 1)
                pe.wait_ge(s_qs, n + 1)
                PE.transpose(p_qT[0:RD, 0:128], rq[:, :], ident[:, :]).then_inc(s_qT, 1)
                pe.wait_ge(s_qTs, n + 1)
                PE.matmul(p_s[:, 0:NE], rqT[:, :], keysT[:, :], start=True, stop=True).then_inc(s_s, 1)
                pe.wait_ge(s_zg, n + 1)
                for k in range(KT):
                    mm = PE.transpose(p_zT[:, 128 * k:128 * k + 128], zg[:, 128 * k:128 * k + 128], ident[:, :])
                mm.then_inc(s_zT, 1)
                pe.wait_ge(s_zlo, n + 1)
                for m, (z, c, k) in enumerate([(z, c, k) for z, c in ((zT_hi, 0), (zT_hi, 1), (zT_lo, 0)) for k in range(KT)]):
                    mm = PE.matmul(p_o[:, :], z[:, k, :], (b_hi, b_lo)[c][:, k, :], start=(m == 0), stop=(m == 3 * KT - 1))
                mm.then_inc(s_o, 1)

        @block.scalar
        def _(act):
            A = nc.scalar
            act.wait_ge(s_in, 64)
            A.activation(r_hi[:, :, :], r_raw[:, :, :], ACT.Copy).then_inc(s_whi, 1)
            A.activation(a_hi[:, :, :], a_raw[:, :, :], ACT.Copy).then_inc(s_whi, 1)
            A.activation(b_hi[:, :, :], b_raw[:, :, :], ACT.Copy).then_inc(s_whi, 1)
            with act.Fori(0, B) as n:
                act.wait_ge(s_yT, n + 1)
                A.activation(yT_hi[:, :, :], p_y[:, :].rearrange("p (k n) -> p k n", k=KT), ACT.Copy).then_inc(s_yhi, 1)
                act.wait_ge(s_q, n + 1)
                A.activation(rq[:, :], p_q[:, 0:RD], ACT.Copy).then_inc(s_qs, 1)
                act.wait_ge(s_qT, n + 1)
                A.activation(rqT[:, :], p_qT[0:RD, 0:128], ACT.Copy).then_inc(s_qTs, 1)
                act.wait_ge(s_g, GS * n + 3)
                A.activation(e[:, :], sc[:, :], ACT.Exp, bias=nm[:, 0:1]).then_inc(s_e, 1)
                act.wait_ge(s_zT, n + 1)
                A.activation(zT_hi[:, :, :], p_zT[:, :].rearrange("p (k n) -> p k n", k=KT), ACT.Copy).then_inc(s_zhi, 1)

        @block.vector
        def _(dve):
            V = nc.vector
            V.tensor_copy(ybuf[:, :], yacc[:, 0, :]).then_inc(s_yb, 1)
            for n, (lo, raw, hi) in enumerate(((r_lo, r_raw, r_hi), (a_lo, a_raw, a_hi), (b_lo, b_raw, b_hi))):
                dve.wait_ge(s_whi, n + 1)
                V.tensor_tensor(lo[:, :, :], raw[:, :, :], hi[:, :, :].bitcast(F32), ALU.subtract).then_inc(s_wlo, 1)

            def batch(n, more):
                dve.wait_ge(s_yhi, n + 1)
                V.tensor_tensor(yT_lo[:, :, :], p_y[:, :].rearrange("p (k n) -> p k n", k=KT), yT_hi[:, :, :].bitcast(F32),
                                ALU.subtract).then_inc(s_ylo, 1)
                if more:
                    V.tensor_copy(ybuf[:, :], yacc[:, bass.ds(n + 1, 1), :].rearrange("p o n -> p (o n)")).then_inc(s_yb, 1)
                dve.wait_ge(s_s, n + 1)
                V.tensor_copy(sc[:, :], p_s[:, 0:NE]).then_inc(s_g, 1)
                wait_alone(dve, s_tick_dve, (s_g, GS * n + 1))
                V.max(v1[:, :], sc[:, :]).then_inc(s_g, 1)
                wait_alone(dve, s_tick_dve, (s_g, GS * n + 2))
                V.tensor_scalar(nm[:, :], v1[:, 0:1], -1.0, None, ALU.mult).then_inc(s_g, 1)
                V.match_replace(r1[:, :], v1[:, :], sc[:, :], -3e38).then_inc(s_g, 1)
                wait_alone(dve, s_tick_dve, (s_g, GS * n + 4))
                V.max(v2[:, :], r1[:, :]).then_inc(s_g, 1)
                wait_alone(dve, s_tick_dve, (s_g, GS * n + 5))
                V.match_replace(r2[:, :], v2[:, :], r1[:, :], -3e38).then_inc(s_g, 1)
                dve.wait_ge(s_g, GS * n + 6)
                V.tensor_tensor(sel[:, :], r2[:, :], sc[:, :], ALU.not_equal).then_inc(s_g, 1)
                wait_alone(dve, s_tick_dve, (s_g, GS * n + 7), (s_e, n + 1))
                V.tensor_tensor_reduce(out=es[:, :], in0=e[:, :], in1=sel[:, :], scale=1.0, scalar=0.0,
                                       op0=ALU.mult, op1=ALU.add, accum_out=tot[:, :]).then_inc(s_g, 1)
                wait_alone(dve, s_tick_dve, (s_g, GS * n + 8))
                V.reciprocal(rt[:, :], tot[:, :]).then_inc(s_g, 1)
                dve.wait_ge(s_g, GS * n + 9)
                V.tensor_scalar(gate[:, :], es[:, :], rt[:, 0:1], 2.0, ALU.mult, ALU.mult).then_inc(s_g, 1)
                dve.wait_ge(s_g, GS * n + 10)
                dve.wait_ge(s_z, n + 1)
                V.tensor_tensor(zg[:, :].rearrange("p (e r) -> p e r", e=NE), p_z[:, :].rearrange("p (e r) -> p e r", e=NE),
                                gate[:, :].unsqueeze(2).to_broadcast([128, NE, RANK]), ALU.mult).then_inc(s_zg, 1)
                dve.wait_ge(s_zhi, n + 1)
                V.tensor_tensor(zT_lo[:, :, :], p_zT[:, :].rearrange("p (k n) -> p k n", k=KT), zT_hi[:, :, :].bitcast(F32),
                                ALU.subtract).then_inc(s_zlo, 1)
                dve.wait_ge(s_o, n + 1)
                x = x1[:, bass.ds(n, 1), :].rearrange("p o n -> p (o n)")
                r = res[:, bass.ds(n, 1), :].rearrange("p o n -> p (o n)")
                V.tensor_tensor(r, p_o[:, :], x, ALU.add).then_inc(s_res, 1)
                V.engine_nop().then_inc(s_g, 1)

            dve.wait_ge(s_x1, 16)
            with dve.Fori(0, B - 1) as n:
                batch(n, True)
            batch(B - 1, False)


def program(nc, t, out):
    dram = {
        "x1": nc.dram_tensor("x1_dram", [B, S, D], F32, kind="Internal").ap(),
        "x1T": nc.dram_tensor("x1T_dram", [B, 128, 2 * KT * 128], F32, kind="Internal").ap(),
        "mask": nc.dram_tensor("mask_dram", [B, NKEY], BF16, kind="Internal").ap(),
        "rden": nc.dram_tensor("rden_dram", [S, REP], F32, kind="Internal").ap(),
    }
    with ExitStack() as ctx:
        keep = {
            "ident": ctx.enter_context(nc.sbuf_tensor("ident", [128, 128], F32)),
            "rope": ctx.enter_context(nc.sbuf_tensor("rope", [128, B, 2, 2, HD], F32)),
            "yacc": ctx.enter_context(nc.sbuf_tensor("yacc", [128, B, D], F32)),
        }
        layer0(nc, t, dram, keep)
        attention(nc, t, dram, keep)
        layer1_ffn(nc, t, dram, keep, out)


def kernel(**inputs):
    import numpy as np
    import concourse.bacc as bacc
    from concourse import mybir as _mybir
    from concourse.bass_utils import run_bass_kernel_spmd

    def a(name):
        return np.asarray(inputs[name])

    x = a("x")
    wq = a("L1_cond_Wq").reshape(HK, GQ, KT, 128).transpose(0, 3, 2, 1).reshape(HK, 128, WQ)
    wkv = np.stack([a("L1_cond_Wk").reshape(HK, HD, KT, 128), a("L1_cond_Wv").reshape(HK, HD, KT, 128)], 1)
    wkv = wkv.transpose(0, 4, 3, 1, 2).reshape(HK, 128, WKV)
    wo = a("L1_cond_Wo").reshape(D, HK, REP, HD).transpose(1, 3, 2, 0).reshape(HK, 128, WO)
    wg = np.concatenate([wq, wkv, wo], 2).reshape(HK, 128, B, CH).transpose(0, 2, 1, 3).reshape(UNITS, 128, CH)
    kv = np.stack([a("L1_cond_k_cache"), a("L1_cond_v_cache")], 3)
    kv = kv.transpose(2, 0, 1, 3, 4).reshape(HK, kv.shape[0], PAGE, 2 * HD)
    laid = {
        "x": x,
        "xT": x.transpose(0, 2, 1),
        "lora_id": a("itok_B_3_7"),
        "pages": a("itok_Bx16_0_63"),
        "seq": a("itok_B_207_1644"),
        "loraT": a("L0_cond_weight").transpose(0, 2, 1),
        "baseT": a("L0_ffn_base_w").T,
        "lgT": np.concatenate([a("L0_ffn_lora_A").reshape(E0 * R0, D), a("L0_ffn_gate_w")], 0).T,
        "loraBT": a("L0_ffn_lora_B").transpose(0, 2, 1).reshape(E0 * R0, D),
        "base_b": a("L0_ffn_base_b"),
        "qn": a("L1_cond_q_norm_w"),
        "kn": a("L1_cond_k_norm_w"),
        "wg": wg,
        "kv": kv,
        "AT": a("L1_ffn_A_w").T,
        "BT": a("L1_ffn_B_w").T,
        "routerT": a("L1_ffn_Wq_w").T,
        "keysT": a("L1_ffn_keys").T,
        "ident": np.eye(128, dtype=np.float32),
        "tok": np.arange(S, dtype=np.float32).reshape(S, 1),
        "keyno": np.arange(L, dtype=np.float32),
        "invf": np.float32(1.0) / (10000.0 ** (np.arange(0, HD, 2, dtype=np.float32) / np.float32(HD)).astype(np.float64)).astype(np.float32),
    }
    nc = bacc.Bacc("TRN2", target_bir_lowering=False, num_devices=1)
    arrays, t = {}, {}
    for name, v in laid.items():
        v = np.ascontiguousarray(v)
        arrays[f"in_{name}"] = v
        t[name] = nc.dram_tensor(f"in_{name}", v.shape, _mybir.dt.from_np(v.dtype), kind="ExternalInput").ap()
    out = nc.dram_tensor("out_x", (B, S, D), _mybir.dt.float32, kind="ExternalOutput").ap()
    program(nc, t, out)
    r = run_bass_kernel_spmd(nc, [arrays], core_ids=[0])
    return r.results[0]["out_x"]
```

```python
from contextlib import ExitStack

import concourse.bass as bass
from concourse import mybir

ALU = mybir.AluOpType
ACT = mybir.ActivationFunctionType
F32 = mybir.dt.float32
F32R = mybir.dt.float32r
BF16 = mybir.dt.bfloat16
I32 = mybir.dt.int32
U32 = mybir.dt.uint32

B, S, D = 8, 128, 512
KT = D // 128
HD, HQ, HK = 128, 32, 8
REP = HQ // HK
GQ = REP * HD
PAGE, NPP = 32, 16
L = PAGE * NPP
LT = L // 128
NKEY = L + S
KTILES = NKEY // 128
E0, R0 = 8, 16
NE, RANK, RD = 64, 8, 16
UNITS = HK * B
WQ, WKV, WO = KT * GQ, KT * 2 * HD, REP * D
WCOLS = WQ + WKV + WO
NPT = 4
CH = WCOLS // B
EPS = 1e-6
NEG = -1e30
TWO_PI_HI = 6.28125
TWO_PI_MID = 2029.0 / 2 ** 20
TWO_PI_LO = 6.283185307179586 - TWO_PI_HI - TWO_PI_MID
ROUND = 1.5 * 2 ** 23
PI_SAFE = 3.1415925


def wait_alone(eng, tick, *waits):
    for s, v in waits:
        eng.wait_ge(s, v)
        eng.sem_inc(tick, 1)


def layer0(nc, t, dram, keep):
    with ExitStack() as ctx:
        def sb(name, shape, dt=F32):
            return ctx.enter_context(nc.sbuf_tensor(name, shape, dt))

        def ps(name, shape, dt=F32):
            return ctx.enter_context(nc.psum_tensor(name, shape, dt))

        def sem(name):
            return ctx.enter_context(nc.semaphore(name))

        ident, rope, yacc = keep["ident"], keep["rope"], keep["yacc"]
        wg_hi, wg_lo, wg_raw = keep["wg_hi"], keep["wg_lo"], keep["wg_raw"]
        NLG = E0 * R0 + E0

        seq_i = sb("seq_i", [128, B], I32)
        seq_f = sb("seq_f", [128, B])
        pos = sb("pos", [128, B])
        tok = sb("tok", [128, 1])
        invf = sb("invf", [128, 64])
        normw = sb("normw", [128, 2, 128])
        keyno = sb("keyno", [1, L])
        mask = sb("mask_rows", [1, B, NKEY], BF16)
        ids = sb("ids", [1, B], I32)
        scratch = yacc[:, :, :].rearrange("p b d -> p (b d)")
        NA = B * 64
        ang = scratch[:, 0:NA].rearrange("p (b n) -> p b n", b=B)
        turn = [scratch[:, (1 + c) * NA:(2 + c) * NA].rearrange("p (b n) -> p b n", b=B) for c in range(2)]
        red = [scratch[:, (3 + c) * NA:(4 + c) * NA].rearrange("p (b n) -> p b n", b=B) for c in range(2)]
        trig = [scratch[:, (5 + c) * NA:(6 + c) * NA].rearrange("p (b n) -> p b n", b=B) for c in range(2)]
        w_raw = sb("w_raw", [128, 2, KT, D])
        w_hi = sb("w_hi", [128, KT, D], F32R)
        w_lo = sb("w_lo", [128, KT, D], F32R)
        base_hi, base_lo = [w[:, WCOLS:WCOLS + KT * D].rearrange("p (k n) -> p k n", k=KT) for w in (wg_hi, wg_lo)]
        base_raw = w_raw[:, 1]
        lg_raw = sb("lg_raw", [128, KT, NLG])
        lg_hi = sb("lg_hi", [128, KT, NLG], F32R)
        lg_lo = sb("lg_lo", [128, KT, NLG], F32R)
        lb_raw = sb("lb_raw", [128, D])
        lb_hi = sb("lb_hi", [128, D], F32R)
        lb_lo = sb("lb_lo", [128, D], F32R)
        bias = sb("bias", [128, D])
        xT_raw = sb("xT_raw", [128, 2, KT, 128])
        x_raw = sb("x_raw", [128, 2, D])
        xT_hi = sb("xT_hi", [128, KT, 128], F32R)
        xT_lo = sb("xT_lo", [128, KT, 128], F32R)
        yT_hi = sb("yT_hi", [128, KT, 128], F32R)
        yT_lo = sb("yT_lo", [128, KT, 128], F32R)
        xb = sb("xb", [128, D])
        lgs = sb("lgs", [128, E0])
        v8 = sb("v8", [128, 8])
        i8 = sb("i8", [128, 8], U32)
        i8f = sb("i8f", [128, 8])
        iota8 = sb("iota8", [128, E0])
        diff = sb("diff", [128, 1])
        ex = sb("ex_l0", [128, 1])
        den = sb("den_l0", [128, 1])
        pr = sb("pr", [128, 2])
        wa = sb("wa", [128, E0])
        wb = sb("wb", [128, E0])
        wf = sb("wf", [128, E0])
        low = sb("low", [128, E0 * R0])
        lowT_hi = sb("lowT_hi", [128, 128], F32R)
        lowT_lo = sb("lowT_lo", [128, 128], F32R)
        x1 = sb("x1_l0", [128, D])
        x1T = sb("x1T_l0", [128, 2, KT, 128], F32R)

        p_y = ps("p_y", [128, KT, 128])
        p_r = [ps("p_r0", [128, D]), ps("p_r1", [128, D])]
        p_lg = ps("p_lg", [128, 512])
        p_t = ps("p_t", [128, 512])
        p_x = ps("p_x", [128, KT, 128])

        s_tick_sp, s_tick_dve = sem("l0_tick_sp"), sem("l0_tick_dve")
        s_tick_pool = sem("l0_tick_pool")
        s_const = sem("l0_const")
        s_ids = sem("l0_ids")
        s_base = sem("l0_base")
        s_low_w = sem("l0_low_w")
        s_w = [sem("l0_w0"), sem("l0_w1")]
        s_wraw, s_wh, s_ws = keep["s_wraw"], keep["s_wh"], keep["s_ws"]
        s_tab = sem("l0_tab")
        s_red = sem("l0_red")
        s_trig = sem("l0_trig")
        s_tables = sem("l0_tables")
        s_whi, s_wlo = sem("l0_whi"), sem("l0_wlo")
        s_bhi, s_blo = sem("l0_bhi"), sem("l0_blo")
        s_bpl = sem("l0_bpl")
        s_xb = sem("l0_xb")
        s_y = sem("l0_y")
        s_yhi, s_ylo = sem("l0_yhi"), sem("l0_ylo")
        s_lg = sem("l0_lg")
        s_base_mm = sem("l0_base_mm")
        s_gate = sem("l0_gate")
        s_exp = sem("l0_exp")
        s_low = sem("l0_low")
        s_lt = sem("l0_lt")
        s_lthi, s_ltlo = sem("l0_lthi"), sem("l0_ltlo")
        s_r = sem("l0_r")
        s_x1 = sem("l0_x1")
        s_xt = sem("l0_xt")
        s_xthi, s_xtlo = sem("l0_xthi"), sem("l0_xtlo")
        s_mask = sem("l0_mask")
        s_mst = sem("l0_mst")
        s_st = sem("l0_st")
        s_stT = sem("l0_stT")

        block = ctx.enter_context(nc.Block())
        HK2 = KT // 2

        @block.sync
        def _(sp):
            def rows(a, n):
                return a.rearrange("(o n) -> o n", o=1).to_broadcast([128, n])

            def load(b, slot):
                a = sp.value_load(ids[0:1, bass.ds(b, 1)], min_val=0, max_val=7)
                sp.dma_start(w_raw[:, slot, :, :],
                             t["loraT"][bass.ds(a, 1)].rearrange("o (k p) n -> p (o k) n", p=128)).then_inc(s_w[slot], 16)
                sp.dma_start(xT_raw[:, slot, :, :],
                             t["xT"][bass.ds(b, 1)].rearrange("o (k p) n -> p (o k) n", p=128)).then_inc(s_w[slot], 16)
                sp.dma_start(x_raw[:, slot, :], t["x"][bass.ds(b, 1)].rearrange("o p n -> (o p) n")).then_inc(s_w[slot], 16)

            def load_wg(c, par):
                sp.dma_start(wg_raw[:, par], t["wg"][bass.ds(c, 1)].rearrange("o p n -> (o p) n")).then_inc(s_wraw[par], 16)

            sp.dma_start(ids[:, :], t["lora_id"].rearrange("(o b) -> o b", o=1)).then_inc(s_ids, 16)
            sp.dma_start(seq_i[:, :], rows(t["seq"], B)).then_inc(s_const, 16)
            sp.dma_start(tok[:, :], t["tok"]).then_inc(s_const, 16)
            sp.dma_start(invf[:, :], rows(t["invf"], 64)).then_inc(s_const, 16)
            sp.wait_ge(s_ids, 16)
            load(0, 0)
            sp.dma_start(normw[:, 0, :], rows(t["qn"], 128)).then_inc(s_const, 16)
            sp.dma_start(normw[:, 1, :], rows(t["kn"], 128)).then_inc(s_const, 16)
            sp.dma_start(keyno[:, :], t["keyno"].rearrange("(o n) -> o n", o=1)).then_inc(s_const, 16)
            sp.dma_start(iota8[:, :], rows(t["keyno"][0:E0], E0)).then_inc(s_const, 16)
            sp.dma_start(ident[:, :], t["ident"]).then_inc(s_const, 16)
            sp.dma_start(lg_raw[:, :, :], t["lgT"].rearrange("(k p) n -> p k n", p=128)).then_inc(s_low_w, 16)
            sp.dma_start(lb_raw[:, :], t["loraBT"]).then_inc(s_low_w, 16)
            sp.dma_start(bias[:, :], rows(t["base_b"], D)).then_inc(s_low_w, 16)
            sp.dma_start(base_raw, t["baseT"].rearrange("(k p) n -> p k n", p=128)).then_inc(s_base, 16)
            load_wg(0, 0)
            load_wg(1, 1)
            sp.wait_ge(s_wlo, 3)
            load(1, 1)
            sp.wait_ge(s_mask, 1 + B)
            sp.dma_start(dram["mask"].rearrange("(o b) n -> o (b n)", o=1), mask[:, :, :].rearrange("p b n -> p (b n)")).then_inc(s_mst, 16)
            sp.wait_ge(s_mst, 16)
            with sp.Fori(1, B // 2) as i:
                for slot in range(2):
                    wait_alone(sp, s_tick_sp, (s_blo, 4 * i + 2 * slot - 2), (s_bpl, 2 * i + slot - 1), (s_xb, 2 * i + slot - 1))
                    load(2 * i + slot, slot)
                    wait_alone(sp, s_tick_sp, (s_ws, 2 * i + slot - 1))
                    load_wg(2 * i + slot, slot)

        def schedule(eng, step):
            step(0, 0, "first")
            with eng.Fori(0, (B - 2) // 2) as i:
                step(2 * i + 1, 1, "body")
                step(2 * i + 2, 0, "body")
            step(B - 1, 1, "last")

        @block.gpsimd
        def _(pool):
            G = nc.gpsimd
            G.memset(mask[:, :, L:NKEY], 0.0).then_inc(s_mask, 1)
            pool.wait_ge(s_low_w, 48)

            def step(n, slot, where):
                pool.wait_ge(s_bhi, 3 * n + 2)
                G.tensor_tensor(w_lo[:, HK2:KT, :], w_raw[:, slot, HK2:KT], w_hi[:, HK2:KT, :].bitcast(F32), ALU.subtract).then_inc(s_bpl, 1)
                if where != "first":
                    pool.wait_ge(s_x1, n)
                G.tensor_tensor(xb[:, :], x_raw[:, slot, :], bias[:, :], ALU.add).then_inc(s_xb, 1)
                wait_alone(pool, s_tick_pool, (s_wraw[slot], (n // 2) * 16 + 16))
                G.tensor_copy(wg_hi[:, bass.ds(n * CH, CH)], wg_raw[:, slot]).then_inc(s_wh, 1)
                wait_alone(pool, s_tick_pool, (s_wh, n + 1))
                G.tensor_tensor(wg_lo[:, bass.ds(n * CH, CH)], wg_raw[:, slot], wg_hi[:, bass.ds(n * CH, CH)].bitcast(F32),
                                ALU.subtract).then_inc(s_ws, 1)
            schedule(pool, step)

        @block.vector
        def _(dve):
            V = nc.vector
            linked = [0]

            def link(ins):
                linked[0] += 1
                ins.then_inc(s_tab, 1)
                dve.wait_ge(s_tab, linked[0])

            dve.wait_ge(s_const, 8 * 16)
            link(V.tensor_copy(seq_f[:, :], seq_i[:, :]))
            link(V.tensor_scalar(pos[:, :], seq_f[:, :], tok[:, 0:1], None, ALU.add))
            link(V.tensor_tensor(ang, pos[:, :].unsqueeze(2).to_broadcast([128, B, 64]),
                                 invf[:, :].unsqueeze(1).to_broadcast([128, B, 64]), ALU.mult))
            for c in range(2):
                link(V.tensor_scalar(turn[c], ang, 1 / 6.283185307179586, 0.25 * c, ALU.mult, ALU.add))
                link(V.tensor_scalar(turn[c], turn[c], ROUND, None, ALU.add))
                link(V.tensor_scalar(turn[c], turn[c], ROUND, None, ALU.subtract))
                link(V.scalar_tensor_tensor(out=red[c], in0=turn[c], scalar=-TWO_PI_HI, in1=ang, op0=ALU.mult, op1=ALU.add))
                link(V.scalar_tensor_tensor(out=red[c], in0=turn[c], scalar=-TWO_PI_MID, in1=red[c], op0=ALU.mult, op1=ALU.add))
                link(V.scalar_tensor_tensor(out=red[c], in0=turn[c], scalar=-TWO_PI_LO, in1=red[c], op0=ALU.mult, op1=ALU.add))
                if c:
                    link(V.tensor_scalar(red[c], red[c], 1.5707963267948966, None, ALU.add))
                link(V.tensor_scalar(red[c], red[c], PI_SAFE, -PI_SAFE, ALU.min, ALU.max))
            V.engine_nop().then_inc(s_red, 1)

            def split_adapter(n, slot):
                dve.wait_ge(s_bhi, 3 * n + 1)
                V.tensor_tensor(w_lo[:, 0:HK2, :], w_raw[:, slot, 0:HK2], w_hi[:, 0:HK2, :].bitcast(F32), ALU.subtract).then_inc(s_blo, 1)
                dve.wait_ge(s_bhi, 3 * n + 3)
                V.tensor_tensor(xT_lo[:, :, :], xT_raw[:, slot], xT_hi[:, :, :].bitcast(F32), ALU.subtract).then_inc(s_blo, 1)

            split_adapter(0, 0)
            dve.wait_ge(s_whi, 3)
            V.tensor_tensor(lg_lo[:, :, :], lg_raw[:, :, :], lg_hi[:, :, :].bitcast(F32), ALU.subtract).then_inc(s_wlo, 1)
            V.tensor_tensor(base_lo[:, :, :], base_raw, base_hi[:, :, :].bitcast(F32), ALU.subtract).then_inc(s_wlo, 1)
            V.tensor_tensor(lb_lo[:, :], lb_raw[:, :], lb_hi[:, :].bitcast(F32), ALU.subtract).then_inc(s_wlo, 1)

            def tables():
                for b in range(B):
                    V.tensor_scalar(mask[:, b, 0:L], keyno[:, :], seq_f[0:1, b:b + 1], NEG, ALU.is_ge, ALU.mult).then_inc(s_mask, 1)
                dve.wait_ge(s_trig, 2)
                for n in range(2):
                    for half in range(2):
                        own = normw[:, n, 64 * half:64 * half + 64].unsqueeze(1).to_broadcast([128, B, 64])
                        other = normw[:, n, 64 - 64 * half:128 - 64 * half].unsqueeze(1).to_broadcast([128, B, 64])
                        V.tensor_tensor(rope[:, :, n, 0, 64 * half:64 * half + 64], trig[1], own, ALU.mult).then_inc(s_tables, 1)
                        V.scalar_tensor_tensor(out=rope[:, :, n, 1, 64 * half:64 * half + 64], in0=trig[0],
                                               scalar=(1.0 if half else -1.0), in1=other, op0=ALU.mult, op1=ALU.mult).then_inc(s_tables, 1)

            def gates(n):
                dve.wait_ge(s_lg, n + 1)
                V.tensor_copy(lgs[:, :], p_lg[:, E0 * R0:NLG]).then_inc(s_gate, 1)
                wait_alone(dve, s_tick_dve, (s_gate, 11 * n + 1))
                V.max(v8[:, :], lgs[:, :]).then_inc(s_gate, 1)
                dve.wait_ge(s_gate, 11 * n + 2)
                V.tensor_tensor(diff[:, :], v8[:, 1:2], v8[:, 0:1], ALU.subtract).then_inc(s_gate, 1)
                V.max_index(i8[:, :], v8[:, :], lgs[:, :]).then_inc(s_gate, 1)
                dve.wait_ge(s_gate, 11 * n + 4)
                V.tensor_copy(i8f[:, :], i8[:, :]).then_inc(s_gate, 1)
                dve.wait_ge(s_exp, n + 1)
                V.tensor_scalar(den[:, :], ex[:, :], 1.0, None, ALU.add).then_inc(s_gate, 1)
                dve.wait_ge(s_gate, 11 * n + 6)
                V.reciprocal(pr[:, 0:1], den[:, :]).then_inc(s_gate, 1)
                dve.wait_ge(s_gate, 11 * n + 7)
                V.tensor_tensor(pr[:, 1:2], pr[:, 0:1], ex[:, :], ALU.mult).then_inc(s_gate, 1)
                dve.wait_ge(s_gate, 11 * n + 8)
                V.tensor_scalar(wa[:, :], iota8[:, :], i8f[:, 0:1], pr[:, 0:1], ALU.is_equal, ALU.mult).then_inc(s_gate, 1)
                V.tensor_scalar(wb[:, :], iota8[:, :], i8f[:, 1:2], pr[:, 1:2], ALU.is_equal, ALU.mult).then_inc(s_gate, 1)
                dve.wait_ge(s_gate, 11 * n + 10)
                V.tensor_tensor(wf[:, :], wa[:, :], wb[:, :], ALU.add).then_inc(s_gate, 1)
                dve.wait_ge(s_gate, 11 * n + 11)
                V.scalar_tensor_tensor(out=low[:, :].rearrange("p (e r) -> p e r", e=E0),
                                       in0=p_lg[:, 0:E0 * R0].rearrange("p (e r) -> p e r", e=E0), scalar=2.0,
                                       in1=wf[:, :].unsqueeze(2).to_broadcast([128, E0, R0]),
                                       op0=ALU.mult, op1=ALU.mult).then_inc(s_low, 1)

            def finish(n, slot):
                dve.wait_ge(s_r, n + 1)
                dve.wait_ge(s_xb, n + 1)
                if not isinstance(n, int) or n > 0:
                    dve.wait_ge(s_st, 16 * n)
                V.tensor_tensor(x1[:, :], p_r[slot][:, :], xb[:, :], ALU.add).then_inc(s_x1, 1)

            def low_parts(n):
                dve.wait_ge(s_lthi, n + 1)
                V.tensor_tensor(lowT_lo[:, :], p_t[:, 0:128], lowT_hi[:, :].bitcast(F32), ALU.subtract).then_inc(s_ltlo, 1)

            def x1T_parts(n):
                dve.wait_ge(s_xthi, n + 1)
                V.tensor_tensor(x1T[:, 1], p_x[:, :, :], x1T[:, 0].bitcast(F32), ALU.subtract).then_inc(s_xtlo, 1)

            def step(n, slot, where):
                if where != "first":
                    low_parts(n - 1)
                dve.wait_ge(s_yhi, n + 1)
                V.tensor_tensor(yT_lo[:, :, :], p_y[:, :, :], yT_hi[:, :, :].bitcast(F32), ALU.subtract).then_inc(s_ylo, 1)
                if where == "first":
                    tables()
                if where != "first":
                    finish(n - 1, 1 - slot)
                gates(n)
                if where != "last":
                    split_adapter(n + 1, 1 - slot)
                if where != "first":
                    x1T_parts(n - 1)

            schedule(dve, step)
            low_parts(B - 1)
            finish(B - 1, 1)
            x1T_parts(B - 1)

        @block.scalar
        def _(act):
            A = nc.scalar

            def split_adapter(n, slot):
                act.wait_ge(s_w[slot], (n // 2) * 48 + 48)
                if not isinstance(n, int) or n > 0:
                    act.wait_ge(s_y, n)
                A.activation(w_hi[:, 0:HK2, :], w_raw[:, slot, 0:HK2], ACT.Copy).then_inc(s_bhi, 1)
                A.activation(w_hi[:, HK2:KT, :], w_raw[:, slot, HK2:KT], ACT.Copy).then_inc(s_bhi, 1)
                A.activation(xT_hi[:, :, :], xT_raw[:, slot], ACT.Copy).then_inc(s_bhi, 1)

            def low_parts(n):
                act.wait_ge(s_lt, n + 1)
                A.activation(lowT_hi[:, :], p_t[:, 0:128], ACT.Copy).then_inc(s_lthi, 1)

            def finish(n):
                act.wait_ge(s_x1, n + 1)
                act.dma_start(dram["x1"][bass.ds(n, 1)].rearrange("o p n -> (o p) n"), x1[:, :]).then_inc(s_st, 16)
                act.wait_ge(s_xt, n + 1)
                if not isinstance(n, int) or n > 0:
                    act.wait_ge(s_stT, 16 * n)
                A.activation(x1T[:, 0], p_x[:, :, :], ACT.Copy).then_inc(s_xthi, 1)
                act.wait_ge(s_xtlo, n + 1)
                act.dma_start(dram["x1T"][bass.ds(n, 1)].rearrange("o p n -> (o p) n"),
                              x1T[:, :, :, :].bitcast(F32).rearrange("p a k n -> p (a k n)")).then_inc(s_stT, 16)

            split_adapter(0, 0)
            act.wait_ge(s_red, 1)
            A.activation(trig[0], red[0], ACT.Sin).then_inc(s_trig, 1)
            A.activation(trig[1], red[1], ACT.Sin).then_inc(s_trig, 1)
            act.wait_ge(s_low_w, 48)
            A.activation(lg_hi[:, :, :], lg_raw[:, :, :], ACT.Copy).then_inc(s_whi, 1)
            A.activation(lb_hi[:, :], lb_raw[:, :], ACT.Copy).then_inc(s_whi, 1)
            act.wait_ge(s_base, 16)
            A.activation(base_hi[:, :, :], base_raw, ACT.Copy).then_inc(s_whi, 1)

            def step(n, slot, where):
                if where != "first":
                    low_parts(n - 1)
                act.wait_ge(s_y, n + 1)
                A.activation(yT_hi[:, :, :], p_y[:, :, :], ACT.Copy).then_inc(s_yhi, 1)
                if where != "last":
                    split_adapter(n + 1, 1 - slot)
                act.wait_ge(s_gate, 11 * n + 3)
                A.activation(ex[:, :], diff[:, :], ACT.Exp).then_inc(s_exp, 1)
                if where != "first":
                    finish(n - 1)

            schedule(act, step)
            low_parts(B - 1)
            finish(B - 1)
            act.wait_ge(s_st, 16 * B)
            act.wait_ge(s_stT, 16 * B)

        @block.tensor
        def _(pe):
            PE = nc.tensor

            def product(out, pairs, width, start=True, stop=True):
                terms = [(a[i], w[j]) for i, j in ((0, 0), (0, 1), (1, 0)) for a, w in pairs]
                for m, (a, w) in enumerate(terms):
                    mm = PE.matmul(out, a, w, start=start and m == 0, stop=stop and m == len(terms) - 1)
                return mm

            def low_turn(n):
                pe.wait_ge(s_low, n + 1)
                PE.transpose(p_t[:, 0:128], low[:, :], ident[:, :]).then_inc(s_lt, 1)

            def low_out(n, slot):
                pe.wait_ge(s_ltlo, n + 1)
                product(p_r[slot][:, :], [((lowT_hi[:, :], lowT_lo[:, :]), (lb_hi[:, :], lb_lo[:, :]))], D, start=False).then_inc(s_r, 1)

            def x1_turn(n):
                pe.wait_ge(s_x1, n + 1)
                for k in range(KT):
                    mm = PE.transpose(p_x[:, k, :], x1[:, 128 * k:128 * k + 128], ident[:, :])
                mm.then_inc(s_xt, 1)

            def step(n, slot, where):
                if where != "first":
                    low_turn(n - 1)
                pe.wait_ge(s_blo, 2 * n + 2)
                pe.wait_ge(s_bpl, n + 1)
                for o in range(KT):
                    mm = product(p_y[:, o, :], [((w_hi[:, k, 128 * o:128 * o + 128], w_lo[:, k, 128 * o:128 * o + 128]),
                                                 (xT_hi[:, k, :], xT_lo[:, k, :])) for k in range(KT)], 128)
                mm.then_inc(s_y, 1)
                if where != "first":
                    low_out(n - 1, 1 - slot)
                else:
                    pe.wait_ge(s_wlo, 3)
                pe.wait_ge(s_ylo, n + 1)
                product(p_lg[:, 0:NLG], [((yT_hi[:, k, :], yT_lo[:, k, :]), (lg_hi[:, k, :], lg_lo[:, k, :])) for k in range(KT)],
                        NLG).then_inc(s_lg, 1)
                product(p_r[slot][:, :], [((yT_hi[:, k, :], yT_lo[:, k, :]), (base_hi[:, k, :], base_lo[:, k, :])) for k in range(KT)],
                        D, stop=False).then_inc(s_base_mm, 1)
                if where != "first":
                    x1_turn(n - 1)

            pe.wait_ge(s_const, 128)
            schedule(pe, step)
            low_turn(B - 1)
            low_out(B - 1, 1)
            x1_turn(B - 1)


def attention(nc, t, dram, keep):
    with ExitStack() as ctx:
        def sb(name, shape, dt=F32):
            return ctx.enter_context(nc.sbuf_tensor(name, shape, dt))

        def ps(name, shape, dt=F32):
            return ctx.enter_context(nc.psum_tensor(name, shape, dt))

        def sem(name):
            return ctx.enter_context(nc.semaphore(name))

        ident, rope, yacc = keep["ident"], keep["rope"], keep["yacc"]
        mask = sb("mask", [128, 2, NKEY], BF16)
        pages = sb("pages", [1, B * NPP], I32)
        w_raw, w_hi, w_lo = keep["wg_raw"], keep["wg_hi"], keep["wg_lo"]
        xT = sb("xT", [128, 2, 2, KT, 128], F32R)
        kv = sb("kv", [128, 2, LT, 2, HD])
        kT_hi = sb("kT_hi", [128, NKEY], F32R)
        kT_lo = sb("kT_lo", [128, NKEY], F32R)
        v_hi = sb("v_hi", [128, 2, KTILES, HD], F32R)
        v_lo = sb("v_lo", [128, 2, KTILES, HD], F32R)
        qT_hi = sb("qT_hi", [128, GQ], F32R)
        qT_lo = sb("qT_lo", [128, GQ], F32R)
        rot_a = sb("rot_a", [128, REP, HD])
        rot_b = sb("rot_b", [128, REP, HD])
        krot_a = sb("krot_a", [128, HD])
        krot_b = sb("krot_b", [128, HD])
        junk = sb("junk", [128, REP + 1, HD])
        ss = sb("ss", [128, REP + 1])
        rs_a = sb("rs_a", [128, REP + 1])
        rs_b = sb("rs_b", [128, REP + 1])
        rstd = sb("rstd", [128, 2, REP + 1])
        c_mul = sb("c_mul", [128, REP + 1])
        c_add = sb("c_add", [128, REP + 1])
        c_pow = sb("c_pow", [128, REP + 1])
        P = sb("P", [128, REP, NKEY])
        mx = sb("mx", [128, REP])
        nb = sb("nb", [128, REP])
        den = sb("den", [128, REP])
        rden = sb("rden", [128, 2, REP])
        bc = sb("bc", [128, S, REP])
        pT_hi = sb("pT_hi", [128, NPT, REP * S], F32R)
        pT_lo = sb("pT_lo", [128, NPT, REP * S], F32R)
        oT = sb("oT", [128, REP * S])
        oT_hi = sb("oT_hi", [128, REP * S], F32R)
        oT_lo = sb("oT_lo", [128, REP * S], F32R)

        bank = [ps(f"bank{n}", [128, 1024]) for n in range(2)]
        b_kv = ps("b_kv", [128, 512])
        b_q = ps("b_q", [128, 512])
        b_y = ps("b_y", [128, 512])
        b_o = ps("b_o", [128, 512])

        s_tick_sp, s_tick_dve, s_tick_pool = sem("s_tick_sp"), sem("s_tick_dve"), sem("s_tick_pool")
        s_pg = sem("s_pg")
        s_c = sem("s_c")
        s_wraw, s_wh, s_ws = keep["s_wraw"], keep["s_wh"], keep["s_ws"]
        s_xT = [sem("s_xT0"), sem("s_xT1")]
        s_kv = [sem("s_kv0"), sem("s_kv1")]
        s_mk = [sem("s_mk0"), sem("s_mk1")]
        s_rw = sem("s_rw")
        s_bc = sem("s_bc")
        s_kvp = sem("s_kvp")
        s_qp = sem("s_qp")
        s_sc = sem("s_sc")
        s_y = sem("s_y")
        s_pt = sem("s_pt")
        s_pv = sem("s_pv")
        s_kcT = sem("s_kcT")
        s_qkT = sem("s_qkT")
        s_sq = sem("s_sq")
        s_vh = sem("s_vh")
        s_ex = sem("s_ex")
        s_pth = sem("s_pth")
        s_kch = sem("s_kch")
        s_qkh = sem("s_qkh")
        s_oh = sem("s_oh")
        s_mx = sem("s_mx")
        s_nb = sem("s_nb")
        s_rq = sem("s_rq")
        s_rk = sem("s_rk")
        s_kr = sem("s_kr")
        s_rd = sem("s_rd")
        s_ya = sem("s_ya")
        s_ptl = sem("s_ptl")
        s_qkl = sem("s_qkl")
        s_ot = sem("s_ot")
        s_rs = sem("s_rs")
        s_qa = sem("s_qa")
        s_vc = sem("s_vc")
        s_vs = sem("s_vs")
        s_ol = sem("s_ol")

        block = ctx.enter_context(nc.Block())
        LAST = UNITS - 1

        @block.sync
        def _(sp):
            sp.dma_start(pages[:, :], t["pages"].rearrange("(o b) p -> o (b p)", o=1)).then_inc(s_pg, 16)
            sp.wait_ge(s_pg, 16)

            def load_x(u, par):
                sp.dma_start(xT[:, par].bitcast(F32).rearrange("p a k n -> p (a k n)"),
                             dram["x1T"][bass.ds(u % B, 1)].rearrange("o p n -> (o p) n")).then_inc(s_xT[par], 16)

            def load_mask(u, par):
                sp.dma_start(mask[:, par], dram["mask"][bass.ds(u % B, 1)].to_broadcast([128, NKEY])).then_inc(s_mk[par], 16)

            def load_w(n, par):
                sp.dma_start(w_raw[:, par], t["wg"][bass.ds(n % UNITS, 1)].rearrange("o p n -> (o p) n")).then_inc(s_wraw[par], 16)

            def page_numbers(u):
                return nc.values_load_multi_w_load_instructions(
                    pages[0:1, bass.ds((u % B) * NPP, NPP)], engines=(mybir.EngineType.SP,), min_val=0, max_val=63)[1]

            def load_kv(u, par, numbers, j0, j1):
                for j in range(j0, j1):
                    page = numbers[j]
                    at = PAGE * (j % 4)
                    src = t["kv"][bass.ds(u // B, 1), bass.ds(page, 1)]
                    sp.dma_start(kv[at:at + PAGE, par, j // 4].rearrange("p a d -> p (a d)"),
                                 src.rearrange("g o k n -> (g o k) n")).then_inc(s_kv[par], 16)

            def rden_out(u, par):
                wait_alone(sp, s_tick_sp, (s_rd, u + 1))
                sp.dma_start(dram["rden"], rden[:, par]).then_inc(s_rw, 16)

            def rden_in(u, skip=False):
                wait_alone(sp, s_tick_sp, (s_rw, 16 * (u + 1)), *([(s_ot, u)] if not skip else []))
                sp.dma_start(bc[:, :, :].rearrange("p s h -> p (s h)"),
                             dram["rden"].rearrange("(o s) h -> o (s h)", o=1).to_broadcast([128, S * REP])).then_inc(s_bc, 16)

            load_mask(0, 0)
            load_mask(1, 1)
            load_x(0, 0)
            load_kv(0, 0, page_numbers(0), 0, NPP)
            load_x(1, 1)
            load_kv(1, 1, page_numbers(1), 0, NPP)
            load_w(B, 0)
            load_w(B + 1, 1)

            def unit(u, par, n, more=True, weights=True):
                if more:
                    wait_alone(sp, s_tick_sp, (s_qp, u + 1))
                    load_x(u + 2, par)
                    wait_alone(sp, s_tick_sp, (s_kcT, u + 1), (s_vs, u + 1))
                    numbers = page_numbers(u + 2)
                    load_kv(u + 2, par, numbers, 0, NPP // 2)
                rden_out(u, par)
                if more:
                    load_mask(u + 2, par)
                    load_kv(u + 2, par, numbers, NPP // 2, 3 * NPP // 4)
                rden_in(u, n == "first")
                if more:
                    load_kv(u + 2, par, numbers, 3 * NPP // 4, NPP)
                if weights:
                    wait_alone(sp, s_tick_sp, (s_ws, u + B + 1))
                    load_w(u + B + 2, par)

            unit(0, 0, "first")
            with sp.Fori(0, (UNITS - 4) // 2) as i:
                unit(2 * i + 1, 1, "body")
                unit(2 * i + 2, 0, "body")
            unit(LAST - 2, 1, "body", weights=False)
            unit(LAST - 1, 0, "body", more=False, weights=False)
            unit(LAST, 1, "last", more=False, weights=False)

        @block.tensor
        def _(pe):
            PE = nc.tensor

            def wait_group(u, chunks):
                pe.wait_ge(s_ws, (u // B) * B + chunks)

            def project(u, par):
                at = ((u // B) % 2) * WCOLS
                pe.wait_ge(s_xT[par], (u // 2) * 16 + 16)
                wait_group(u, 5)
                terms = [(a, w, k) for a, w in ((0, w_hi), (0, w_lo), (1, w_hi)) for k in range(KT)]
                for m, (a, w, k) in enumerate(terms):
                    mm = PE.matmul(b_kv[:, 0:2 * HD], xT[:, par, a, k], w[:, bass.ds(at + WQ + 2 * HD * k, 2 * HD)],
                                   start=(m == 0), stop=(m == len(terms) - 1))
                mm.then_inc(s_kvp, 1)
                for m, (a, w, k) in enumerate(terms):
                    mm = PE.matmul(b_q[:, :], xT[:, par, a, k], w[:, bass.ds(at + GQ * k, GQ)],
                                   start=(m == 0), stop=(m == len(terms) - 1))
                mm.then_inc(s_qp, 1)

            def turn(u, par):
                pe.wait_ge(s_kv[par], (u // 2) * 16 * NPP + 16 * NPP)
                if not isinstance(u, int) or u > 0:
                    pe.wait_ge(s_ya, u)
                for k in range(LT):
                    mm = PE.transpose(b_y[:, 128 * k:128 * k + 128], kv[:, par, k, 0], ident[:, :])
                mm.then_inc(s_kcT, 1)
                pe.wait_ge(s_kr, 2 * u + 2)
                PE.transpose(b_kv[:, 0:128], krot_a[:, :], ident[:, :])
                pe.wait_ge(s_qa, u + 1)
                for h in range(REP):
                    mm = PE.transpose(b_q[:, 128 * h:128 * h + 128], rot_a[:, h], ident[:, :])
                mm.then_inc(s_qkT, 1)

            def scores(u, par):
                pe.wait_ge(s_qkl, 3 * u + 3)
                for h in range(REP):
                    if h >= 2:
                        pe.wait_ge(s_mx, 4 * u + h - 1)
                    out = bank[h % 2]
                    q = slice(128 * h, 128 * h + 128)
                    terms = ((qT_hi, kT_hi), (qT_hi, kT_lo), (qT_lo, kT_hi))
                    for m, (a, k) in enumerate(terms):
                        PE.matmul(out[:, 0:L], a[:, q], k[:, 0:L], start=(m == 0), stop=(m == 2))
                        mm = PE.matmul(out[:, L:NKEY], a[:, q], k[:, L:NKEY], start=(m == 0), stop=(m == 2))
                    mm.then_inc(s_sc, 1)

            def output(u):
                at = ((u // B) % 2) * WCOLS + WQ + WKV
                pe.wait_ge(s_ol, u + 1)
                wait_group(u, B)
                terms = [(o, w, h) for o, w in ((oT_hi, w_hi), (oT_hi, w_lo), (oT_lo, w_hi)) for h in range(REP)]
                for m, (o, w, h) in enumerate(terms):
                    mm = PE.matmul(b_y[:, :], o[:, 128 * h:128 * h + 128], w[:, bass.ds(at + D * h, D)],
                                   start=(m == 0), stop=(m == len(terms) - 1))
                mm.then_inc(s_y, 1)

            def p_turn(u, k):
                for h in range(REP):
                    mm = PE.transpose(bank[(k % 4) // 2][:, 512 * (k % 2) + 128 * h:512 * (k % 2) + 128 * h + 128],
                                      P[:, h, 128 * k:128 * k + 128], ident[:, :])
                mm.then_inc(s_pt, 1)

            def pv(u, par, k):
                pe.wait_ge(s_ptl, 5 * u + k + 1)
                for m, (v, p) in enumerate(((v_hi, pT_hi), (v_lo, pT_hi), (v_hi, pT_lo))):
                    mm = PE.matmul(b_o[:, :], v[:, par, k], p[:, k % NPT], start=(k == 0 and m == 0),
                                   stop=(k == KTILES - 1 and m == 2))
                mm.then_inc(s_pv, 1)

            def unit(u, par, n):
                scores(u, par)
                if n != "last":
                    project(u + 1, 1 - par)
                if n != "first":
                    output(u - 1)
                pe.wait_ge(s_ex, 4 * u + 4)
                for k in range(4):
                    p_turn(u, k)
                pe.wait_ge(s_vs, u + 1)
                pv(u, par, 0)
                p_turn(u, 4)
                if n != "last":
                    turn(u + 1, 1 - par)
                for k in range(1, KTILES):
                    pv(u, par, k)

            project(0, 0)
            turn(0, 0)
            unit(0, 0, "first")
            with pe.Fori(0, (UNITS - 2) // 2) as i:
                unit(2 * i + 1, 1, "body")
                unit(2 * i + 2, 0, "body")
            unit(LAST, 1, "last")
            output(LAST)

        @block.scalar
        def _(act):
            A = nc.scalar

            def own(u, par):
                act.wait_ge(s_kvp, u + 1)
                A.activation(v_hi[:, par, LT], b_kv[:, HD:2 * HD], ACT.Copy).then_inc(s_vh, 1)
                A.activation(junk[:, REP], b_kv[:, 0:HD], ACT.Square, accum_out=ss[:, REP:REP + 1]).then_inc(s_sq, 1)
                act.wait_ge(s_qp, u + 1)
                for h in range(REP):
                    A.activation(junk[:, h], b_q[:, 128 * h:128 * h + 128], ACT.Square, accum_out=ss[:, h:h + 1]).then_inc(s_sq, 1)

            def turned(u, par):
                act.wait_ge(s_kcT, u + 1)
                A.activation(kT_hi[:, 0:L], b_y[:, :], ACT.Copy).then_inc(s_kch, 1)
                act.wait_ge(s_qkT, u + 1)
                A.activation(kT_hi[:, L:NKEY], b_kv[:, 0:128], ACT.Copy).then_inc(s_qkh, 1)
                A.activation(qT_hi[:, :], b_q[:, :], ACT.Copy).then_inc(s_qkh, 1)

            def p_hi(u, k):
                act.wait_ge(s_pt, 5 * u + k + 1)
                if k >= NPT:
                    act.wait_ge(s_pv, 5 * u + k - NPT + 1)
                A.activation(pT_hi[:, k % NPT], bank[(k % 4) // 2][:, 512 * (k % 2):512 * (k % 2) + 512], ACT.Copy).then_inc(s_pth, 1)

            def out_hi(u):
                act.wait_ge(s_ot, u + 1)
                A.activation(oT_hi[:, :], oT[:, :], ACT.Copy).then_inc(s_oh, 1)

            def unit(u, par, n):
                for h in range(REP):
                    act.wait_ge(s_nb, 4 * u + h + 1)
                    A.activation(P[:, h], P[:, h], ACT.Exp, bias=nb[:, h:h + 1], scale=rstd[:, par, h:h + 1],
                                 accum_out=den[:, h:h + 1]).then_inc(s_ex, 1)
                    if h == 1 and n != "first":
                        out_hi(u - 1)
                if n != "last":
                    own(u + 1, 1 - par)
                for k in range(KTILES):
                    p_hi(u, k)
                if n != "last":
                    turned(u + 1, 1 - par)

            own(0, 0)
            turned(0, 0)
            unit(0, 0, "first")
            with act.Fori(0, (UNITS - 2) // 2) as i:
                unit(2 * i + 1, 1, "body")
                unit(2 * i + 2, 0, "body")
            unit(LAST, 1, "last")
            out_hi(LAST)

        @block.vector
        def _(dve):
            V = nc.vector
            def tab(at, n, j, lo, hi, reps):
                a = rope[:, bass.ds(at, 1), n, j, lo:hi]
                return a.to_broadcast([128, reps, hi - lo]) if reps > 1 else a

            def rotate_q(u):
                at = u % B
                dve.wait_ge(s_sq, 5 * u + 5)
                q = b_q[:, :].rearrange("p (h d) -> p h d", h=REP)

                V.tensor_tensor(rot_a[:, :, :], q, tab(at, 0, 0, 0, HD, REP), ALU.mult).then_inc(s_rq, 1)
                V.tensor_tensor(rot_b[:, :, 0:64], q[:, :, 64:128], tab(at, 0, 1, 0, 64, REP), ALU.mult).then_inc(s_rq, 1)
                V.tensor_tensor(rot_b[:, :, 64:128], q[:, :, 0:64], tab(at, 0, 1, 64, 128, REP), ALU.mult).then_inc(s_rq, 1)

            def rotate_k(u, par):
                at = u % B
                dve.wait_ge(s_rs, 3 * u + 3)
                rk = rstd[:, par, REP:REP + 1]
                k1 = b_kv[:, 0:HD].unsqueeze(1)
                V.scalar_tensor_tensor(out=krot_a[:, :].unsqueeze(1), in0=k1, scalar=rk, in1=tab(at, 1, 0, 0, HD, 1),
                                       op0=ALU.mult, op1=ALU.mult).then_inc(s_rk, 1)
                V.scalar_tensor_tensor(out=krot_b[:, 0:64].unsqueeze(1), in0=k1[:, :, 64:128], scalar=rk, in1=tab(at, 1, 1, 0, 64, 1),
                                       op0=ALU.mult, op1=ALU.mult).then_inc(s_rk, 1)
                V.scalar_tensor_tensor(out=krot_b[:, 64:128].unsqueeze(1), in0=k1[:, :, 0:64], scalar=rk, in1=tab(at, 1, 1, 64, 128, 1),
                                       op0=ALU.mult, op1=ALU.mult).then_inc(s_rk, 1)
                dve.wait_ge(s_vh, u + 1)
                V.tensor_tensor(v_lo[:, par, LT], b_kv[:, HD:2 * HD], v_hi[:, par, LT].bitcast(F32), ALU.subtract).then_inc(s_kr, 1)
                dve.wait_ge(s_rk, 3 * u + 3)
                V.tensor_tensor(krot_a[:, :], krot_a[:, :], krot_b[:, :], ALU.add).then_inc(s_kr, 1)

            def turned(u, par):
                dve.wait_ge(s_kch, u + 1)
                V.tensor_tensor(kT_lo[:, 0:L], b_y[:, :], kT_hi[:, 0:L].bitcast(F32), ALU.subtract).then_inc(s_qkl, 1)
                dve.wait_ge(s_qkh, 2 * u + 2)
                V.tensor_tensor(kT_lo[:, L:NKEY], b_kv[:, 0:128], kT_hi[:, L:NKEY].bitcast(F32), ALU.subtract).then_inc(s_qkl, 1)
                V.tensor_tensor(qT_lo[:, :], b_q[:, :], qT_hi[:, :].bitcast(F32), ALU.subtract).then_inc(s_qkl, 1)

            def p_lo(u, k):
                dve.wait_ge(s_pth, 5 * u + k + 1)
                V.tensor_tensor(pT_lo[:, k % NPT], bank[(k % 4) // 2][:, 512 * (k % 2):512 * (k % 2) + 512],
                                pT_hi[:, k % NPT].bitcast(F32), ALU.subtract).then_inc(s_ptl, 1)

            def add_y(u):
                dve.wait_ge(s_y, u + 1)
                dve.wait_ge(s_ya, u + 1)
                ya = yacc[:, bass.ds(u % B, 1), :].rearrange("p o n -> p (o n)")
                V.tensor_tensor(ya, b_y[:, :], ya, ALU.add).then_inc(s_ya, 1)

            def unit(u, par, n):
                dve.wait_ge(s_mk[par], (u // 2) * 16 + 16)

                def biggest(h):
                    wait_alone(dve, s_tick_dve, (s_sc, 4 * u + h + 1))
                    V.tensor_tensor_reduce(out=P[:, h], in0=bank[h % 2][:, 0:NKEY], in1=mask[:, par], scale=1.0, scalar=-3e38,
                                           op0=ALU.add, op1=ALU.max, accum_out=mx[:, h:h + 1]).then_inc(s_mx, 1)

                def bias(h):
                    dve.wait_ge(s_mx, 4 * u + h + 1)
                    V.tensor_scalar(nb[:, h:h + 1], mx[:, h:h + 1], -1.0, rstd[:, par, h:h + 1], ALU.mult, ALU.mult).then_inc(s_nb, 1)

                biggest(0)
                biggest(1)
                bias(0)
                bias(1)
                if n != "first":
                    out_norm(u - 1)
                biggest(2)
                bias(2)
                biggest(3)
                bias(3)
                dve.wait_ge(s_ex, 4 * u + 4)
                V.reciprocal(rden[:, par], den[:, :]).then_inc(s_rd, 1)
                if n != "last":
                    rotate_q(u + 1)
                    rotate_k(u + 1, 1 - par)
                p_lo(u, 0)
                if n != "first":
                    add_y(u - 1)
                for k in range(1, KTILES):
                    p_lo(u, k)
                if n != "last":
                    turned(u + 1, 1 - par)

            def out_norm(u):
                dve.wait_ge(s_pv, 5 * u + 5)
                dve.wait_ge(s_bc, 16 * u + 16)
                V.tensor_tensor(oT[:, :].rearrange("p (h s) -> p h s", h=REP), b_o[:, :].rearrange("p (h s) -> p h s", h=REP),
                                bc[:, :, :].rearrange("p s h -> p h s"), ALU.mult).then_inc(s_ot, 1)

            rotate_q(0)
            rotate_k(0, 0)
            turned(0, 0)
            unit(0, 0, "first")
            with dve.Fori(0, (UNITS - 2) // 2) as i:
                unit(2 * i + 1, 1, "body")
                unit(2 * i + 2, 0, "body")
            unit(LAST, 1, "last")
            out_norm(LAST)
            add_y(LAST)

        @block.gpsimd
        def _(pool):
            G = nc.gpsimd
            G.memset(yacc[:, :, :], 0.0).then_inc(s_ya, 1)
            G.memset(c_mul[:, 0:REP], 1.0).then_inc(s_c, 1)
            G.memset(c_mul[:, REP:REP + 1], 1.0 / HD).then_inc(s_c, 1)
            G.memset(c_add[:, 0:REP], HD * EPS).then_inc(s_c, 1)
            G.memset(c_add[:, REP:REP + 1], EPS).then_inc(s_c, 1)
            G.memset(c_pow[:, :], -0.5).then_inc(s_c, 1)

            def chunk(n, par, group_par, added=None):
                at = group_par * WCOLS + (n % B) * CH
                wait_alone(pool, s_tick_pool, *([(s_ya, added)] if added is not None else []), (s_wraw[par], (n // 2) * 16 + 16))
                G.tensor_copy(w_hi[:, bass.ds(at, CH)], w_raw[:, par]).then_inc(s_wh, 1)
                wait_alone(pool, s_tick_pool, (s_wh, n + 1))
                G.tensor_tensor(w_lo[:, bass.ds(at, CH)], w_raw[:, par], w_hi[:, bass.ds(at, CH)].bitcast(F32), ALU.subtract).then_inc(s_ws, 1)

            def norms(u, par):
                pool.wait_ge(s_sq, 5 * u + 5)
                G.tensor_tensor(rs_a[:, :], ss[:, :], c_mul[:, :], ALU.mult).then_inc(s_rs, 1)
                pool.wait_ge(s_rs, 3 * u + 1)
                G.tensor_tensor(rs_b[:, :], rs_a[:, :], c_add[:, :], ALU.add).then_inc(s_rs, 1)
                pool.wait_ge(s_rs, 3 * u + 2)
                G.tensor_tensor(rstd[:, par], rs_b[:, :], c_pow[:, :], ALU.pow).then_inc(s_rs, 1)

            def add_q(u):
                pool.wait_ge(s_rq, 3 * u + 3)
                G.tensor_tensor(rot_a[:, :, :], rot_a[:, :, :], rot_b[:, :, :], ALU.add).then_inc(s_qa, 1)

            def values(u, par):
                wait_alone(pool, s_tick_pool, (s_kv[par], (u // 2) * 16 * NPP + 16 * NPP))
                G.tensor_copy(v_hi[:, par, 0:LT], kv[:, par, :, 1]).then_inc(s_vc, 1)
                pool.wait_ge(s_vc, u + 1)
                G.tensor_tensor(v_lo[:, par, 0:LT], kv[:, par, :, 1], v_hi[:, par, 0:LT].bitcast(F32), ALU.subtract).then_inc(s_vs, 1)

            def out_lo(u):
                pool.wait_ge(s_oh, u + 1)
                G.tensor_tensor(oT_lo[:, :], oT[:, :], oT_hi[:, :].bitcast(F32), ALU.subtract).then_inc(s_ol, 1)

            def unit(u, par, n):
                if n != "first":
                    out_lo(u - 1)
                if n != "last":
                    norms(u + 1, 1 - par)
                    add_q(u + 1)
                    chunk(u + B, par, (u // B + 1) % 2, u if n == "body" else None)
                    values(u + 1, 1 - par)

            pool.wait_ge(s_c, 5)
            norms(0, 0)
            add_q(0)
            values(0, 0)
            unit(0, 0, "first")
            with pool.Fori(0, (UNITS - 2) // 2) as i:
                unit(2 * i + 1, 1, "body")
                unit(2 * i + 2, 0, "body")
            unit(LAST, 1, "last")
            out_lo(LAST)


def layer1_ffn(nc, t, dram, keep, out):
    with ExitStack() as ctx:
        def sb(name, shape, dt=F32):
            return ctx.enter_context(nc.sbuf_tensor(name, shape, dt))

        def ps(name, shape, dt=F32):
            return ctx.enter_context(nc.psum_tensor(name, shape, dt))

        def sem(name):
            return ctx.enter_context(nc.semaphore(name))

        ident, yacc = keep["ident"], keep["yacc"]
        NZ = NE * RANK
        a_raw = sb("a_raw", [128, KT, NZ])
        a_hi, a_lo = [w[:, 0:KT * NZ].rearrange("p (k n) -> p k n", k=KT) for w in (keep["wg_hi"], keep["wg_lo"])]
        b_hi, b_lo = [w[:, KT * NZ:KT * (NZ + D)].rearrange("p (k n) -> p k n", k=KT) for w in (keep["wg_hi"], keep["wg_lo"])]
        b_raw = sb("b_raw", [128, KT, D])
        r_raw = sb("r_raw", [128, KT, RD])
        r_hi = sb("r_hi", [128, KT, RD], F32R)
        r_lo = sb("r_lo", [128, KT, RD], F32R)
        keysT = sb("keysT", [RD, NE])
        yT_hi = sb("y1T_hi", [128, KT, 128], F32R)
        yT_lo = sb("y1T_lo", [128, KT, 128], F32R)
        rq = sb("rq", [128, RD])
        rqT = sb("rqT", [RD, 128])
        sc = sb("sc", [128, NE])
        v1 = sb("v1", [128, 8])
        v2 = sb("v2", [128, 8])
        r1 = sb("r1", [128, NE])
        r2 = sb("r2", [128, NE])
        nm = sb("nm", [128, 1])
        e = sb("e", [128, NE])
        sel = sb("sel", [128, NE])
        es = sb("es", [128, NE])
        tot = sb("tot", [128, 1])
        rt = sb("rt", [128, 1])
        gate = sb("gate", [128, NE])
        zg = sb("zg", [128, NZ])
        zT_hi = sb("zT_hi", [128, KT, 128], F32R)
        zT_lo = sb("zT_lo", [128, KT, 128], F32R)
        x1 = sb("x1_l1", [128, B, D])
        res = sb("res", [128, B, D])
        ybuf = sb("ybuf", [128, D])

        p_y = ps("p1_y", [128, 512])
        p_z = ps("p1_z", [128, 512])
        p_q = ps("p1_q", [128, 512])
        p_qT = ps("p1_qT", [128, 512])
        p_s = ps("p1_s", [128, 512])
        p_zT = ps("p1_zT", [128, 512])
        p_o = ps("p1_o", [128, 512])

        s_tick_sp, s_tick_dve = sem("f_tick_sp"), sem("f_tick_dve")
        s_in = sem("f_in")
        s_x1 = sem("f_x1")
        s_whi, s_wlo = sem("f_whi"), sem("f_wlo")
        s_yT = sem("f_yT")
        s_yhi, s_ylo = sem("f_yhi"), sem("f_ylo")
        s_z = sem("f_z")
        s_q = sem("f_q")
        s_qs = sem("f_qs")
        s_qT = sem("f_qT")
        s_qTs = sem("f_qTs")
        s_s = sem("f_s")
        s_g = sem("f_g")
        s_e = sem("f_e")
        s_zg = sem("f_zg")
        s_zT = sem("f_zT")
        s_zhi, s_zlo = sem("f_zhi"), sem("f_zlo")
        s_o = sem("f_o")
        s_res = sem("f_res")
        s_out = sem("f_out")
        s_yb = sem("f_yb")
        GS = 11

        block = ctx.enter_context(nc.Block())

        @block.sync
        def _(sp):
            sp.dma_start(r_raw[:, :, :], t["routerT"].rearrange("(k p) n -> p k n", p=128)).then_inc(s_in, 16)
            sp.dma_start(a_raw[:, :, :], t["AT"].rearrange("(k p) n -> p k n", p=128)).then_inc(s_in, 16)
            sp.dma_start(keysT[:, :], t["keysT"]).then_inc(s_in, 16)
            sp.dma_start(b_raw[:, :, :], t["BT"].rearrange("(k p) n -> p k n", p=128)).then_inc(s_in, 16)
            sp.dma_start(x1[:, :, :], dram["x1"].rearrange("b p n -> p b n")).then_inc(s_x1, 16)
            with sp.Fori(0, B) as n:
                wait_alone(sp, s_tick_sp, (s_res, n + 1))
                sp.dma_start(out[bass.ds(n, 1)].rearrange("o p n -> (o p) n"),
                             res[:, bass.ds(n, 1), :].rearrange("p o n -> p (o n)")).then_inc(s_out, 16)
            sp.wait_ge(s_out, 16 * B)

        @block.tensor
        def _(pe):
            PE = nc.tensor
            pe.wait_ge(s_wlo, 3)
            with pe.Fori(0, B) as n:
                pe.wait_ge(s_yb, n + 1)
                for k in range(KT):
                    mm = PE.transpose(p_y[:, 128 * k:128 * k + 128], ybuf[:, 128 * k:128 * k + 128], ident[:, :])
                mm.then_inc(s_yT, 1)
                pe.wait_ge(s_ylo, n + 1)
                terms = [(y, c, k) for y, c in ((yT_hi, 0), (yT_hi, 1), (yT_lo, 0)) for k in range(KT)]
                for m, (y, c, k) in enumerate(terms):
                    mm = PE.matmul(p_q[:, 0:RD], y[:, k, :], (r_hi, r_lo)[c][:, k, :], start=(m == 0), stop=(m == len(terms) - 1))
                mm.then_inc(s_q, 1)
                for m, (y, c, k) in enumerate(terms):
                    mm = PE.matmul(p_z[:, :], y[:, k, :], (a_hi, a_lo)[c][:, k, :], start=(m == 0), stop=(m == len(terms) - 1))
                mm.then_inc(s_z, 1)
                pe.wait_ge(s_qs, n + 1)
                PE.transpose(p_qT[0:RD, 0:128], rq[:, :], ident[:, :]).then_inc(s_qT, 1)
                pe.wait_ge(s_qTs, n + 1)
                PE.matmul(p_s[:, 0:NE], rqT[:, :], keysT[:, :], start=True, stop=True).then_inc(s_s, 1)
                pe.wait_ge(s_zg, n + 1)
                for k in range(KT):
                    mm = PE.transpose(p_zT[:, 128 * k:128 * k + 128], zg[:, 128 * k:128 * k + 128], ident[:, :])
                mm.then_inc(s_zT, 1)
                pe.wait_ge(s_zlo, n + 1)
                for m, (z, c, k) in enumerate([(z, c, k) for z, c in ((zT_hi, 0), (zT_hi, 1), (zT_lo, 0)) for k in range(KT)]):
                    mm = PE.matmul(p_o[:, :], z[:, k, :], (b_hi, b_lo)[c][:, k, :], start=(m == 0), stop=(m == 3 * KT - 1))
                mm.then_inc(s_o, 1)

        @block.scalar
        def _(act):
            A = nc.scalar
            act.wait_ge(s_in, 64)
            A.activation(r_hi[:, :, :], r_raw[:, :, :], ACT.Copy).then_inc(s_whi, 1)
            A.activation(a_hi[:, :, :], a_raw[:, :, :], ACT.Copy).then_inc(s_whi, 1)
            A.activation(b_hi[:, :, :], b_raw[:, :, :], ACT.Copy).then_inc(s_whi, 1)
            with act.Fori(0, B) as n:
                act.wait_ge(s_yT, n + 1)
                A.activation(yT_hi[:, :, :], p_y[:, :].rearrange("p (k n) -> p k n", k=KT), ACT.Copy).then_inc(s_yhi, 1)
                act.wait_ge(s_q, n + 1)
                A.activation(rq[:, :], p_q[:, 0:RD], ACT.Copy).then_inc(s_qs, 1)
                act.wait_ge(s_qT, n + 1)
                A.activation(rqT[:, :], p_qT[0:RD, 0:128], ACT.Copy).then_inc(s_qTs, 1)
                act.wait_ge(s_g, GS * n + 3)
                A.activation(e[:, :], sc[:, :], ACT.Exp, bias=nm[:, 0:1]).then_inc(s_e, 1)
                act.wait_ge(s_zT, n + 1)
                A.activation(zT_hi[:, :, :], p_zT[:, :].rearrange("p (k n) -> p k n", k=KT), ACT.Copy).then_inc(s_zhi, 1)

        @block.vector
        def _(dve):
            V = nc.vector
            V.tensor_copy(ybuf[:, :], yacc[:, 0, :]).then_inc(s_yb, 1)
            for n, (lo, raw, hi) in enumerate(((r_lo, r_raw, r_hi), (a_lo, a_raw, a_hi), (b_lo, b_raw, b_hi))):
                dve.wait_ge(s_whi, n + 1)
                V.tensor_tensor(lo[:, :, :], raw[:, :, :], hi[:, :, :].bitcast(F32), ALU.subtract).then_inc(s_wlo, 1)

            def batch(n, more):
                dve.wait_ge(s_yhi, n + 1)
                V.tensor_tensor(yT_lo[:, :, :], p_y[:, :].rearrange("p (k n) -> p k n", k=KT), yT_hi[:, :, :].bitcast(F32),
                                ALU.subtract).then_inc(s_ylo, 1)
                if more:
                    V.tensor_copy(ybuf[:, :], yacc[:, bass.ds(n + 1, 1), :].rearrange("p o n -> p (o n)")).then_inc(s_yb, 1)
                dve.wait_ge(s_s, n + 1)
                V.tensor_copy(sc[:, :], p_s[:, 0:NE]).then_inc(s_g, 1)
                wait_alone(dve, s_tick_dve, (s_g, GS * n + 1))
                V.max(v1[:, :], sc[:, :]).then_inc(s_g, 1)
                wait_alone(dve, s_tick_dve, (s_g, GS * n + 2))
                V.tensor_scalar(nm[:, :], v1[:, 0:1], -1.0, None, ALU.mult).then_inc(s_g, 1)
                V.match_replace(r1[:, :], v1[:, :], sc[:, :], -3e38).then_inc(s_g, 1)
                wait_alone(dve, s_tick_dve, (s_g, GS * n + 4))
                V.max(v2[:, :], r1[:, :]).then_inc(s_g, 1)
                wait_alone(dve, s_tick_dve, (s_g, GS * n + 5))
                V.match_replace(r2[:, :], v2[:, :], r1[:, :], -3e38).then_inc(s_g, 1)
                dve.wait_ge(s_g, GS * n + 6)
                V.tensor_tensor(sel[:, :], r2[:, :], sc[:, :], ALU.not_equal).then_inc(s_g, 1)
                wait_alone(dve, s_tick_dve, (s_g, GS * n + 7), (s_e, n + 1))
                V.tensor_tensor_reduce(out=es[:, :], in0=e[:, :], in1=sel[:, :], scale=1.0, scalar=0.0,
                                       op0=ALU.mult, op1=ALU.add, accum_out=tot[:, :]).then_inc(s_g, 1)
                wait_alone(dve, s_tick_dve, (s_g, GS * n + 8))
                V.reciprocal(rt[:, :], tot[:, :]).then_inc(s_g, 1)
                dve.wait_ge(s_g, GS * n + 9)
                V.tensor_scalar(gate[:, :], es[:, :], rt[:, 0:1], 2.0, ALU.mult, ALU.mult).then_inc(s_g, 1)
                dve.wait_ge(s_g, GS * n + 10)
                dve.wait_ge(s_z, n + 1)
                V.tensor_tensor(zg[:, :].rearrange("p (e r) -> p e r", e=NE), p_z[:, :].rearrange("p (e r) -> p e r", e=NE),
                                gate[:, :].unsqueeze(2).to_broadcast([128, NE, RANK]), ALU.mult).then_inc(s_zg, 1)
                dve.wait_ge(s_zhi, n + 1)
                V.tensor_tensor(zT_lo[:, :, :], p_zT[:, :].rearrange("p (k n) -> p k n", k=KT), zT_hi[:, :, :].bitcast(F32),
                                ALU.subtract).then_inc(s_zlo, 1)
                dve.wait_ge(s_o, n + 1)
                x = x1[:, bass.ds(n, 1), :].rearrange("p o n -> p (o n)")
                r = res[:, bass.ds(n, 1), :].rearrange("p o n -> p (o n)")
                V.tensor_tensor(r, p_o[:, :], x, ALU.add).then_inc(s_res, 1)
                V.engine_nop().then_inc(s_g, 1)

            dve.wait_ge(s_x1, 16)
            with dve.Fori(0, B - 1) as n:
                batch(n, True)
            batch(B - 1, False)


def program(nc, t, out):
    dram = {
        "x1": nc.dram_tensor("x1_dram", [B, S, D], F32, kind="Internal").ap(),
        "x1T": nc.dram_tensor("x1T_dram", [B, 128, 2 * KT * 128], F32, kind="Internal").ap(),
        "mask": nc.dram_tensor("mask_dram", [B, NKEY], BF16, kind="Internal").ap(),
        "rden": nc.dram_tensor("rden_dram", [S, REP], F32, kind="Internal").ap(),
    }
    with ExitStack() as ctx:
        keep = {
            "ident": ctx.enter_context(nc.sbuf_tensor("ident", [128, 128], F32)),
            "rope": ctx.enter_context(nc.sbuf_tensor("rope", [128, B, 2, 2, HD], F32)),
            "s_wraw": [ctx.enter_context(nc.semaphore(f"s_wraw{n}")) for n in range(2)],
            "s_wh": ctx.enter_context(nc.semaphore("s_wh")),
            "s_ws": ctx.enter_context(nc.semaphore("s_ws")),
            "wg_raw": ctx.enter_context(nc.sbuf_tensor("wg_raw", [128, 2, CH], F32)),
            "wg_hi": ctx.enter_context(nc.sbuf_tensor("wg_hi", [128, 2 * WCOLS], F32R)),
            "wg_lo": ctx.enter_context(nc.sbuf_tensor("wg_lo", [128, 2 * WCOLS], F32R)),
            "yacc": ctx.enter_context(nc.sbuf_tensor("yacc", [128, B, D], F32)),
        }
        layer0(nc, t, dram, keep)
        attention(nc, t, dram, keep)
        layer1_ffn(nc, t, dram, keep, out)


def kernel(**inputs):
    import numpy as np
    import concourse.bacc as bacc
    from concourse import mybir as _mybir
    from concourse.bass_utils import run_bass_kernel_spmd

    def a(name):
        return np.asarray(inputs[name])

    x = a("x")
    wq = a("L1_cond_Wq").reshape(HK, GQ, KT, 128).transpose(0, 3, 2, 1).reshape(HK, 128, WQ)
    wkv = np.stack([a("L1_cond_Wk").reshape(HK, HD, KT, 128), a("L1_cond_Wv").reshape(HK, HD, KT, 128)], 1)
    wkv = wkv.transpose(0, 4, 3, 1, 2).reshape(HK, 128, WKV)
    wo = a("L1_cond_Wo").reshape(D, HK, REP, HD).transpose(1, 3, 2, 0).reshape(HK, 128, WO)
    wg = np.concatenate([wq, wkv, wo], 2).reshape(HK, 128, B, CH).transpose(0, 2, 1, 3).reshape(UNITS, 128, CH)
    kv = np.stack([a("L1_cond_k_cache"), a("L1_cond_v_cache")], 3)
    kv = kv.transpose(2, 0, 1, 3, 4).reshape(HK, kv.shape[0], PAGE, 2 * HD)
    laid = {
        "x": x,
        "xT": x.transpose(0, 2, 1),
        "lora_id": a("itok_B_3_7"),
        "pages": a("itok_Bx16_0_63"),
        "seq": a("itok_B_207_1644"),
        "loraT": a("L0_cond_weight").transpose(0, 2, 1),
        "baseT": a("L0_ffn_base_w").T,
        "lgT": np.concatenate([a("L0_ffn_lora_A").reshape(E0 * R0, D), a("L0_ffn_gate_w")], 0).T,
        "loraBT": a("L0_ffn_lora_B").transpose(0, 2, 1).reshape(E0 * R0, D),
        "base_b": a("L0_ffn_base_b"),
        "qn": a("L1_cond_q_norm_w"),
        "kn": a("L1_cond_k_norm_w"),
        "wg": wg,
        "kv": kv,
        "AT": a("L1_ffn_A_w").T,
        "BT": a("L1_ffn_B_w").T,
        "routerT": a("L1_ffn_Wq_w").T,
        "keysT": a("L1_ffn_keys").T,
        "ident": np.eye(128, dtype=np.float32),
        "tok": np.arange(S, dtype=np.float32).reshape(S, 1),
        "keyno": np.arange(L, dtype=np.float32),
        "invf": np.float32(1.0) / (10000.0 ** (np.arange(0, HD, 2, dtype=np.float32) / np.float32(HD)).astype(np.float64)).astype(np.float32),
    }
    nc = bacc.Bacc("TRN2", target_bir_lowering=False, num_devices=1)
    arrays, t = {}, {}
    for name, v in laid.items():
        v = np.ascontiguousarray(v)
        arrays[f"in_{name}"] = v
        t[name] = nc.dram_tensor(f"in_{name}", v.shape, _mybir.dt.from_np(v.dtype), kind="ExternalInput").ap()
    out = nc.dram_tensor("out_x", (B, S, D), _mybir.dt.float32, kind="ExternalOutput").ap()
    program(nc, t, out)
    r = run_bass_kernel_spmd(nc, [arrays], core_ids=[0])
    return r.results[0]["out_x"]
```

```python
from contextlib import ExitStack

import concourse.bass as bass
from concourse import mybir

ALU = mybir.AluOpType
ACT = mybir.ActivationFunctionType
F32 = mybir.dt.float32
F32R = mybir.dt.float32r
BF16 = mybir.dt.bfloat16
I32 = mybir.dt.int32
U32 = mybir.dt.uint32

B, S, D = 8, 128, 512
KT = D // 128
HD, HQ, HK = 128, 32, 8
REP = HQ // HK
GQ = REP * HD
PAGE, NPP = 32, 16
L = PAGE * NPP
LT = L // 128
NKEY = L + S
KTILES = NKEY // 128
E0, R0 = 8, 16
NE, RANK, RD = 64, 8, 16
UNITS = HK * B
WQ, WKV, WO = KT * GQ, KT * 2 * HD, REP * D
WCOLS = WQ + WKV + WO
NZ = NE * RANK
NPT = 4
CH = WCOLS // B
FCOLS = KT * (NZ + D + RD)
assert FCOLS <= (B - 1) * CH
EPS = 1e-6
NEG = -1e30
TWO_PI_HI = 6.28125
TWO_PI_MID = 2029.0 / 2 ** 20
TWO_PI_LO = 6.283185307179586 - TWO_PI_HI - TWO_PI_MID
ROUND = 1.5 * 2 ** 23
PI_SAFE = 3.1415925


def wait_alone(eng, tick, *waits):
    for s, v in waits:
        eng.wait_ge(s, v)
        eng.sem_inc(tick, 1)


def page_numbers(nc, keep, u):
    return nc.values_load_multi_w_load_instructions(
        keep["pages"][0:1, bass.ds((u % B) * NPP, NPP)], engines=(mybir.EngineType.SP,), min_val=0, max_val=63)[1]


def load_kv(nc, sp, t, keep, u, slot, numbers, j0, j1):
    for j in range(j0, j1):
        at = PAGE * (j % 4)
        src = t["kv"][bass.ds(u // B, 1), bass.ds(numbers[j], 1)]
        sp.dma_start(keep["kv"][at:at + PAGE, slot, j // 4].rearrange("p a d -> p (a d)"),
                     src.rearrange("g o k n -> (g o k) n")).then_inc(keep["s_kv"][slot], 16)


def load_x1T(sp, dram, keep, u, slot):
    sp.dma_start(keep["xT"][:, slot].bitcast(F32).rearrange("p a k n -> p (a k n)"),
                 dram["x1T"][bass.ds(u % B, 1)].rearrange("o p n -> (o p) n")).then_inc(keep["s_xT"][slot], 16)


def layer0(nc, t, dram, keep):
    with ExitStack() as ctx:
        def sb(name, shape, dt=F32):
            return ctx.enter_context(nc.sbuf_tensor(name, shape, dt))

        def ps(name, shape, dt=F32):
            return ctx.enter_context(nc.psum_tensor(name, shape, dt))

        def sem(name):
            return ctx.enter_context(nc.semaphore(name))

        ident, rope, yacc = keep["ident"], keep["rope"], keep["yacc"]
        wg_hi, wg_lo, wg_raw = keep["wg_hi"], keep["wg_lo"], keep["wg_raw"]
        NLG = E0 * R0 + E0

        seq_i = sb("seq_i", [128, B], I32)
        seq_f = sb("seq_f", [128, B])
        pos = sb("pos", [128, B])
        tok = sb("tok", [128, 1])
        invf = sb("invf", [128, 64])
        normw = sb("normw", [128, 2, 128])
        keyno = sb("keyno", [1, L])
        ids = sb("ids", [1, B], I32)
        scratch = yacc[:, :, :].rearrange("p b d -> p (b d)")
        NA = B * 64
        ang = scratch[:, 0:NA].rearrange("p (b n) -> p b n", b=B)
        turn = [scratch[:, (1 + c) * NA:(2 + c) * NA].rearrange("p (b n) -> p b n", b=B) for c in range(2)]
        red = [scratch[:, (3 + c) * NA:(4 + c) * NA].rearrange("p (b n) -> p b n", b=B) for c in range(2)]
        mask = scratch[0:1, 0:B * NKEY // 2].bitcast(BF16).rearrange("p (b n) -> p b n", b=B)
        assert B * NKEY // 2 <= 5 * NA
        trig = [scratch[:, (5 + c) * NA:(6 + c) * NA].rearrange("p (b n) -> p b n", b=B) for c in range(2)]
        w_raw = [keep["raw"], sb("w_raw1", [128, KT, D])[:, :, :]]

        def borrowed(at, n):
            return [w[:, WCOLS + at:WCOLS + at + KT * n].rearrange("p (k n) -> p k n", k=KT) for w in (wg_hi, wg_lo)]

        base_hi, base_lo = borrowed(0, D)
        w_hi, w_lo = [[sb(name, [128, KT, D], F32R)[:, :, :], second]
                      for name, second in zip(("w_hi", "w_lo"), borrowed(KT * D, D))]
        xT_hi, xT_lo = [[sb(name, [128, KT, 128], F32R)[:, :, :], second]
                        for name, second in zip(("xT_hi", "xT_lo"), borrowed(2 * KT * D, 128))]
        yT_hi, yT_lo = borrowed(2 * KT * D + KT * 128, 128)
        base_raw = keep["base_raw"]
        lg_raw = sb("lg_raw", [128, KT, NLG])
        lg_hi = sb("lg_hi", [128, KT, NLG], F32R)
        lg_lo = sb("lg_lo", [128, KT, NLG], F32R)
        lb_raw = sb("lb_raw", [128, D])
        lb_hi = sb("lb_hi", [128, D], F32R)
        lb_lo = sb("lb_lo", [128, D], F32R)
        bias = sb("bias", [128, D])
        xT_raw = sb("xT_raw", [128, 2, KT, 128])
        x_raw = sb("x_raw", [128, 2, D])
        y = sb("y_l0", [128, D])
        xb = sb("xb", [128, 2, D])
        lgs = sb("lgs", [128, E0])
        v8 = sb("v8", [128, 8])
        i8 = sb("i8", [128, 8], U32)
        i8f = sb("i8f", [128, 8])
        iota8 = sb("iota8", [128, E0])
        diff = sb("diff", [128, 1])
        ex = sb("ex_l0", [128, 1])
        den = sb("den_l0", [128, 1])
        pr = sb("pr", [128, 2])
        wa = sb("wa", [128, E0])
        wb = sb("wb", [128, E0])
        wf = sb("wf", [128, E0])
        low = sb("low", [128, E0 * R0])
        lowT_hi = sb("lowT_hi", [128, 128], F32R)
        lowT_lo = sb("lowT_lo", [128, 128], F32R)
        x1T = base_raw[:, 0:2].bitcast(F32R).rearrange("p a (k n) -> p a k n", k=KT)
        x1 = base_raw[:, 2]

        p_y = ps("p_y", [128, D])
        p_yT = ps("p_yT", [128, KT, 128])
        p_r = [ps("p_r0", [128, D]), ps("p_r1", [128, D])]
        p_lg = ps("p_lg", [128, 512])
        p_t = ps("p_t", [128, 512])
        p_x = ps("p_x", [128, KT, 128])

        s_tick_sp, s_tick_dve = sem("l0_tick_sp"), sem("l0_tick_dve")
        s_tick_pool = sem("l0_tick_pool")
        s_ang = sem("l0_ang")
        s_const = sem("l0_const")
        s_ids = sem("l0_ids")
        s_base = sem("l0_base")
        s_low_w = sem("l0_low_w")
        s_bias = sem("l0_bias")
        s_w = [sem("l0_w0"), sem("l0_w1")]
        s_x = [sem("l0_x0"), sem("l0_x1")]
        s_wraw, s_wh, s_ws = keep["s_wraw"], keep["s_wh"], keep["s_ws"]
        s_tab = sem("l0_tab")
        s_red = sem("l0_red")
        s_trig = sem("l0_trig")
        s_tables = sem("l0_tables")
        s_whi, s_wlo = sem("l0_whi"), sem("l0_wlo")
        s_bhi, s_blo = sem("l0_bhi"), sem("l0_blo")
        s_bpl = sem("l0_bpl")
        s_xb = sem("l0_xb")
        s_y = sem("l0_y")
        s_yc = sem("l0_yc")
        s_yT = sem("l0_yT")
        s_yhi, s_ylo = sem("l0_yhi"), sem("l0_ylo")
        s_lg = sem("l0_lg")
        s_base_mm = sem("l0_base_mm")
        s_gate = sem("l0_gate")
        s_exp = sem("l0_exp")
        s_low = sem("l0_low")
        s_lt = sem("l0_lt")
        s_lthi, s_ltlo = sem("l0_lthi"), sem("l0_ltlo")
        s_r = sem("l0_r")
        s_x1 = sem("l0_x1s")
        s_xt = sem("l0_xt")
        s_xthi, s_xtlo = sem("l0_xthi"), sem("l0_xtlo")
        s_mask = sem("l0_mask")
        s_mst = sem("l0_mst")
        s_st, s_stT = keep["s_st"], keep["s_stT"]

        block = ctx.enter_context(nc.Block())
        HK2 = KT // 2

        @block.sync
        def _(sp):
            def rows(a, n):
                return a.rearrange("(o n) -> o n", o=1).to_broadcast([128, n])

            def load_w(b, slot):
                a = sp.value_load(ids[0:1, bass.ds(b, 1)], min_val=0, max_val=7)
                sp.dma_start(w_raw[slot],
                             t["loraT"][bass.ds(a, 1)].rearrange("o (k p) n -> p (o k) n", p=128)).then_inc(s_w[slot], 16)
                sp.dma_start(xT_raw[:, slot, :, :],
                             t["xT"][bass.ds(b, 1)].rearrange("o (k p) n -> p (o k) n", p=128)).then_inc(s_w[slot], 16)

            def load_x(b, slot):
                sp.dma_start(x_raw[:, slot, :], t["x"][bass.ds(b, 1)].rearrange("o p n -> (o p) n")).then_inc(s_x[slot], 16)

            def load_wg(c, slot):
                sp.dma_start(wg_raw[:, slot], t["wg"][bass.ds(c, 1)].rearrange("o p n -> (o p) n")).then_inc(s_wraw[slot], 16)

            sp.dma_start(ids[:, :], t["lora_id"].rearrange("(o b) -> o b", o=1)).then_inc(s_ids, 16)
            sp.dma_start(seq_i[:, :], rows(t["seq"], B)).then_inc(s_ang, 16)
            sp.dma_start(tok[:, :], t["tok"]).then_inc(s_ang, 16)
            sp.dma_start(invf[:, :], rows(t["invf"], 64)).then_inc(s_ang, 16)
            sp.wait_ge(s_ids, 16)
            load_w(0, 0)
            sp.dma_start(ident[:, :], t["ident"]).then_inc(s_const, 16)
            sp.dma_start(lg_raw[:, :, :], t["lgT"].rearrange("(k p) n -> p k n", p=128)).then_inc(s_low_w, 16)
            load_w(1, 1)
            sp.dma_start(iota8[:, :], rows(t["keyno"][0:E0], E0)).then_inc(s_const, 16)
            sp.dma_start(base_raw[:, :, :], t["baseT"].rearrange("(k p) n -> p k n", p=128)).then_inc(s_base, 16)
            sp.dma_start(lb_raw[:, :], t["loraBT"]).then_inc(s_base, 16)
            sp.dma_start(bias[:, :], rows(t["base_b"], D)).then_inc(s_bias, 16)
            load_x(0, 0)
            sp.dma_start(keyno[:, :], t["keyno"].rearrange("(o n) -> o n", o=1)).then_inc(s_const, 16)
            sp.dma_start(normw[:, 0, :], rows(t["qn"], 128)).then_inc(s_const, 16)
            sp.dma_start(normw[:, 1, :], rows(t["kn"], 128)).then_inc(s_const, 16)
            load_wg(0, 0)
            load_x(1, 1)
            load_wg(1, 1)

            def next_w(b, slot):
                wait_alone(sp, s_tick_sp, (s_blo, 2 * b - 2), (s_bpl, b - 1))
                load_w(b, slot)

            def next_x(b, slot):
                wait_alone(sp, s_tick_sp, (s_xb, b - 1))
                load_x(b, slot)
                wait_alone(sp, s_tick_sp, (s_ws, b - 1))
                load_wg(b, slot)

            sp.dma_start(keep["pages"][:, :], t["pages"].rearrange("(o b) p -> o (b p)", o=1)).then_inc(s_ids, 16)
            next_w(2, 0)
            next_w(3, 1)
            with sp.Fori(1, B // 2 - 1) as i:
                for slot in range(2):
                    next_w(2 * i + slot + 2, slot)
                    next_x(2 * i + slot, slot)
            sp.wait_ge(s_mask, 1 + B)
            sp.dma_start(dram["mask"].rearrange("(o b) n -> o (b n)", o=1), mask.rearrange("p b n -> p (b n)")).then_inc(s_mst, 16)
            next_x(B - 2, 0)
            sp.wait_ge(s_ids, 32)
            sp.wait_ge(s_blo, 2 * B - 2)
            sp.wait_ge(s_bpl, B - 1)
            sp.wait_ge(s_stT, 32)
            for u in range(2):
                load_x1T(sp, dram, keep, u, u)
            load_kv(nc, sp, t, keep, 0, 0, page_numbers(nc, keep, 0), 0, NPP)
            next_x(B - 1, 1)
            load_kv(nc, sp, t, keep, 1, 1, page_numbers(nc, keep, 1), 0, NPP // 2)
            sp.wait_ge(s_mst, 16)

        def schedule(eng, step):
            step(0, 0, "first")
            step(1, 1, "second")
            with eng.Fori(1, B // 2 - 1) as i:
                step(2 * i, 0, "body")
                step(2 * i + 1, 1, "body")
            step(B - 2, 0, "closing")
            step(B - 1, 1, "last")

        @block.gpsimd
        def _(pool):
            G = nc.gpsimd

            def split_adapter(n, slot):
                pool.wait_ge(s_bhi, 3 * n + 2)
                G.tensor_tensor(w_lo[slot][:, HK2:KT, :], w_raw[slot][:, HK2:KT], w_hi[slot][:, HK2:KT, :].bitcast(F32),
                                ALU.subtract).then_inc(s_bpl, 1)

            def step(n, slot, where):
                if where not in ("closing", "last"):
                    split_adapter(n + 2, slot)
                wait_alone(pool, s_tick_pool, (s_x[slot], (n // 2) * 16 + 16))
                if where not in ("first", "second"):
                    pool.wait_ge(s_x1, n - 1)
                G.tensor_tensor(xb[:, slot], x_raw[:, slot, :], bias[:, :], ALU.add).then_inc(s_xb, 1)
                wait_alone(pool, s_tick_pool, (s_wraw[slot], (n // 2) * 16 + 16))
                G.tensor_copy(wg_hi[:, bass.ds(n * CH, CH)], wg_raw[:, slot]).then_inc(s_wh, 1)
                wait_alone(pool, s_tick_pool, (s_wh, n + 1))
                G.tensor_tensor(wg_lo[:, bass.ds(n * CH, CH)], wg_raw[:, slot], wg_hi[:, bass.ds(n * CH, CH)].bitcast(F32),
                                ALU.subtract).then_inc(s_ws, 1)

            split_adapter(0, 0)
            split_adapter(1, 1)
            pool.wait_ge(s_trig, 2)
            G.memset(mask[:, :, L:NKEY], 0.0).then_inc(s_mask, 1)
            pool.wait_ge(s_bias, 16)
            schedule(pool, step)

        @block.vector
        def _(dve):
            V = nc.vector
            linked = [0]

            def link(ins):
                linked[0] += 1
                ins.then_inc(s_tab, 1)
                dve.wait_ge(s_tab, linked[0])

            def angles(c):
                link(V.tensor_scalar(turn[c], ang, 1 / 6.283185307179586, 0.25 * c, ALU.mult, ALU.add))
                link(V.tensor_scalar(turn[c], turn[c], ROUND, None, ALU.add))
                link(V.tensor_scalar(turn[c], turn[c], ROUND, None, ALU.subtract))
                link(V.scalar_tensor_tensor(out=red[c], in0=turn[c], scalar=-TWO_PI_HI, in1=ang, op0=ALU.mult, op1=ALU.add))
                link(V.scalar_tensor_tensor(out=red[c], in0=turn[c], scalar=-TWO_PI_MID, in1=red[c], op0=ALU.mult, op1=ALU.add))
                link(V.scalar_tensor_tensor(out=red[c], in0=turn[c], scalar=-TWO_PI_LO, in1=red[c], op0=ALU.mult, op1=ALU.add))
                if c:
                    link(V.tensor_scalar(red[c], red[c], 1.5707963267948966, None, ALU.add))
                link(V.tensor_scalar(red[c], red[c], PI_SAFE, -PI_SAFE, ALU.min, ALU.max))

            def masks():
                dve.wait_ge(s_trig, 2)
                for b in range(B):
                    V.tensor_scalar(mask[:, b, 0:L], keyno[:, :], seq_f[0:1, b:b + 1], NEG, ALU.is_ge, ALU.mult).then_inc(s_mask, 1)

            def tables():
                dve.wait_ge(s_trig, 2)
                for n in range(2):
                    for half in range(2):
                        own = normw[:, n, 64 * half:64 * half + 64].unsqueeze(1).to_broadcast([128, B, 64])
                        other = normw[:, n, 64 - 64 * half:128 - 64 * half].unsqueeze(1).to_broadcast([128, B, 64])
                        V.tensor_tensor(rope[:, :, n, 0, 64 * half:64 * half + 64], trig[1], own, ALU.mult).then_inc(s_tables, 1)
                        V.scalar_tensor_tensor(out=rope[:, :, n, 1, 64 * half:64 * half + 64], in0=trig[0],
                                               scalar=(1.0 if half else -1.0), in1=other, op0=ALU.mult, op1=ALU.mult).then_inc(s_tables, 1)

            def split_adapter(n, slot):
                dve.wait_ge(s_bhi, 3 * n + 1)
                V.tensor_tensor(w_lo[slot][:, 0:HK2, :], w_raw[slot][:, 0:HK2], w_hi[slot][:, 0:HK2, :].bitcast(F32),
                                ALU.subtract).then_inc(s_blo, 1)
                dve.wait_ge(s_bhi, 3 * n + 3)
                V.tensor_tensor(xT_lo[slot], xT_raw[:, slot], xT_hi[slot].bitcast(F32), ALU.subtract).then_inc(s_blo, 1)

            def gates(n, before=None):
                dve.wait_ge(s_lg, n + 1)
                V.tensor_copy(lgs[:, :], p_lg[:, E0 * R0:NLG]).then_inc(s_gate, 1)
                wait_alone(dve, s_tick_dve, (s_gate, 11 * n + 1))
                V.max(v8[:, :], lgs[:, :]).then_inc(s_gate, 1)
                dve.wait_ge(s_gate, 11 * n + 2)
                V.tensor_tensor(diff[:, :], v8[:, 1:2], v8[:, 0:1], ALU.subtract).then_inc(s_gate, 1)
                V.max_index(i8[:, :], v8[:, :], lgs[:, :]).then_inc(s_gate, 1)
                dve.wait_ge(s_gate, 11 * n + 4)
                V.tensor_copy(i8f[:, :], i8[:, :]).then_inc(s_gate, 1)
                if before is not None:
                    finish(n - 1, before)
                dve.wait_ge(s_exp, n + 1)
                V.tensor_scalar(den[:, :], ex[:, :], 1.0, None, ALU.add).then_inc(s_gate, 1)
                dve.wait_ge(s_gate, 11 * n + 6)
                V.reciprocal(pr[:, 0:1], den[:, :]).then_inc(s_gate, 1)
                dve.wait_ge(s_gate, 11 * n + 7)
                V.tensor_tensor(pr[:, 1:2], pr[:, 0:1], ex[:, :], ALU.mult).then_inc(s_gate, 1)
                dve.wait_ge(s_gate, 11 * n + 8)
                V.tensor_scalar(wa[:, :], iota8[:, :], i8f[:, 0:1], pr[:, 0:1], ALU.is_equal, ALU.mult).then_inc(s_gate, 1)
                V.tensor_scalar(wb[:, :], iota8[:, :], i8f[:, 1:2], pr[:, 1:2], ALU.is_equal, ALU.mult).then_inc(s_gate, 1)
                dve.wait_ge(s_gate, 11 * n + 10)
                V.tensor_tensor(wf[:, :], wa[:, :], wb[:, :], ALU.add).then_inc(s_gate, 1)
                dve.wait_ge(s_gate, 11 * n + 11)
                V.scalar_tensor_tensor(out=low[:, :].rearrange("p (e r) -> p e r", e=E0),
                                       in0=p_lg[:, 0:E0 * R0].rearrange("p (e r) -> p e r", e=E0), scalar=2.0,
                                       in1=wf[:, :].unsqueeze(2).to_broadcast([128, E0, R0]),
                                       op0=ALU.mult, op1=ALU.mult).then_inc(s_low, 1)

            def finish(n, slot):
                dve.wait_ge(s_r, n + 1)
                dve.wait_ge(s_xb, n + 1)
                if not isinstance(n, int) or n > 0:
                    dve.wait_ge(s_st, 16 * n)
                V.tensor_tensor(x1, p_r[slot][:, :], xb[:, slot], ALU.add).then_inc(s_x1, 1)

            def y_parts(n):
                dve.wait_ge(s_yhi, n + 1)
                V.tensor_tensor(yT_lo, p_yT[:, :, :], yT_hi.bitcast(F32), ALU.subtract).then_inc(s_ylo, 1)

            def low_parts(n):
                dve.wait_ge(s_lthi, n + 1)
                V.tensor_tensor(lowT_lo[:, :], p_t[:, 0:128], lowT_hi[:, :].bitcast(F32), ALU.subtract).then_inc(s_ltlo, 1)

            def x1T_parts(n):
                dve.wait_ge(s_xthi, n + 1)
                V.tensor_tensor(x1T[:, 1], p_x[:, :, :], x1T[:, 0].bitcast(F32), ALU.subtract).then_inc(s_xtlo, 1)

            def step(n, slot, where):
                y_parts(n)
                if where == "first":
                    dve.wait_ge(s_whi, 2)
                    V.tensor_tensor(base_lo, base_raw[:, :, :], base_hi.bitcast(F32), ALU.subtract).then_inc(s_wlo, 1)
                    dve.wait_ge(s_whi, 3)
                    V.tensor_tensor(lb_lo[:, :], lb_raw[:, :], lb_hi[:, :].bitcast(F32), ALU.subtract).then_inc(s_wlo, 1)
                if where != "first":
                    low_parts(n - 1)
                if where not in ("first", "second"):
                    x1T_parts(n - 2)
                if where not in ("closing", "last"):
                    split_adapter(n + 2, slot)
                gates(n, None if where == "first" else 1 - slot)
                if where == "first":
                    masks()
                if where == "second":
                    tables()

            dve.wait_ge(s_ang, 48)
            link(V.tensor_copy(seq_f[:, :], seq_i[:, :]))
            link(V.tensor_scalar(pos[:, :], seq_f[:, :], tok[:, 0:1], None, ALU.add))
            link(V.tensor_tensor(ang, pos[:, :].unsqueeze(2).to_broadcast([128, B, 64]),
                                 invf[:, :].unsqueeze(1).to_broadcast([128, B, 64]), ALU.mult))
            angles(0)
            V.engine_nop().then_inc(s_red, 1)
            split_adapter(0, 0)
            dve.wait_ge(s_whi, 1)
            V.tensor_tensor(lg_lo[:, :, :], lg_raw[:, :, :], lg_hi[:, :, :].bitcast(F32), ALU.subtract).then_inc(s_wlo, 1)
            angles(1)
            V.engine_nop().then_inc(s_red, 1)
            split_adapter(1, 1)
            dve.wait_ge(s_const, 5 * 16)
            schedule(dve, step)
            low_parts(B - 1)
            x1T_parts(B - 2)
            finish(B - 1, 1)
            x1T_parts(B - 1)

        @block.scalar
        def _(act):
            A = nc.scalar

            def split_adapter(n, slot):
                act.wait_ge(s_w[slot], (n // 2) * 32 + 32)
                A.activation(w_hi[slot][:, 0:HK2, :], w_raw[slot][:, 0:HK2], ACT.Copy).then_inc(s_bhi, 1)
                A.activation(w_hi[slot][:, HK2:KT, :], w_raw[slot][:, HK2:KT], ACT.Copy).then_inc(s_bhi, 1)
                A.activation(xT_hi[slot], xT_raw[:, slot], ACT.Copy).then_inc(s_bhi, 1)

            def y_copy(n):
                act.wait_ge(s_y, n + 1)
                if not isinstance(n, int) or n > 0:
                    act.wait_ge(s_yT, n)
                A.activation(y[:, :], p_y[:, :], ACT.Copy).then_inc(s_yc, 1)

            def y_hi(n):
                act.wait_ge(s_yT, n + 1)
                A.activation(yT_hi, p_yT[:, :, :], ACT.Copy).then_inc(s_yhi, 1)

            def low_parts(n):
                act.wait_ge(s_lt, n + 1)
                A.activation(lowT_hi[:, :], p_t[:, 0:128], ACT.Copy).then_inc(s_lthi, 1)

            def x1T_hi(n):
                act.wait_ge(s_xt, n + 1)
                if not isinstance(n, int) or n > 0:
                    act.wait_ge(s_stT, 16 * n)
                A.activation(x1T[:, 0], p_x[:, :, :], ACT.Copy).then_inc(s_xthi, 1)

            def store_x1(n):
                act.wait_ge(s_x1, n + 1)
                act.dma_start(dram["x1"][bass.ds(n, 1)].rearrange("o p n -> (o p) n"), x1).then_inc(s_st, 16)

            def store_x1T(n):
                act.wait_ge(s_xtlo, n + 1)
                act.dma_start(dram["x1T"][bass.ds(n, 1)].rearrange("o p n -> (o p) n"),
                              x1T.bitcast(F32).rearrange("p a k n -> p (a k n)")).then_inc(s_stT, 16)

            def step(n, slot, where):
                y_hi(n)
                if where == "first":
                    act.wait_ge(s_base, 32)
                    A.activation(base_hi, base_raw[:, :, :], ACT.Copy).then_inc(s_whi, 1)
                    A.activation(lb_hi[:, :], lb_raw[:, :], ACT.Copy).then_inc(s_whi, 1)
                    act.wait_ge(s_red, 2)
                    A.activation(trig[1], red[1], ACT.Sin).then_inc(s_trig, 1)
                if where != "first":
                    low_parts(n - 1)
                if where not in ("first", "second"):
                    x1T_hi(n - 2)
                if where not in ("closing", "last"):
                    split_adapter(n + 2, slot)
                if where != "last":
                    y_copy(n + 1)
                if where not in ("first", "second"):
                    store_x1T(n - 2)
                act.wait_ge(s_gate, 11 * n + 3)
                A.activation(ex[:, :], diff[:, :], ACT.Exp).then_inc(s_exp, 1)
                if where != "first":
                    store_x1(n - 1)

            split_adapter(0, 0)
            act.wait_ge(s_low_w, 16)
            A.activation(lg_hi[:, :, :], lg_raw[:, :, :], ACT.Copy).then_inc(s_whi, 1)
            act.wait_ge(s_red, 1)
            A.activation(trig[0], red[0], ACT.Sin).then_inc(s_trig, 1)
            split_adapter(1, 1)
            y_copy(0)
            schedule(act, step)
            low_parts(B - 1)
            x1T_hi(B - 2)
            store_x1T(B - 2)
            store_x1(B - 1)
            x1T_hi(B - 1)
            store_x1T(B - 1)

        @block.tensor
        def _(pe):
            PE = nc.tensor

            def product(out, pairs, start=True, stop=True):
                terms = [(a[i], w[j]) for i, j in ((0, 0), (0, 1), (1, 0)) for a, w in pairs]
                for m, (a, w) in enumerate(terms):
                    mm = PE.matmul(out, a, w, start=start and m == 0, stop=stop and m == len(terms) - 1)
                return mm

            def adapter(n, slot):
                pe.wait_ge(s_blo, 2 * n + 2)
                pe.wait_ge(s_bpl, n + 1)
                product(p_y[:, :], [((xT_hi[slot][:, k], xT_lo[slot][:, k]), (w_hi[slot][:, k], w_lo[slot][:, k]))
                                    for k in range(KT)]).then_inc(s_y, 1)

            def low_turn(n):
                pe.wait_ge(s_low, n + 1)
                PE.transpose(p_t[:, 0:128], low[:, :], ident[:, :]).then_inc(s_lt, 1)

            def low_out(n, slot):
                pe.wait_ge(s_ltlo, n + 1)
                product(p_r[slot][:, :], [((lowT_hi[:, :], lowT_lo[:, :]), (lb_hi[:, :], lb_lo[:, :]))], start=False).then_inc(s_r, 1)

            def x1_turn(n):
                pe.wait_ge(s_x1, n + 1)
                for k in range(KT):
                    mm = PE.transpose(p_x[:, k, :], x1[:, 128 * k:128 * k + 128], ident[:, :])
                mm.then_inc(s_xt, 1)

            def step(n, slot, where):
                pe.wait_ge(s_yc, n + 1)
                for k in range(KT):
                    mm = PE.transpose(p_yT[:, k, :], y[:, 128 * k:128 * k + 128], ident[:, :])
                mm.then_inc(s_yT, 1)
                if where != "first":
                    low_turn(n - 1)
                if where != "last":
                    adapter(n + 1, 1 - slot)
                if where == "first":
                    pe.wait_ge(s_wlo, 1)
                pe.wait_ge(s_ylo, n + 1)
                product(p_lg[:, 0:NLG], [((yT_hi[:, k, :], yT_lo[:, k, :]), (lg_hi[:, k, :], lg_lo[:, k, :]))
                                         for k in range(KT)]).then_inc(s_lg, 1)
                if where == "first":
                    pe.wait_ge(s_wlo, 3)
                else:
                    low_out(n - 1, 1 - slot)
                product(p_r[slot][:, :], [((yT_hi[:, k, :], yT_lo[:, k, :]), (base_hi[:, k, :], base_lo[:, k, :]))
                                          for k in range(KT)], stop=False).then_inc(s_base_mm, 1)
                if where != "first":
                    x1_turn(n - 1)

            adapter(0, 0)
            pe.wait_ge(s_const, 80)
            schedule(pe, step)
            low_turn(B - 1)
            low_out(B - 1, 1)
            x1_turn(B - 1)


def attention(nc, t, dram, keep):
    with ExitStack() as ctx:
        def sb(name, shape, dt=F32):
            return ctx.enter_context(nc.sbuf_tensor(name, shape, dt))

        def ps(name, shape, dt=F32):
            return ctx.enter_context(nc.psum_tensor(name, shape, dt))

        def sem(name):
            return ctx.enter_context(nc.semaphore(name))

        ident, rope, yacc = keep["ident"], keep["rope"], keep["yacc"]
        mask = sb("mask", [128, 2, NKEY], BF16)
        w_raw, w_hi, w_lo = keep["wg_raw"], keep["wg_hi"], keep["wg_lo"]
        xT, kv = keep["xT"], keep["kv"]
        kT_hi = sb("kT_hi", [128, NKEY], F32R)
        kT_lo = sb("kT_lo", [128, NKEY], F32R)
        v_hi = sb("v_hi", [128, 2, KTILES, HD], F32R)
        v_lo = sb("v_lo", [128, 2, KTILES, HD], F32R)
        qT_hi = sb("qT_hi", [128, GQ], F32R)
        qT_lo = sb("qT_lo", [128, GQ], F32R)
        rot_a = sb("rot_a", [128, REP, HD])
        rot_b = sb("rot_b", [128, REP, HD])
        krot_a = sb("krot_a", [128, HD])
        krot_b = sb("krot_b", [128, HD])
        junk = sb("junk", [128, REP + 1, HD])
        ss = sb("ss", [128, REP + 1])
        rs_a = sb("rs_a", [128, REP + 1])
        rs_b = sb("rs_b", [128, REP + 1])
        rstd = sb("rstd", [128, 2, REP + 1])
        c_mul = sb("c_mul", [128, REP + 1])
        c_add = sb("c_add", [128, REP + 1])
        c_pow = sb("c_pow", [128, REP + 1])
        P = sb("P", [128, REP, NKEY])
        mx = sb("mx", [128, REP])
        nb = sb("nb", [128, REP])
        den = sb("den", [128, REP])
        rden = sb("rden", [128, 2, REP])
        bc = sb("bc", [128, S, REP])
        pT_hi = sb("pT_hi", [128, NPT, REP * S], F32R)
        pT_lo = sb("pT_lo", [128, NPT, REP * S], F32R)
        oT = sb("oT", [128, REP * S])
        oT_hi = sb("oT_hi", [128, REP * S], F32R)
        oT_lo = sb("oT_lo", [128, REP * S], F32R)

        bank = [ps(f"bank{n}", [128, 1024]) for n in range(2)]
        b_kv = ps("b_kv", [128, 512])
        b_q = ps("b_q", [128, 512])
        b_y = ps("b_y", [128, 512])
        b_o = ps("b_o", [128, 512])

        s_tick_sp, s_tick_dve, s_tick_pool = sem("s_tick_sp"), sem("s_tick_dve"), sem("s_tick_pool")
        s_c = sem("s_c")
        s_wraw, s_wh, s_ws = keep["s_wraw"], keep["s_wh"], keep["s_ws"]
        s_xT, s_kv = keep["s_xT"], keep["s_kv"]
        s_mk = [sem("s_mk0"), sem("s_mk1")]
        s_rw = sem("s_rw")
        s_bc = sem("s_bc")
        s_kvp = sem("s_kvp")
        s_qp = sem("s_qp")
        s_sc = sem("s_sc")
        s_y = sem("s_y")
        s_pt = sem("s_pt")
        s_pv = sem("s_pv")
        s_kcT = sem("s_kcT")
        s_qkT = sem("s_qkT")
        s_sq = sem("s_sq")
        s_vh = sem("s_vh")
        s_ex = sem("s_ex")
        s_pth = sem("s_pth")
        s_kch = sem("s_kch")
        s_qkh = sem("s_qkh")
        s_oh = sem("s_oh")
        s_mx = sem("s_mx")
        s_nb = sem("s_nb")
        s_rq = sem("s_rq")
        s_rk = sem("s_rk")
        s_kr = sem("s_kr")
        s_rd = sem("s_rd")
        s_ya = sem("s_ya")
        s_ptl = sem("s_ptl")
        s_qkl = sem("s_qkl")
        s_ot = sem("s_ot")
        s_rs = sem("s_rs")
        s_qa = sem("s_qa")
        s_vc = sem("s_vc")
        s_vs = sem("s_vs")
        s_ol = sem("s_ol")

        block = ctx.enter_context(nc.Block())
        LAST = UNITS - 1

        @block.sync
        def _(sp):
            def load_mask(u, par):
                sp.dma_start(mask[:, par], dram["mask"][bass.ds(u % B, 1)].to_broadcast([128, NKEY])).then_inc(s_mk[par], 16)

            def load_w(n, par):
                sp.dma_start(w_raw[:, par], t["wg"][bass.ds(n, 1)].rearrange("o p n -> (o p) n")).then_inc(s_wraw[par], 16)

            def rden_out(u, par):
                wait_alone(sp, s_tick_sp, (s_rd, u + 1))
                sp.dma_start(dram["rden"], rden[:, par]).then_inc(s_rw, 16)

            def rden_in(u, skip=False):
                wait_alone(sp, s_tick_sp, (s_rw, 16 * (u + 1)))
                if not skip:
                    wait_alone(sp, s_tick_sp, (s_ot, u))
                sp.dma_start(bc[:, :, :].rearrange("p s h -> p (s h)"),
                             dram["rden"].rearrange("(o s) h -> o (s h)", o=1).to_broadcast([128, S * REP])).then_inc(s_bc, 16)

            load_mask(0, 0)
            load_mask(1, 1)
            load_kv(nc, sp, t, keep, 1, 1, page_numbers(nc, keep, 1), NPP // 2, NPP)
            load_w(B, 0)
            load_w(B + 1, 1)
            sp.wait_ge(keep["s_stT"], 16 * B)

            def unit(u, par, n, more=True, weights=True):
                if more:
                    wait_alone(sp, s_tick_sp, (s_qp, u + 1))
                    load_x1T(sp, dram, keep, u + 2, par)
                    wait_alone(sp, s_tick_sp, (s_kcT, u + 1), (s_vs, u + 1))
                    numbers = page_numbers(nc, keep, u + 2)
                    load_kv(nc, sp, t, keep, u + 2, par, numbers, 0, NPP // 2)
                rden_out(u, par)
                if more:
                    load_mask(u + 2, par)
                    load_kv(nc, sp, t, keep, u + 2, par, numbers, NPP // 2, 3 * NPP // 4)
                rden_in(u, n == "first")
                if more:
                    load_kv(nc, sp, t, keep, u + 2, par, numbers, 3 * NPP // 4, NPP)
                if weights:
                    wait_alone(sp, s_tick_sp, (s_ws, u + B + 1))
                    load_w(u + B + 2, par)

            unit(0, 0, "first")
            with sp.Fori(0, (UNITS - 4) // 2) as i:
                unit(2 * i + 1, 1, "body")
                unit(2 * i + 2, 0, "body")
            unit(LAST - 2, 1, "body", weights=False)
            unit(LAST - 1, 0, "body", more=False, weights=False)
            unit(LAST, 1, "last", more=False, weights=False)

        @block.tensor
        def _(pe):
            PE = nc.tensor

            def wait_group(u, chunks):
                pe.wait_ge(s_ws, (u // B) * B + chunks)

            terms3 = [(a, w, k) for a, w in ((0, w_hi), (0, w_lo), (1, w_hi)) for k in range(KT)]

            def project_kv(u, par):
                at = ((u // B) % 2) * WCOLS
                pe.wait_ge(s_xT[par], (u // 2) * 16 + 16)
                wait_group(u, 5)
                for m, (a, w, k) in enumerate(terms3):
                    mm = PE.matmul(b_kv[:, 0:2 * HD], xT[:, par, a, k], w[:, bass.ds(at + WQ + 2 * HD * k, 2 * HD)],
                                   start=(m == 0), stop=(m == len(terms3) - 1))
                mm.then_inc(s_kvp, 1)

            def project_q(u, par):
                at = ((u // B) % 2) * WCOLS
                for m, (a, w, k) in enumerate(terms3):
                    mm = PE.matmul(b_q[:, :], xT[:, par, a, k], w[:, bass.ds(at + GQ * k, GQ)],
                                   start=(m == 0), stop=(m == len(terms3) - 1))
                mm.then_inc(s_qp, 1)

            def turn(u, par):
                pe.wait_ge(s_kv[par], (u // 2) * 16 * NPP + 16 * NPP)
                if not isinstance(u, int) or u > 0:
                    pe.wait_ge(s_ya, u)
                for k in range(LT):
                    mm = PE.transpose(b_y[:, 128 * k:128 * k + 128], kv[:, par, k, 0], ident[:, :])
                mm.then_inc(s_kcT, 1)
                pe.wait_ge(s_kr, 2 * u + 2)
                PE.transpose(b_kv[:, 0:128], krot_a[:, :], ident[:, :])
                pe.wait_ge(s_qa, u + 1)
                for h in range(REP):
                    mm = PE.transpose(b_q[:, 128 * h:128 * h + 128], rot_a[:, h], ident[:, :])
                mm.then_inc(s_qkT, 1)

            def scores(u, heads):
                for h in heads:
                    if h >= 2:
                        pe.wait_ge(s_mx, 4 * u + h - 1)
                    out = bank[h % 2]
                    q = slice(128 * h, 128 * h + 128)
                    terms = ((qT_hi, kT_hi), (qT_hi, kT_lo), (qT_lo, kT_hi))
                    for m, (a, k) in enumerate(terms):
                        for half in range(2):
                            mm = PE.matmul(out[:, 512 * half:512 * half + NKEY // 2], a[:, q],
                                           k[:, NKEY // 2 * half:NKEY // 2 * (half + 1)], start=(m == 0), stop=(m == 2))
                    mm.then_inc(s_sc, 1)

            def output(u):
                at = ((u // B) % 2) * WCOLS + WQ + WKV
                pe.wait_ge(s_ol, u + 1)
                wait_group(u, B)
                terms = [(o, w, h) for o, w in ((oT_hi, w_hi), (oT_hi, w_lo), (oT_lo, w_hi)) for h in range(REP)]
                for m, (o, w, h) in enumerate(terms):
                    mm = PE.matmul(b_y[:, :], o[:, 128 * h:128 * h + 128], w[:, bass.ds(at + D * h, D)],
                                   start=(m == 0), stop=(m == len(terms) - 1))
                mm.then_inc(s_y, 1)

            def p_turn(u, k):
                for h in range(REP):
                    mm = PE.transpose(bank[(k % 4) // 2][:, 512 * (k % 2) + 128 * h:512 * (k % 2) + 128 * h + 128],
                                      P[:, h, 128 * k:128 * k + 128], ident[:, :])
                mm.then_inc(s_pt, 1)

            def pv(u, par, k):
                pe.wait_ge(s_ptl, 5 * u + k + 1)
                for m, (v, p) in enumerate(((v_hi, pT_hi), (v_lo, pT_hi), (v_hi, pT_lo))):
                    mm = PE.matmul(b_o[:, :], v[:, par, k], p[:, k % NPT], start=(k == 0 and m == 0),
                                   stop=(k == KTILES - 1 and m == 2))
                mm.then_inc(s_pv, 1)

            def unit(u, par, n):
                pe.wait_ge(s_qkl, 3 * u + 3)
                scores(u, (0, 1))
                if n != "last":
                    project_kv(u + 1, 1 - par)
                scores(u, (2, 3))
                if n != "last":
                    project_q(u + 1, 1 - par)
                pe.wait_ge(s_ex, 4 * u + 4)
                p_turn(u, 0)
                p_turn(u, 1)
                if n != "first":
                    output(u - 1)
                p_turn(u, 2)
                p_turn(u, 3)
                pe.wait_ge(s_vs, u + 1)
                pv(u, par, 0)
                p_turn(u, 4)
                if n != "last":
                    turn(u + 1, 1 - par)
                for k in range(1, KTILES):
                    pv(u, par, k)

            project_kv(0, 0)
            project_q(0, 0)
            turn(0, 0)
            unit(0, 0, "first")
            with pe.Fori(0, (UNITS - 2) // 2) as i:
                unit(2 * i + 1, 1, "body")
                unit(2 * i + 2, 0, "body")
            unit(LAST, 1, "last")
            output(LAST)

        @block.scalar
        def _(act):
            A = nc.scalar

            def own(u, par):
                act.wait_ge(s_kvp, u + 1)
                A.activation(v_hi[:, par, LT], b_kv[:, HD:2 * HD], ACT.Copy).then_inc(s_vh, 1)
                A.activation(junk[:, REP], b_kv[:, 0:HD], ACT.Square, accum_out=ss[:, REP:REP + 1]).then_inc(s_sq, 1)
                act.wait_ge(s_qp, u + 1)
                for h in range(REP):
                    A.activation(junk[:, h], b_q[:, 128 * h:128 * h + 128], ACT.Square, accum_out=ss[:, h:h + 1]).then_inc(s_sq, 1)

            def turned(u, par):
                act.wait_ge(s_kcT, u + 1)
                A.activation(kT_hi[:, 0:L], b_y[:, :], ACT.Copy).then_inc(s_kch, 1)
                act.wait_ge(s_qkT, u + 1)
                A.activation(kT_hi[:, L:NKEY], b_kv[:, 0:128], ACT.Copy).then_inc(s_qkh, 1)
                A.activation(qT_hi[:, :], b_q[:, :], ACT.Copy).then_inc(s_qkh, 1)

            def p_hi(u, k):
                act.wait_ge(s_pt, 5 * u + k + 1)
                if k >= NPT:
                    act.wait_ge(s_pv, 5 * u + k - NPT + 1)
                A.activation(pT_hi[:, k % NPT], bank[(k % 4) // 2][:, 512 * (k % 2):512 * (k % 2) + 512], ACT.Copy).then_inc(s_pth, 1)

            def out_hi(u):
                act.wait_ge(s_ot, u + 1)
                A.activation(oT_hi[:, :], oT[:, :], ACT.Copy).then_inc(s_oh, 1)

            def unit(u, par, n):
                for h in range(REP):
                    act.wait_ge(s_nb, 4 * u + h + 1)
                    A.activation(P[:, h], P[:, h], ACT.Exp, bias=nb[:, h:h + 1], scale=rstd[:, par, h:h + 1],
                                 accum_out=den[:, h:h + 1]).then_inc(s_ex, 1)
                    if h == 1 and n != "first":
                        out_hi(u - 1)
                if n != "last":
                    own(u + 1, 1 - par)
                for k in range(KTILES):
                    p_hi(u, k)
                if n != "last":
                    turned(u + 1, 1 - par)

            own(0, 0)
            turned(0, 0)
            unit(0, 0, "first")
            with act.Fori(0, (UNITS - 2) // 2) as i:
                unit(2 * i + 1, 1, "body")
                unit(2 * i + 2, 0, "body")
            unit(LAST, 1, "last")
            out_hi(LAST)

        @block.vector
        def _(dve):
            V = nc.vector
            def tab(at, n, j, lo, hi, reps):
                a = rope[:, bass.ds(at, 1), n, j, lo:hi]
                return a.to_broadcast([128, reps, hi - lo]) if reps > 1 else a

            def rotate_q(u):
                at = u % B
                dve.wait_ge(s_sq, 5 * u + 5)
                q = b_q[:, :].rearrange("p (h d) -> p h d", h=REP)

                V.tensor_tensor(rot_a[:, :, :], q, tab(at, 0, 0, 0, HD, REP), ALU.mult).then_inc(s_rq, 1)
                V.tensor_tensor(rot_b[:, :, 0:64], q[:, :, 64:128], tab(at, 0, 1, 0, 64, REP), ALU.mult).then_inc(s_rq, 1)
                V.tensor_tensor(rot_b[:, :, 64:128], q[:, :, 0:64], tab(at, 0, 1, 64, 128, REP), ALU.mult).then_inc(s_rq, 1)

            def rotate_k(u, par):
                at = u % B
                dve.wait_ge(s_rs, 3 * u + 3)
                rk = rstd[:, par, REP:REP + 1]
                k1 = b_kv[:, 0:HD].unsqueeze(1)
                V.scalar_tensor_tensor(out=krot_a[:, :].unsqueeze(1), in0=k1, scalar=rk, in1=tab(at, 1, 0, 0, HD, 1),
                                       op0=ALU.mult, op1=ALU.mult).then_inc(s_rk, 1)
                V.scalar_tensor_tensor(out=krot_b[:, 0:64].unsqueeze(1), in0=k1[:, :, 64:128], scalar=rk, in1=tab(at, 1, 1, 0, 64, 1),
                                       op0=ALU.mult, op1=ALU.mult).then_inc(s_rk, 1)
                V.scalar_tensor_tensor(out=krot_b[:, 64:128].unsqueeze(1), in0=k1[:, :, 0:64], scalar=rk, in1=tab(at, 1, 1, 64, 128, 1),
                                       op0=ALU.mult, op1=ALU.mult).then_inc(s_rk, 1)

            def finish_k(u, par):
                dve.wait_ge(s_vh, u + 1)
                V.tensor_tensor(v_lo[:, par, LT], b_kv[:, HD:2 * HD], v_hi[:, par, LT].bitcast(F32), ALU.subtract).then_inc(s_kr, 1)
                dve.wait_ge(s_rk, 3 * u + 3)
                V.tensor_tensor(krot_a[:, :], krot_a[:, :], krot_b[:, :], ALU.add).then_inc(s_kr, 1)

            def turned(u, par):
                dve.wait_ge(s_kch, u + 1)
                V.tensor_tensor(kT_lo[:, 0:L], b_y[:, :], kT_hi[:, 0:L].bitcast(F32), ALU.subtract).then_inc(s_qkl, 1)
                dve.wait_ge(s_qkh, 2 * u + 2)
                V.tensor_tensor(kT_lo[:, L:NKEY], b_kv[:, 0:128], kT_hi[:, L:NKEY].bitcast(F32), ALU.subtract).then_inc(s_qkl, 1)
                V.tensor_tensor(qT_lo[:, :], b_q[:, :], qT_hi[:, :].bitcast(F32), ALU.subtract).then_inc(s_qkl, 1)

            def p_lo(u, k):
                dve.wait_ge(s_pth, 5 * u + k + 1)
                V.tensor_tensor(pT_lo[:, k % NPT], bank[(k % 4) // 2][:, 512 * (k % 2):512 * (k % 2) + 512],
                                pT_hi[:, k % NPT].bitcast(F32), ALU.subtract).then_inc(s_ptl, 1)

            def add_y(u):
                dve.wait_ge(s_y, u + 1)
                dve.wait_ge(s_ya, u + 1)
                ya = yacc[:, bass.ds(u % B, 1), :].rearrange("p o n -> p (o n)")
                V.tensor_tensor(ya, b_y[:, :], ya, ALU.add).then_inc(s_ya, 1)

            def halves(a):
                return a.rearrange("p (t n) -> p t n", t=2)

            def unit(u, par, n):
                dve.wait_ge(s_mk[par], (u // 2) * 16 + 16)

                def biggest(h):
                    wait_alone(dve, s_tick_dve, (s_sc, 4 * u + h + 1))
                    V.tensor_tensor_reduce(out=halves(P[:, h]), in0=bank[h % 2][:, :].rearrange("p (t n) -> p t n", t=2)[:, :, 0:NKEY // 2],
                                           in1=halves(mask[:, par]), scale=1.0, scalar=-3e38,
                                           op0=ALU.add, op1=ALU.max, accum_out=mx[:, h:h + 1]).then_inc(s_mx, 1)

                def bias(h):
                    dve.wait_ge(s_mx, 4 * u + h + 1)
                    V.tensor_scalar(nb[:, h:h + 1], mx[:, h:h + 1], -1.0, rstd[:, par, h:h + 1], ALU.mult, ALU.mult).then_inc(s_nb, 1)

                biggest(0)
                biggest(1)
                bias(0)
                bias(1)
                if n != "first":
                    out_norm(u - 1)
                biggest(2)
                bias(2)
                biggest(3)
                bias(3)
                dve.wait_ge(s_ex, 4 * u + 4)
                V.reciprocal(rden[:, par], den[:, :]).then_inc(s_rd, 1)
                if n != "last":
                    rotate_q(u + 1)
                p_lo(u, 0)
                if n != "last":
                    rotate_k(u + 1, 1 - par)
                    finish_k(u + 1, 1 - par)
                if n != "first":
                    add_y(u - 1)
                for k in range(1, KTILES):
                    p_lo(u, k)
                if n != "last":
                    turned(u + 1, 1 - par)

            def out_norm(u):
                dve.wait_ge(s_pv, 5 * u + 5)
                dve.wait_ge(s_bc, 16 * u + 16)
                V.tensor_tensor(oT[:, :].rearrange("p (h s) -> p h s", h=REP), b_o[:, :].rearrange("p (h s) -> p h s", h=REP),
                                bc[:, :, :].rearrange("p s h -> p h s"), ALU.mult).then_inc(s_ot, 1)

            rotate_q(0)
            rotate_k(0, 0)
            finish_k(0, 0)
            turned(0, 0)
            unit(0, 0, "first")
            with dve.Fori(0, (UNITS - 2) // 2) as i:
                unit(2 * i + 1, 1, "body")
                unit(2 * i + 2, 0, "body")
            unit(LAST, 1, "last")
            out_norm(LAST)
            add_y(LAST)

        @block.gpsimd
        def _(pool):
            G = nc.gpsimd
            G.memset(yacc[:, :, :], 0.0).then_inc(s_ya, 1)
            G.memset(c_mul[:, 0:REP], 1.0).then_inc(s_c, 1)
            G.memset(c_mul[:, REP:REP + 1], 1.0 / HD).then_inc(s_c, 1)
            G.memset(c_add[:, 0:REP], HD * EPS).then_inc(s_c, 1)
            G.memset(c_add[:, REP:REP + 1], EPS).then_inc(s_c, 1)
            G.memset(c_pow[:, :], -0.5).then_inc(s_c, 1)

            def chunk(n, par, group_par, added=None):
                at = group_par * WCOLS + (n % B) * CH
                wait_alone(pool, s_tick_pool, *([(s_ya, added)] if added is not None else []), (s_wraw[par], (n // 2) * 16 + 16))
                G.tensor_copy(w_hi[:, bass.ds(at, CH)], w_raw[:, par]).then_inc(s_wh, 1)
                wait_alone(pool, s_tick_pool, (s_wh, n + 1))
                G.tensor_tensor(w_lo[:, bass.ds(at, CH)], w_raw[:, par], w_hi[:, bass.ds(at, CH)].bitcast(F32), ALU.subtract).then_inc(s_ws, 1)

            def norms(u, par):
                pool.wait_ge(s_sq, 5 * u + 5)
                G.tensor_tensor(rs_a[:, :], ss[:, :], c_mul[:, :], ALU.mult).then_inc(s_rs, 1)
                pool.wait_ge(s_rs, 3 * u + 1)
                G.tensor_tensor(rs_b[:, :], rs_a[:, :], c_add[:, :], ALU.add).then_inc(s_rs, 1)
                pool.wait_ge(s_rs, 3 * u + 2)
                G.tensor_tensor(rstd[:, par], rs_b[:, :], c_pow[:, :], ALU.pow).then_inc(s_rs, 1)

            def add_q(u):
                pool.wait_ge(s_rq, 3 * u + 3)
                G.tensor_tensor(rot_a[:, :, :], rot_a[:, :, :], rot_b[:, :, :], ALU.add).then_inc(s_qa, 1)

            def values(u, par):
                wait_alone(pool, s_tick_pool, (s_kv[par], (u // 2) * 16 * NPP + 16 * NPP))
                G.tensor_copy(v_hi[:, par, 0:LT], kv[:, par, :, 1]).then_inc(s_vc, 1)
                pool.wait_ge(s_vc, u + 1)
                G.tensor_tensor(v_lo[:, par, 0:LT], kv[:, par, :, 1], v_hi[:, par, 0:LT].bitcast(F32), ALU.subtract).then_inc(s_vs, 1)

            def out_lo(u):
                pool.wait_ge(s_oh, u + 1)
                G.tensor_tensor(oT_lo[:, :], oT[:, :], oT_hi[:, :].bitcast(F32), ALU.subtract).then_inc(s_ol, 1)

            def unit(u, par, n):
                if n != "first":
                    out_lo(u - 1)
                if n != "last":
                    norms(u + 1, 1 - par)
                    add_q(u + 1)
                    chunk(u + B, par, (u // B + 1) % 2, u if n == "body" else None)
                    values(u + 1, 1 - par)

            pool.wait_ge(s_c, 5)
            norms(0, 0)
            add_q(0)
            values(0, 0)
            unit(0, 0, "first")
            with pool.Fori(0, (UNITS - 2) // 2) as i:
                unit(2 * i + 1, 1, "body")
                unit(2 * i + 2, 0, "body")
            unit(LAST, 1, "last")
            out_lo(LAST)


def layer1_ffn(nc, t, dram, keep, out):
    with ExitStack() as ctx:
        def sb(name, shape, dt=F32):
            return ctx.enter_context(nc.sbuf_tensor(name, shape, dt))

        def ps(name, shape, dt=F32):
            return ctx.enter_context(nc.psum_tensor(name, shape, dt))

        def sem(name):
            return ctx.enter_context(nc.semaphore(name))

        ident, yacc = keep["ident"], keep["yacc"]

        def parts(at, n):
            return [w[:, at:at + KT * n].rearrange("p (k n) -> p k n", k=KT) for w in (keep["wg_hi"], keep["wg_lo"])]

        a_w, b_w = parts(0, NZ + RD), parts(KT * (NZ + RD), D)
        keysT = sb("keysT", [RD, NE])
        ybuf = sb("ybuf", [128, 2, D])
        yT = [sb("y1T_hi", [128, 2, KT, 128], F32R), sb("y1T_lo", [128, 2, KT, 128], F32R)]
        rq = sb("rq", [128, RD])
        rqT = sb("rqT", [RD, 128])
        sc = sb("sc", [128, NE])
        v1 = sb("v1", [128, 8])
        v2 = sb("v2", [128, 8])
        r1 = sb("r1", [128, NE])
        r2 = sb("r2", [128, NE])
        nm = sb("nm", [128, 1])
        e = sb("e", [128, NE])
        sel = sb("sel", [128, NE])
        es = sb("es", [128, NE])
        tot = sb("tot", [128, 1])
        rt = sb("rt", [128, 1])
        gate = sb("gate", [128, NE])
        zg = sb("zg", [128, NZ])
        zT = [sb("zT_hi", [128, KT, 128], F32R), sb("zT_lo", [128, KT, 128], F32R)]
        x1 = sb("x1_l1", [128, B, D])
        res = sb("res", [128, B, D])

        p_y = ps("p1_y", [128, KT, 128])
        p_z = [ps("p1_z0", [128, 2, 512]), ps("p1_z1", [128, 2, 512])]
        p_qs = ps("p1_qs", [128, 512])
        p_qT, p_s = p_qs[0:RD, 0:128], p_qs[:, 256:256 + NE]
        p_zT = ps("p1_zT", [128, KT, 128])
        p_o = ps("p1_o", [128, D])

        s_tick_sp, s_tick_dve, s_tick_pool = sem("f_tick_sp"), sem("f_tick_dve"), sem("f_tick_pool")
        s_in = sem("f_in")
        s_x1 = sem("f_x1")
        s_yb = sem("f_yb")
        s_yT = sem("f_yT")
        s_yhi, s_ylo = sem("f_yhi"), sem("f_ylo")
        s_z = sem("f_z")
        s_qs = sem("f_qs")
        s_qT = sem("f_qT")
        s_qTs = sem("f_qTs")
        s_s = sem("f_s")
        s_g = sem("f_g")
        s_e = sem("f_e")
        s_zg = sem("f_zg")
        s_zT = sem("f_zT")
        s_zhi, s_zlo = sem("f_zhi"), sem("f_zlo")
        s_o = sem("f_o")
        s_res = sem("f_res")
        s_out = sem("f_out")
        GS = 10
        HZ = NZ // 2
        PASSES = ((0, 0), (0, 1), (1, 0))

        block = ctx.enter_context(nc.Block())

        def schedule(eng, step):
            step(0, 0, "first")
            step(1, 1, "second")
            with eng.Fori(1, B // 2 - 1) as i:
                step(2 * i, 0, "body")
                step(2 * i + 1, 1, "body")
            step(B - 2, 0, "body")
            step(B - 1, 1, "last")

        @block.sync
        def _(sp):
            sp.dma_start(keysT[:, :], t["keysT"]).then_inc(s_in, 16)
            sp.wait_ge(keep["s_st"], 16 * B)
            sp.dma_start(x1[:, :, :], dram["x1"].rearrange("b p n -> p b n")).then_inc(s_x1, 16)
            with sp.Fori(0, B) as n:
                wait_alone(sp, s_tick_sp, (s_res, n + 1))
                sp.dma_start(out[bass.ds(n, 1)].rearrange("o p n -> (o p) n"),
                             res[:, bass.ds(n, 1), :].rearrange("p o n -> p (o n)")).then_inc(s_out, 16)
            sp.wait_ge(s_out, 16 * B)

        @block.gpsimd
        def _(pool):
            G = nc.gpsimd
            G.tensor_copy(ybuf[:, 1], yacc[:, 1]).then_inc(s_yb, 1)
            with pool.Fori(1, B // 2) as i:
                for slot in range(2):
                    wait_alone(pool, s_tick_pool, (s_yT, 2 * i + slot - 1))
                    G.tensor_copy(ybuf[:, slot], yacc[:, bass.ds(2 * i + slot, 1), :].rearrange("p o n -> p (o n)")).then_inc(s_yb, 1)

        @block.tensor
        def _(pe):
            PE = nc.tensor

            def turn_y(n, y):
                for k in range(KT):
                    mm = PE.transpose(p_y[:, k], y[:, 128 * k:128 * k + 128], ident[:, :])
                mm.then_inc(s_yT, 1)

            def inside(n, slot):
                pe.wait_ge(s_ylo, n + 1)
                terms = [(i, j, k) for i, j in PASSES for k in range(KT)]
                for m, (i, j, k) in enumerate(terms):
                    for half, width in enumerate((HZ, HZ + RD)):
                        mm = PE.matmul(p_z[slot][:, half, 0:width], yT[i][:, slot, k], a_w[j][:, k, HZ * half:HZ * half + width],
                                       start=(m == 0), stop=(m == len(terms) - 1))
                mm.then_inc(s_z, 1)

            def result(n):
                pe.wait_ge(s_zlo, n + 1)
                if not isinstance(n, int) or n > 0:
                    pe.wait_ge(s_res, n)
                terms = [(i, j, k) for i, j in PASSES for k in range(KT)]
                for m, (i, j, k) in enumerate(terms):
                    mm = PE.matmul(p_o[:, :], zT[i][:, k], b_w[j][:, k], start=(m == 0), stop=(m == len(terms) - 1))
                mm.then_inc(s_o, 1)

            def turn_z(n):
                pe.wait_ge(s_zg, 2 * n + 2)
                for k in range(KT):
                    mm = PE.transpose(p_zT[:, k], zg[:, 128 * k:128 * k + 128], ident[:, :])
                mm.then_inc(s_zT, 1)

            def step(n, slot, where):
                inside(n, slot)
                if where != "last":
                    pe.wait_ge(s_yb, n + 1)
                    turn_y(n + 1, ybuf[:, 1 - slot])
                if where not in ("first", "second"):
                    result(n - 2)
                pe.wait_ge(s_qs, n + 1)
                PE.transpose(p_qT, rq[:, :], ident[:, :]).then_inc(s_qT, 1)
                if where != "first":
                    turn_z(n - 1)
                pe.wait_ge(s_qTs, n + 1)
                PE.matmul(p_s, rqT[:, :], keysT[:, :], start=True, stop=True).then_inc(s_s, 1)

            turn_y(0, yacc[:, 0])
            pe.wait_ge(s_in, 16)
            schedule(pe, step)
            result(B - 2)
            turn_z(B - 1)
            result(B - 1)

        @block.scalar
        def _(act):
            A = nc.scalar

            def y_hi(n, slot):
                act.wait_ge(s_yT, n + 1)
                A.activation(yT[0][:, slot], p_y[:, :, :], ACT.Copy).then_inc(s_yhi, 1)

            def z_hi(n):
                act.wait_ge(s_zT, n + 1)
                A.activation(zT[0][:, :, :], p_zT[:, :, :], ACT.Copy).then_inc(s_zhi, 1)

            def step(n, slot, where):
                act.wait_ge(s_z, n + 1)
                A.activation(rq[:, :], p_z[slot][:, 1, HZ:HZ + RD], ACT.Copy).then_inc(s_qs, 1)
                if where != "last":
                    y_hi(n + 1, 1 - slot)
                if where != "first":
                    act.wait_ge(s_g, GS * n - GS + 1)
                act.wait_ge(s_qT, n + 1)
                A.activation(rqT[:, :], p_qT, ACT.Copy).then_inc(s_qTs, 1)
                if where != "first":
                    z_hi(n - 1)
                act.wait_ge(s_g, GS * n + 3)
                A.activation(e[:, :], sc[:, :], ACT.Exp, bias=nm[:, 0:1]).then_inc(s_e, 1)

            y_hi(0, 0)
            schedule(act, step)
            z_hi(B - 1)

        @block.vector
        def _(dve):
            V = nc.vector

            def y_lo(n, slot):
                dve.wait_ge(s_yhi, n + 1)
                V.tensor_tensor(yT[1][:, slot], p_y[:, :, :], yT[0][:, slot].bitcast(F32), ALU.subtract).then_inc(s_ylo, 1)

            def z_lo(n):
                dve.wait_ge(s_zhi, n + 1)
                V.tensor_tensor(zT[1][:, :, :], p_zT[:, :, :], zT[0][:, :, :].bitcast(F32), ALU.subtract).then_inc(s_zlo, 1)

            def gated(n, slot):
                wait_alone(dve, s_tick_dve, (s_g, GS * n + 1))
                V.max(v1[:, :], sc[:, :]).then_inc(s_g, 1)
                wait_alone(dve, s_tick_dve, (s_g, GS * n + 2))
                V.tensor_scalar(nm[:, :], v1[:, 0:1], -1.0, None, ALU.mult).then_inc(s_g, 1)
                V.match_replace(r1[:, :], v1[:, :], sc[:, :], -3e38).then_inc(s_g, 1)
                wait_alone(dve, s_tick_dve, (s_g, GS * n + 4))
                V.max(v2[:, :], r1[:, :]).then_inc(s_g, 1)
                wait_alone(dve, s_tick_dve, (s_g, GS * n + 5))
                V.match_replace(r2[:, :], v2[:, :], r1[:, :], -3e38).then_inc(s_g, 1)
                dve.wait_ge(s_g, GS * n + 6)
                V.tensor_tensor(sel[:, :], r2[:, :], sc[:, :], ALU.not_equal).then_inc(s_g, 1)
                wait_alone(dve, s_tick_dve, (s_g, GS * n + 7), (s_e, n + 1))
                V.tensor_tensor_reduce(out=es[:, :], in0=e[:, :], in1=sel[:, :], scale=1.0, scalar=0.0,
                                       op0=ALU.mult, op1=ALU.add, accum_out=tot[:, :]).then_inc(s_g, 1)
                wait_alone(dve, s_tick_dve, (s_g, GS * n + 8))
                V.reciprocal(rt[:, :], tot[:, :]).then_inc(s_g, 1)
                dve.wait_ge(s_g, GS * n + 9)
                V.tensor_scalar(gate[:, :], es[:, :], rt[:, 0:1], 2.0, ALU.mult, ALU.mult).then_inc(s_g, 1)
                dve.wait_ge(s_g, GS * n + 10)
                dve.wait_ge(s_z, n + 1)
                for half in range(2):
                    experts = slice(NE // 2 * half, NE // 2 * (half + 1))
                    V.tensor_tensor(zg[:, HZ * half:HZ * half + HZ].rearrange("p (e r) -> p e r", r=RANK),
                                    p_z[slot][:, half, 0:HZ].rearrange("p (e r) -> p e r", r=RANK),
                                    gate[:, experts].unsqueeze(2).to_broadcast([128, NE // 2, RANK]), ALU.mult).then_inc(s_zg, 1)

            def add_x1(n):
                dve.wait_ge(s_x1, 16)
                dve.wait_ge(s_o, n + 1)
                x = x1[:, bass.ds(n, 1), :].rearrange("p o n -> p (o n)")
                r = res[:, bass.ds(n, 1), :].rearrange("p o n -> p (o n)")
                V.tensor_tensor(r, p_o[:, :], x, ALU.add).then_inc(s_res, 1)

            def step(n, slot, where):
                if where != "last":
                    y_lo(n + 1, 1 - slot)
                if where not in ("first", "second"):
                    add_x1(n - 2)
                dve.wait_ge(s_s, n + 1)
                V.tensor_copy(sc[:, :], p_s).then_inc(s_g, 1)
                if where != "first":
                    z_lo(n - 1)
                gated(n, slot)

            y_lo(0, 0)
            schedule(dve, step)
            add_x1(B - 2)
            z_lo(B - 1)
            add_x1(B - 1)


def program(nc, t, out):
    dram = {
        "x1": nc.dram_tensor("x1_dram", [B, S, D], F32, kind="Internal").ap(),
        "x1T": nc.dram_tensor("x1T_dram", [B, 128, 2 * KT * 128], F32, kind="Internal").ap(),
        "mask": nc.dram_tensor("mask_dram", [B, NKEY], BF16, kind="Internal").ap(),
        "rden": nc.dram_tensor("rden_dram", [S, REP], F32, kind="Internal").ap(),
    }
    with ExitStack() as ctx:
        def sb(name, shape, dt=F32):
            return ctx.enter_context(nc.sbuf_tensor(name, shape, dt))

        def sem(name):
            return ctx.enter_context(nc.semaphore(name))

        raw = sb("raw", [128, KT, D])[:, :, :]
        keep = {
            "ident": sb("ident", [128, 128]),
            "rope": sb("rope", [128, B, 2, 2, HD]),
            "pages": sb("pages", [1, B * NPP], I32),
            "raw": raw,
            "kv": raw.rearrange("p k d -> p (k d)").rearrange("p (s t a d) -> p s t a d", s=2, t=LT, a=2),
            "xT": sb("xT", [128, 2, 2, KT, 128], F32R),
            "base_raw": sb("base_raw", [128, KT, D]),
            "wg_raw": sb("wg_raw", [128, 2, CH]),
            "wg_hi": sb("wg_hi", [128, 2 * WCOLS], F32R),
            "wg_lo": sb("wg_lo", [128, 2 * WCOLS], F32R),
            "yacc": sb("yacc", [128, B, D]),
            "s_st": sem("s_st"),
            "s_stT": sem("s_stT"),
            "s_xT": [sem("s_xT0"), sem("s_xT1")],
            "s_kv": [sem("s_kv0"), sem("s_kv1")],
            "s_wraw": [sem("s_wraw0"), sem("s_wraw1")],
            "s_wh": sem("s_wh"),
            "s_ws": sem("s_ws"),
        }
        layer0(nc, t, dram, keep)
        attention(nc, t, dram, keep)
        layer1_ffn(nc, t, dram, keep, out)


def kernel(**inputs):
    import numpy as np
    import concourse.bacc as bacc
    from concourse import mybir as _mybir
    from concourse.bass_utils import run_bass_kernel_spmd

    def a(name):
        return np.asarray(inputs[name])

    x = a("x")
    wq = a("L1_cond_Wq").reshape(HK, GQ, KT, 128).transpose(0, 3, 2, 1).reshape(HK, 128, WQ)
    wkv = np.stack([a("L1_cond_Wk").reshape(HK, HD, KT, 128), a("L1_cond_Wv").reshape(HK, HD, KT, 128)], 1)
    wkv = wkv.transpose(0, 4, 3, 1, 2).reshape(HK, 128, WKV)
    wo = a("L1_cond_Wo").reshape(D, HK, REP, HD).transpose(1, 3, 2, 0).reshape(HK, 128, WO)
    wg = np.concatenate([wq, wkv, wo], 2).reshape(HK, 128, B, CH).transpose(0, 2, 1, 3).reshape(UNITS, 128, CH)
    inside = np.concatenate([a("L1_ffn_A_w"), a("L1_ffn_Wq_w")], 0)
    ffn = [w.T.reshape(KT, 128, -1).transpose(1, 0, 2).reshape(128, -1) for w in (inside, a("L1_ffn_B_w"))]
    ffn = np.concatenate(ffn + [np.zeros((128, (B - 1) * CH - FCOLS), np.float32)], 1)
    wg = np.concatenate([wg, ffn.reshape(128, B - 1, CH).transpose(1, 0, 2)], 0)
    kv = np.stack([a("L1_cond_k_cache"), a("L1_cond_v_cache")], 3)
    kv = kv.transpose(2, 0, 1, 3, 4).reshape(HK, kv.shape[0], PAGE, 2 * HD)
    laid = {
        "x": x,
        "xT": x.transpose(0, 2, 1),
        "lora_id": a("itok_B_3_7"),
        "pages": a("itok_Bx16_0_63"),
        "seq": a("itok_B_207_1644"),
        "loraT": a("L0_cond_weight").transpose(0, 2, 1),
        "baseT": a("L0_ffn_base_w").T,
        "lgT": np.concatenate([a("L0_ffn_lora_A").reshape(E0 * R0, D), a("L0_ffn_gate_w")], 0).T,
        "loraBT": a("L0_ffn_lora_B").transpose(0, 2, 1).reshape(E0 * R0, D),
        "base_b": a("L0_ffn_base_b"),
        "qn": a("L1_cond_q_norm_w"),
        "kn": a("L1_cond_k_norm_w"),
        "wg": wg,
        "kv": kv,
        "keysT": a("L1_ffn_keys").T,
        "ident": np.eye(128, dtype=np.float32),
        "tok": np.arange(S, dtype=np.float32).reshape(S, 1),
        "keyno": np.arange(L, dtype=np.float32),
        "invf": np.float32(1.0) / (10000.0 ** (np.arange(0, HD, 2, dtype=np.float32) / np.float32(HD)).astype(np.float64)).astype(np.float32),
    }
    nc = bacc.Bacc("TRN2", target_bir_lowering=False, num_devices=1)
    arrays, t = {}, {}
    for name, v in laid.items():
        v = np.ascontiguousarray(v)
        arrays[f"in_{name}"] = v
        t[name] = nc.dram_tensor(f"in_{name}", v.shape, _mybir.dt.from_np(v.dtype), kind="ExternalInput").ap()
    out = nc.dram_tensor("out_x", (B, S, D), _mybir.dt.float32, kind="ExternalOutput").ap()
    program(nc, t, out)
    r = run_bass_kernel_spmd(nc, [arrays], core_ids=[0])
    return r.results[0]["out_x"]
```
